# Optimizing a Trainium2 kernel written in Bass

```python
import numpy as np
import jax
import jax.numpy as jnp

def _softmax(x, axis=-1):
    return jax.nn.softmax(x, axis=axis)

def _gelu(x):
    return jax.nn.gelu(x, approximate=True)

def _silu(x):
    return jax.nn.silu(x)

def _sigmoid(x):
    return jax.nn.sigmoid(x)

def _layernorm(x, axis=-1, eps=1e-05):
    m = jnp.mean(x, axis=axis, keepdims=True)
    v = jnp.var(x, axis=axis, keepdims=True)
    return (x - m) / jnp.sqrt(v + eps)

def _scatter_add(tgt, idx, src, axis=0):
    return tgt.at[idx].add(src)

def _segment_sum(src, seg, n):
    return jax.ops.segment_sum(src, seg, n)
kernel_name = 'mk_decoder_preln_d1_seqx_r8_a33182'

def setup_inputs(seed: int=0):
    np.random.seed(seed)
    _w = jnp.asarray

    def _rec_inputs():
        import jax
        import jax.numpy as jnp
        _rk = jax.random.key(seed)
        x = -0.0002928 + 1 * jax.random.normal(jax.random.fold_in(_rk, 1), (8, 256, 128), jnp.float32)
        _lenS = 256 - jax.random.randint(jax.random.fold_in(_rk, 7), (8,), 0, max(1, 256 // 4) + 1, jnp.int32)
        _lenS2 = 1601 - jax.random.randint(jax.random.fold_in(_rk, 8), (8,), 0, max(1, 1601 // 4) + 1, jnp.int32)
        _ctx_1024P = jax.random.normal(jax.random.fold_in(_rk, 11), (8, 16, 128), jnp.float32)
        _ctx_1024c = jax.random.dirichlet(jax.random.fold_in(_rk, 511), 0.3 * jnp.ones((16,), jnp.float32), (8, 1601))
        _ctx_1024t = jnp.einsum('bsk,bkd->bsd', _ctx_1024c, _ctx_1024P)
        _ctx_1024t = _ctx_1024t * jax.lax.rsqrt(jnp.mean(jnp.square(_ctx_1024t)) + 1e-12) * 0.953939
        ctx_1024 = -1.39393e-06 + 0.999914 * (_ctx_1024t + 0.3 * jax.random.normal(jax.random.fold_in(_rk, 611), (8, 1601, 128), jnp.float32))
        return (x, ctx_1024)
    x, ctx_1024 = _rec_inputs()

    def _L0_attn_setup():
        import jax, jax.numpy as jnp
        import numpy as np
        from jax import lax
        D_MODEL = 128
        D_STATE = 64
        HEADDIM = 64
        EXPAND = 2
        D_INNER = EXPAND * D_MODEL
        NHEADS = D_INNER // HEADDIM
        ROPE_FRACTION = min(0.5, HEADDIM / D_STATE)
        ROPE_DIM = int(ROPE_FRACTION * D_STATE)
        key = jax.random.key(seed)
        ks = jax.random.split(key, 8)
        B, L = (2, 256)
        d_in_proj = 2 * D_INNER + 2 * D_STATE + NHEADS
        x = jax.random.normal(ks[0], (B, L, D_MODEL), dtype=jnp.float32)
        W_in = jax.random.normal(ks[1], (D_MODEL, d_in_proj), dtype=jnp.float32) * 0.02
        W_out = jax.random.normal(ks[2], (D_INNER, D_MODEL), dtype=jnp.float32) * 0.02
        dt_bias = jax.random.normal(ks[3], (NHEADS,), dtype=jnp.float32) * 0.1
        A_log = jnp.log(jax.random.uniform(ks[4], (NHEADS,), minval=1.0, maxval=16.0, dtype=jnp.float32))
        D_skip = jnp.ones((NHEADS,), dtype=jnp.float32)
        norm_weight = jnp.ones((D_INNER,), dtype=jnp.float32)
        return {'x': x, 'W_in': W_in, 'W_out': W_out, 'dt_bias': dt_bias, 'A_log': A_log, 'D_skip': D_skip, 'norm_weight': norm_weight}
    _L0_attn_all = _L0_attn_setup()
    _L0_attn_in = {k: v for k, v in _L0_attn_all.items() if k in ('W_in', 'W_out', 'dt_bias', 'A_log', 'D_skip', 'norm_weight')}
    del _L0_attn_all

    def _L0_xattn_setup():
        import jax, jax.numpy as jnp
        import numpy as np
        D_MODEL = 128
        HEADS = 16
        DK = D_MODEL // HEADS
        B, S = (1, 512)
        key = jax.random.key(seed)
        ks = jax.random.split(key, 11)
        sd = 1.0 / np.sqrt(D_MODEL)
        return {'q': jax.random.normal(ks[0], (B, S, D_MODEL), jnp.float32), 'k': jax.random.normal(ks[1], (B, S, D_MODEL), jnp.float32), 'v': jax.random.normal(ks[2], (B, S, D_MODEL), jnp.float32), 'Wq': jax.random.uniform(ks[3], (D_MODEL, D_MODEL), jnp.float32, -sd, sd), 'bq': jax.random.uniform(ks[4], (D_MODEL,), jnp.float32, -sd, sd), 'Wk': jax.random.uniform(ks[5], (D_MODEL, DK), jnp.float32, -sd, sd), 'bk': jax.random.uniform(ks[6], (DK,), jnp.float32, -sd, sd), 'Wv': jax.random.uniform(ks[7], (D_MODEL, DK), jnp.float32, -sd, sd), 'bv': jax.random.uniform(ks[8], (DK,), jnp.float32, -sd, sd), 'Wo': jax.random.uniform(ks[9], (D_MODEL, D_MODEL), jnp.float32, -sd, sd), 'bo': jax.random.uniform(ks[10], (D_MODEL,), jnp.float32, -sd, sd)}
    _L0_xattn_all = _L0_xattn_setup()
    _L0_xattn_in = {k: v for k, v in _L0_xattn_all.items() if k in ('Wq', 'bq', 'Wk', 'bk', 'Wv', 'bv', 'Wo', 'bo')}
    del _L0_xattn_all

    def _L0_ffn_setup():
        import jax, jax.numpy as jnp
        import numpy as np
        TOP_K = 2
        NUM_EXPERTS = 8
        key = jax.random.key(seed)
        ks = jax.random.split(key, 8)
        h, d, ds, E = (128, 64, 128, NUM_EXPERTS)
        s = 1.0 / np.sqrt(h)
        return {'x': jax.random.normal(ks[0], (2, 256, h), jnp.float32), 'router': jax.random.normal(ks[1], (h, E), jnp.float32) * s, 'experts_gate': jax.random.normal(ks[2], (E, h, d), jnp.float32) * s, 'experts_up': jax.random.normal(ks[3], (E, h, d), jnp.float32) * s, 'experts_down': jax.random.normal(ks[4], (E, d, h), jnp.float32) * (1.0 / np.sqrt(d)), 'shared_gate': jax.random.normal(ks[5], (h, ds), jnp.float32) * s, 'shared_up': jax.random.normal(ks[6], (h, ds), jnp.float32) * s, 'shared_down': jax.random.normal(ks[7], (ds, h), jnp.float32) * (1.0 / np.sqrt(ds))}
    _L0_ffn_all = _L0_ffn_setup()
    _L0_ffn_in = {k: v for k, v in _L0_ffn_all.items() if k in ('router', 'experts_gate', 'experts_up', 'experts_down', 'shared_gate', 'shared_up', 'shared_down')}
    del _L0_ffn_all
    return {'x': x, 'ctx_1024': ctx_1024, 'L0_attn_W_in': _L0_attn_in['W_in'], 'L0_attn_W_out': _L0_attn_in['W_out'], 'L0_attn_dt_bias': _L0_attn_in['dt_bias'], 'L0_attn_A_log': _L0_attn_in['A_log'], 'L0_attn_D_skip': _L0_attn_in['D_skip'], 'L0_attn_norm_weight': _L0_attn_in['norm_weight'], 'L0_xattn_Wq': _L0_xattn_in['Wq'], 'L0_xattn_bq': _L0_xattn_in['bq'], 'L0_xattn_Wk': _L0_xattn_in['Wk'], 'L0_xattn_bk': _L0_xattn_in['bk'], 'L0_xattn_Wv': _L0_xattn_in['Wv'], 'L0_xattn_bv': _L0_xattn_in['bv'], 'L0_xattn_Wo': _L0_xattn_in['Wo'], 'L0_xattn_bo': _L0_xattn_in['bo'], 'L0_ffn_router': _L0_ffn_in['router'], 'L0_ffn_experts_gate': _L0_ffn_in['experts_gate'], 'L0_ffn_experts_up': _L0_ffn_in['experts_up'], 'L0_ffn_experts_down': _L0_ffn_in['experts_down'], 'L0_ffn_shared_gate': _L0_ffn_in['shared_gate'], 'L0_ffn_shared_up': _L0_ffn_in['shared_up'], 'L0_ffn_shared_down': _L0_ffn_in['shared_down']}

def reference(x, ctx_1024, L0_attn_W_in, L0_attn_W_out, L0_attn_dt_bias, L0_attn_A_log, L0_attn_D_skip, L0_attn_norm_weight, L0_xattn_Wq, L0_xattn_bq, L0_xattn_Wk, L0_xattn_bk, L0_xattn_Wv, L0_xattn_bv, L0_xattn_Wo, L0_xattn_bo, L0_ffn_router, L0_ffn_experts_gate, L0_ffn_experts_up, L0_ffn_experts_down, L0_ffn_shared_gate, L0_ffn_shared_up, L0_ffn_shared_down):
    import jax
    import jax.numpy as jnp

    def _L0_attn_ref(x, W_in, W_out, dt_bias, A_log, D_skip, norm_weight):
        import jax, jax.numpy as jnp
        import numpy as np
        from jax import lax
        D_MODEL = 128
        D_STATE = 64
        HEADDIM = 64
        EXPAND = 2
        D_INNER = EXPAND * D_MODEL
        NHEADS = D_INNER // HEADDIM
        ROPE_FRACTION = min(0.5, HEADDIM / D_STATE)
        ROPE_DIM = int(ROPE_FRACTION * D_STATE)
        Bsz, L, _ = x.shape
        H, P, N = (NHEADS, HEADDIM, D_STATE)
        pairs = ROPE_DIM // 2
        zxbcdt = x @ W_in
        z = zxbcdt[..., :D_INNER]
        xs = zxbcdt[..., D_INNER:2 * D_INNER].reshape(Bsz, L, H, P)
        Bm = zxbcdt[..., 2 * D_INNER:2 * D_INNER + N]
        Cm = zxbcdt[..., 2 * D_INNER + N:2 * D_INNER + 2 * N]
        dt = jax.nn.softplus(zxbcdt[..., 2 * D_INNER + 2 * N:] + dt_bias)
        decay = jnp.exp(-jnp.exp(A_log) * dt)
        inv_freq = 1.0 / 10000.0 ** (jnp.arange(pairs, dtype=jnp.float32) / pairs)
        angle = dt[..., None] * inv_freq
        cos, sin = (jnp.cos(angle), jnp.sin(angle))

        def step(h, inp):
            dt_t, dec_t, B_t, C_t, x_t, cos_t, sin_t = inp
            hr = h[:, :, :ROPE_DIM, :].reshape(Bsz, H, pairs, 2, P)
            h1, h2 = (hr[..., 0, :], hr[..., 1, :])
            c, s = (cos_t[..., None], sin_t[..., None])
            rot = jnp.stack([c * h1 - s * h2, s * h1 + c * h2], axis=-2)
            h_rot = jnp.concatenate([rot.reshape(Bsz, H, ROPE_DIM, P), h[:, :, ROPE_DIM:, :]], axis=2)
            h_new = dec_t[..., None, None] * h_rot + dt_t[..., None, None] * B_t[:, None, :, None] * x_t[:, :, None, :]
            y_t = jnp.einsum('bhnp,bn->bhp', h_new, C_t)
            return (h_new, y_t)
        h0 = jnp.zeros((Bsz, H, N, P), x.dtype)
        lfirst = lambda a: jnp.moveaxis(a, 1, 0)
        inputs = (lfirst(dt), lfirst(decay), lfirst(Bm), lfirst(Cm), lfirst(xs), lfirst(cos), lfirst(sin))
        _, ys = lax.scan(step, h0, inputs)
        y = jnp.moveaxis(ys, 0, 1) + D_skip[None, None, :, None] * xs
        y = y.reshape(Bsz, L, D_INNER)
        y = y * jax.nn.silu(z)
        y = y * lax.rsqrt(jnp.mean(y * y, axis=-1, keepdims=True) + 1e-05) * norm_weight
        return y @ W_out

    def _L0_xattn_ref(q, k, v, Wq, bq, Wk, bk, Wv, bv, Wo, bo):
        import jax, jax.numpy as jnp
        import numpy as np
        D_MODEL = 128
        HEADS = 16
        DK = D_MODEL // HEADS
        B, S = (1, 512)
        b, s, d = q.shape
        qp = (q @ Wq + bq).reshape(b, s, HEADS, DK).transpose(0, 2, 1, 3)
        kp = k @ Wk + bk
        vp = v @ Wv + bv
        scores = jnp.einsum('bhqd,bkd->bhqk', qp, kp)
        attn = jax.nn.softmax(scores, axis=-1)
        out = jnp.einsum('bhqk,bkd->bhqd', attn, vp)
        out = out.transpose(0, 2, 1, 3).reshape(b, s, d)
        return out @ Wo + bo

    def _L0_ffn_ref(x, router, experts_gate, experts_up, experts_down, shared_gate, shared_up, shared_down):
        import jax, jax.numpy as jnp
        import numpy as np
        TOP_K = 2
        NUM_EXPERTS = 8
        b, s, h = x.shape
        E = router.shape[1]
        shared_act = jax.nn.silu(jnp.einsum('bsh,hd->bsd', x, shared_gate))
        shared_up_out = jnp.einsum('bsh,hd->bsd', x, shared_up)
        shared_out = jnp.einsum('bsd,dh->bsh', shared_act * shared_up_out, shared_down)
        router_probs = jax.nn.softmax(jnp.einsum('bsh,he->bse', x, router), axis=-1)
        topk_probs, topk_idx = jax.lax.top_k(router_probs, TOP_K)
        coef = jnp.sum(jax.nn.one_hot(topk_idx, E, dtype=x.dtype) * topk_probs[..., None], axis=2)
        coef = coef.reshape(b * s, E)
        x_flat = x.reshape(b * s, h)
        gate = jnp.einsum('th,ehd->etd', x_flat, experts_gate)
        up = jnp.einsum('th,ehd->etd', x_flat, experts_up)
        expert_out = jnp.einsum('etd,edh->eth', jax.nn.silu(gate) * up, experts_down)
        routed = jnp.einsum('eth,te->th', expert_out, coef)
        return routed.reshape(b, s, h) + shared_out
    x = x + _L0_attn_ref(_layernorm(x, axis=-1), L0_attn_W_in, L0_attn_W_out, L0_attn_dt_bias, L0_attn_A_log, L0_attn_D_skip, L0_attn_norm_weight)
    x = x + _L0_xattn_ref(_layernorm(x, axis=-1), ctx_1024, ctx_1024, L0_xattn_Wq, L0_xattn_bq, L0_xattn_Wk, L0_xattn_bk, L0_xattn_Wv, L0_xattn_bv, L0_xattn_Wo, L0_xattn_bo)
    x = x + _L0_ffn_ref(_layernorm(x, axis=-1), L0_ffn_router, L0_ffn_experts_gate, L0_ffn_experts_up, L0_ffn_experts_down, L0_ffn_shared_gate, L0_ffn_shared_up, L0_ffn_shared_down)
    return x

_drawn_inputs = setup_inputs


def setup_inputs(seed=0):
    import zlib

    import numpy as np

    out = dict(_drawn_inputs(seed))
    spreads = {'L0_attn_D_skip': (1.0, 0.2), 'L0_attn_norm_weight': (1.0, 0.2)}
    factors = {'L0_attn_dt_bias': 3.342, 'L0_attn_A_log': 7.841, 'L0_xattn_bq': 4.307, 'L0_xattn_bk': 8.0}
    for name, (base, spread) in spreads.items():
        noise = np.random.default_rng([zlib.crc32(name.encode()), seed]).standard_normal(out[name].shape)
        drawn = base * np.exp(spread * noise) if base else spread * noise
        out[name] = jnp.asarray(drawn.astype(out[name].dtype))
    for name, factor in factors.items():
        out[name] = (out[name] * factor).astype(out[name].dtype)
    return out
```

```python
from contextlib import ExitStack

import numpy as np

import concourse.bass as bass
from concourse import mybir

B, L, D = 8, 256, 128
P = 128
CH = L // P
NT = B * CH
NH, HD, NS = 4, 64, 64
DI = NH * HD
PAIRS = 16
XH, DK = 16, 8
S = 1601
KT = -(-S // P)
SP = KT * P
TAIL = S - (KT - 1) * P
NE, ED, SD = 8, 64, 128
HT = (NE * ED + SD) // P
EPS = 1e-5
PARTS = 3
QK = PARTS * PARTS * DK
MROW = 96
GH = XH // 2
GC = GH * L
NB = GC // 512
NQ = GC // P
HALF = -(-(S + 1) // 4)
SPANS = ((0, HALF - 1), (2 * (HALF - 1), S - HALF))
LOGCAP = 200.0
ROUND = 1.5 * 2.0 ** 23
TWO_PI_HI = float(np.float32(6.28125))
TWO_PI_LO = float(np.float32(2 * np.pi - 6.28125))
PI = float(np.nextafter(np.float32(np.pi), np.float32(0)))
SCRATCH = 18200
CST_IDENT, CST_GT, CST_LE, CST_FREQ, CST_RANK, CST_SEL, CST_W = 0, 128, 256, 384, 400, 408, 408 + 4 * 128


def shape_constants():
    c = np.zeros((P, CST_W), np.float32)
    r = np.arange(P)
    c[:, CST_IDENT:CST_IDENT + P] = np.eye(P)
    c[:, CST_GT:CST_GT + P] = r[:, None] > r[None, :]
    c[:, CST_LE:CST_LE + P] = r[:, None] <= r[None, :]
    freq = np.float32(1.0) / np.power(np.float32(10000.0), np.arange(PAIRS, dtype=np.float32) / np.float32(PAIRS))
    c[:, CST_FREQ:CST_FREQ + PAIRS] = freq.astype(np.float32)
    c[:, CST_RANK:CST_RANK + NE] = NE - np.arange(NE)
    for k in range(HT - 1):
        for row in range(PARTS * NE):
            e = row % NE
            if e // 2 == k:
                at = CST_SEL + k * P + (e % 2) * ED
                c[row, at:at + ED] = 1.0
    return c


class Steps:

    def __init__(self, eng, sem, index=0, per=0, settle=None):
        self.eng, self.sem, self.base, self.per, self.k, self.settle = eng, sem, index * per, per, 0, settle

    def __call__(self, ins):
        self.k += 1
        ins.then_inc(self.sem, 1)
        self.eng.wait_ge(self.sem, self.base + self.k)
        if self.settle:
            self.settle(self.eng)

    def end(self):
        assert self.k == self.per, (self.sem, self.k, self.per)


PRIME = 1
PRIMED = (("projected", 2), ("z_saved", 2), ("bcd_saved", 2), ("xnT_saved", 0), ("xn_turned", 0), ("ctxT_saved", 4),
          ("kv_made", 0), ("kv_turned", 0), ("k_stacked", 0), ("ks_turned", 2), ("ks_saved", 2),
          ("b_rotated", 0), ("b_plain", 0), ("c_ready", 0), ("dtx_made", 0), ("seg_made", 2), ("btt_made", 0),
          ("btt_saved", 0), ("ctt_made", 0), ("ctt_saved", 0), ("seg_summed", 2), ("decays_made", 2),
          ("products_made", 2), ("mixed", 2), ("state_made", 0), ("state_saved", 0), ("y_made", 0), ("y_read", 0),
          ("y_gated", 0), ("yt_made", 0), ("yt_saved", 0), ("mix_out", 0), ("x1_made", 0), ("norm_summed", 0),
          ("normed", 0), ("normed_turned", 0), ("normed_saved", 0), ("q_made", 0), ("q_read", 0), ("q_split", 0), ("q_in_dram", 0),
          ("q_stacked", 2), ("unit_made", 2), ("unit_taken", 2), ("max_split", 0), ("max_turned", 0),
          ("max_saved", 0), ("max_stacked", 0), ("scored", 2), ("powered", 2), ("summed", 2), ("sums_saved", 0),
          ("sums_turned", 0), ("heads_out", 0),
          ("on_copied", 0), ("on_turned", 0), ("onT_saved", 0), ("o_made", 0), ("x2_made", 0), ("xn3_made", 0),
          ("x3_turned", 0), ("x3_saved", 0), ("lg_made", 0), ("lg_saved", 0), ("gate_made", 2), ("gate_used", 2),
          ("up_made", 2), ("up_used", 2), ("down_made", 0), ("out_made", 0))
TOP_SHIFT = 2
LATE = 3
MIX_ORDER = ("btt", "ctt", "seg0", "seg1", "mix0", "mix1", "state", "y", "yt", "out", "norm", "q")
MIX_SLOTS = {0: (("btt",), ()), 1: ((), ("ctt",)), 2: (("seg0",), ("seg1",)), 3: (("mix0",), ("mix1",)),
             4: (("state",), ("y",)), 6: (("yt",), ()), 7: (("out",), ()), 10: (("norm",), ()), 11: (("q",), ())}
POOL_STEPS, MIX_STEPS, RMS_STEPS, NORM_STEPS, Q_STEPS, MAX_STEPS = 8, 5, 4, 5, 3, 4
N_SMALL = 21
LN_STEPS, MID_E, MID_U, MID_DT, MID_CUM, K_STEPS = 5, 2, 3, 11, 15, 4


def layer_norm_sums(step, X, XC, SQ, st):
    ALU, AX = mybir.AluOpType, mybir.AxisListType
    v = step.eng
    step(v.reduce_sum(st[:, 0, :], X, axis=AX.X))
    step(v.tensor_scalar(st[:, 0, :], st[:, 0, :], -1.0 / D, None, ALU.mult))
    step(v.tensor_tensor(XC, X, bc(st[:, 0, :], 2, D), ALU.add))
    step(v.tensor_tensor(SQ, XC, XC, ALU.mult))
    step(v.reduce_sum(st[:, 1, :], SQ, axis=AX.X))


def bc(ap, axis, n):
    v = ap.unsqueeze(axis)
    shape = list(v.shape)
    shape[axis] = n
    return v.to_broadcast(shape)


def build(nc, x, ctx_1024, W_in, W_out, dt_bias, A_log, D_skip, norm_weight, Wq, bq, Wk, bk, Wv, bv, Wo, bo,
          router, e_gate, e_up, e_down, s_gate, s_up, s_down, consts, out):
    f32, bf16 = mybir.dt.float32, mybir.dt.bfloat16
    ALU, ACT, AX = mybir.AluOpType, mybir.ActivationFunctionType, mybir.AxisListType
    ds = bass.ds
    es = ExitStack()
    with es:
        def sb(name, shape, dt=f32):
            return es.enter_context(nc.sbuf_tensor(name, shape, dt))

        def sem(name):
            return es.enter_context(nc.semaphore(name))

        X = sb("X", [P, NT, D])
        Z = sb("Z", [P, NT, DI])
        XS = sb("XS", [P, NT, DI])
        BCD = sb("BCD", [P, NT, 2 * NS + NH])
        COS = sb("COS", [P, NT, NH, PAIRS])
        SIN = sb("SIN", [P, NT, NH, PAIRS])
        KSall = sb("KSall", [P, B, SP], bf16)
        Vall = sb("Vall", [P, B, KT, 32])
        ONall = sb("ONall", [P, NT, D])
        CST = sb("CST", [P, CST_W])
        identb = sb("identb", [P, P], bf16)
        selb = sb("selb", [PARTS * NE, HT - 1, P], bf16)
        bigb = sb("bigb", [P, NH, P], bf16)
        Win = sb("Win", [P, 2 * DI + 2 * NS + NH])
        Wout = sb("Wout", [P, 2, D])
        nw = sb("nw", [P, 2])
        eps = sb("eps", [P, 1])
        hb = sb("hb", [P, 3, NH])
        WqS = sb("WqS", [P, D])
        bqS = sb("bqS", [P, 1])
        WkvS = sb("WkvS", [P, 32])
        bkvS = sb("bkvS", [P, 1])
        WoS = sb("WoS", [P, D])
        boS = sb("boS", [P, D])
        RT = sb("RT", [P, NE])
        WG = sb("WG", [P, HT * P])
        WU = sb("WU", [P, HT * P])
        WD = sb("WD", [P, HT, D])
        ident = CST[:, CST_IDENT:CST_IDENT + P]
        mask_gt = CST[:, CST_GT:CST_GT + P]
        mask_le = CST[:, CST_LE:CST_LE + P]
        freq = CST[:, CST_FREQ:CST_FREQ + PAIRS]
        rank = CST[:, CST_RANK:CST_RANK + NE]
        st = sb("st", [P, 4, NT])
        DT = sb("DT", [P, 2, NT, NH])
        CUM = sb("CUM", [P, 2, NT, NH])
        EC = sb("EC", [P, NT, NH])
        tm = sb("tm", [P, 6, NT * NH])

        SCR = sb("SCR", [P, SCRATCH])
        taken = [0]

        def scr(shape, dt=f32):
            n = int(np.prod(shape)) * (2 if dt == bf16 else 4) // 4
            v = SCR[:, taken[0]:taken[0] + n]
            taken[0] += n
            assert taken[0] <= SCRATCH, taken[0]
            if dt == bf16:
                v = v.bitcast(bf16)
            if len(shape) == 2:
                v = v.rearrange("p (a b) -> p a b", b=shape[1])
            if len(shape) == 3:
                v = v.rearrange("p (a b c) -> p a b c", b=shape[1], c=shape[2])
            return v

        XC = scr([NT, D])
        SQ = scr([NT, D])
        CTX = [scr([KT, D]) for _ in range(2)]
        CTXT = scr([2048])
        xns = scr([CH, D])
        xnT = scr([CH, P])
        KVT = scr([512])
        KF = scr([16, DK])
        KR = scr([16, DK])
        KPt = [scr([16, DK], bf16) for _ in range(PARTS)]
        KST = scr([16, P], bf16)
        first_top = taken[0]
        ANG = CTX[0][:, 0:8, :].rearrange("p a b -> p (a b)").rearrange("p (n h i) -> p n h i", n=NT, h=NH)
        TR = CTX[1][:, 0:8, :].rearrange("p a b -> p (a b)").rearrange("p (n h i) -> p n h i", n=NT, h=NH)
        T2 = CTXT[:, 0:1024].rearrange("p (n h i) -> p n h i", n=NT, h=NH)
        taken[0] = 0
        PE_ = scr([2, NB, 512])
        KSa = scr([SP], bf16)
        KSb = scr([SP], bf16)
        Vc = scr([KT, 32])
        Qg = [scr([GC], bf16) for _ in range(2)]
        QF = scr([L])
        QP = scr([PARTS, L], bf16)
        BT = scr([CH, NH, NS])
        CT = scr([CH, NH, NS])
        CE = scr([NH, NS])
        r1 = scr([CH * NH, PAIRS])
        r2 = scr([CH * NH, PAIRS])
        c1 = scr([CH * NH, PAIRS])
        c2 = scr([CH * NH, PAIRS])
        BTT = scr([CH * 2, P])
        CTZ = scr([CH, NH, P])
        CET = scr([2, P])
        SR = scr([NH, P])
        LM = scr([CH, NH, P])
        dtx = scr([CH, NH, HD])
        dtxe = scr([NH, HD])
        HZ = scr([NH, HD])
        Y = scr([CH, DI])
        YT = scr([CH * 2, P])
        junk = scr([DI])
        rms = scr([6])
        NMX = scr([2, NQ])
        NM = scr([NQ])
        NR = scr([NQ])
        MP = scr([PARTS, NQ], bf16)
        MT = scr([P], bf16)
        OT = scr([512])
        rdn = scr([16])
        lx = scr([CH, D])
        lq = scr([CH, D])
        ln = scr([8])
        lnT = scr([L])
        X3T = Z[:, 0:8, :].rearrange("p a b -> p (a b)")
        SG = Z[:, 8:12, :].rearrange("p a b -> p (a b)").rearrange("p (a b) -> p a b", b=512)
        Hb = XS[:, 0:10, :].rearrange("p a b -> p (a b)").rearrange("p (a b) -> p a b", b=512)
        T8 = XS[:, 10:16, :].rearrange("p a b -> p (a b)")
        LG, SH, KY, S1, S2_, PB = [T8[:, k * 128:(k + 1) * 128].rearrange("p (n e) -> p n e", e=NE) for k in range(6)]
        CP = T8[:, 768:768 + 256].bitcast(bf16).rearrange("p (n e) -> p n e", e=32)
        red = T8[:, 1024:1024 + 16]
        rcp = T8[:, 1040:1040 + 16]
        CR = T8[:, 1056:1056 + 128].rearrange("p (n e) -> p n e", e=NE)
        CTs = Z[:, 12:16, :].rearrange("p a b -> p (a b)")[0:PARTS * NE, :].bitcast(bf16)

        PS = es.enter_context(nc.psum_tensor("PS", [P, 8, 512], f32))
        UNIT, RING, ACC, AUX = 0, 4, 6, 7


        sems = {}

        def S_(name):
            if name not in sems:
                sems[name] = es.enter_context(nc.semaphore(name))
            return sems[name]

        primed = []
        for name, n in PRIMED:
            primed += [S_(f"{name}{k}") for k in range(n)] if n else [S_(name)]
        with nc.Block() as block:
            @block.sync
            def _(sp):
                for p in primed[0::4]:
                    sp.sem_inc(p, PRIME)

            @block.gpsimd
            def _(pool):
                for p in primed[1::4]:
                    pool.sem_inc(p, PRIME)

            @block.scalar
            def _(act):
                for p in primed[2::4]:
                    act.sem_inc(p, PRIME)

            @block.vector
            def _(dve):
                for p in primed[3::4]:
                    dve.sem_inc(p, PRIME)

        def settle(eng):
            eng.sem_inc(S_("settled"), 1)

        q_dram = nc.dram_tensor("q_parts", (XH, PARTS, DK, L), bf16, kind="Internal").ap()

        def row(v):
            return v.rearrange("(o a) -> o a", o=1).to_broadcast([P, v.shape[0]])

        def col(v):
            return v.rearrange("(a o) -> a o", o=1)

        def bank(k):
            return PS[:, k, :]

        def bankb(k):
            return PS[:, k, :].bitcast(bf16)

        with nc.Block() as block:
            x_in, w_in, c_in, w_set = S_("x_in"), S_("w_in"), S_("c_in"), S_("w_set")
            zeroed, consts_cast = S_("zeroed"), S_("consts_cast")
            ctx_in = [S_("ctx_in0"), S_("ctx_in1")]
            ln_vec, ln_act = S_("ln_vec"), S_("ln_act")
            xn_made, xn_turned, xnT_saved = S_("xn_made"), S_("xn_turned"), S_("xnT_saved")
            projected = [S_("projected0"), S_("projected1")]
            z_saved = [S_("z_saved0"), S_("z_saved1")]
            bcd_saved = [S_("bcd_saved0"), S_("bcd_saved1")]
            ctx_turned = [S_(f"ctx_turned{q}") for q in range(4)]
            ctxT_saved = [S_(f"ctxT_saved{q}") for q in range(4)]
            kv_made, kv_saved, kv_turned, v_saved = S_("kv_made"), S_("kv_saved"), S_("kv_turned"), S_("v_saved")
            k_split, k_steps, k_stacked = S_("k_split"), S_("k_steps"), S_("k_stacked")
            ks_turned = [S_("ks_turned0"), S_("ks_turned1")]
            ks_saved = [S_("ks_saved0"), S_("ks_saved1")]
            mid_vec, mid_act, cum_made = S_("mid_vec"), S_("mid_act"), S_("cum_made")
            trig_arg, sin_made, z_gated = S_("trig_arg"), S_("sin_made"), S_("z_gated")

            @block.sync
            def _(sp):
                sp.dma_start(X[:, :, :], x.rearrange("b (c p) d -> p (b c) d", p=P)).then_inc(x_in, 16)
                sp.dma_start(CST[:, :], consts).then_inc(c_in, 16)
                sp.dma_start(Win[:, :], W_in).then_inc(w_in, 16)
                sp.wait_ge(zeroed, 1)

                def load_context(b, half):
                    main = ctx_1024[:, 0:(KT - 1) * P, :].rearrange("b (p j) d -> p b j d", p=P)
                    tail = ctx_1024[:, (KT - 1) * P:S, :].rearrange("b p d -> p b d")
                    sp.dma_start(CTX[half][:, 0:KT - 1, :].unsqueeze(1), main[:, ds(b, 1)]).then_inc(ctx_in[half], 16)
                    sp.dma_start(CTX[half][0:TAIL, KT - 1:KT, :], tail[:, ds(b, 1)]).then_inc(ctx_in[half], 16)

                load_context(0, 0)
                small = [(WkvS[:, 0:DK], Wk), (WkvS[:, DK:2 * DK], Wv)]
                small += [(bkvS[32 * j:32 * j + DK, :], col(bk)) for j in range(4)]
                small += [(bkvS[32 * j + DK:32 * j + 2 * DK, :], col(bv)) for j in range(4)]
                small += [(hb[:, 0, :], row(dt_bias)), (hb[:, 1, :], row(A_log)), (hb[:, 2, :], row(D_skip))]
                small += [(Wout[:, :, :], W_out.rearrange("(k p) d -> p k d", p=P)),
                          (nw[:, 0:1], col(norm_weight[0:P])), (nw[:, 1:2], col(norm_weight[P:2 * P])),
                          (WqS[:, :], Wq), (bqS[:, :], col(bq)), (WoS[:, :], Wo), (boS[:, :], row(bo)),
                          (RT[:, :], router)]
                for n, (to, what) in enumerate(small):
                    sp.dma_start(to, what).then_inc(w_set, 16)
                assert len(small) == N_SMALL
                load_context(1, 1)
                with sp.Fori(1, B // 2) as i:
                    for half in range(2):
                        sp.wait_ge(ctx_turned[3], 2 * i + half - 1)
                        load_context(2 * i + half, half)
                for k, (gate, up) in enumerate(((e_gate, e_up),)):
                    for to, what in ((WG, gate), (WU, up)):
                        sp.dma_start(to[:, 0:NE * ED].rearrange("p (e d) -> p e d", e=NE),
                                     what.rearrange("e h d -> h e d")).then_inc(w_set, 16)
                sp.dma_start(WG[:, NE * ED:], s_gate).then_inc(w_set, 16)
                sp.dma_start(WU[:, NE * ED:], s_up).then_inc(w_set, 16)
                sp.dma_start(WD[:, 0:HT - 1, :], e_down.rearrange("(k e) d h -> (e d) k h", e=2)).then_inc(w_set, 16)
                sp.dma_start(WD[:, HT - 1, :], s_down).then_inc(w_set, 16)
                sp.wait_ge(w_set, 16 * (N_SMALL + 6))

            @block.gpsimd
            def _(pool):
                g = Steps(pool, S_("pool_zeroes"))
                g(nc.gpsimd.memset(WkvS[:, :], 0.0))
                g(nc.gpsimd.memset(bkvS[:, :], 0.0))
                g(nc.gpsimd.memset(eps[:, :], EPS))
                for half in range(2):
                    g(nc.gpsimd.memset(CTX[half][64:P, KT - 1, :], 0.0))
                g(nc.gpsimd.memset(CTXT[:, SP:2048], 0.0))
                g(nc.gpsimd.memset(KST[:, :, :], 0.0))
                g(nc.gpsimd.memset(Vall[:, :, :, :], 0.0))
                g(nc.gpsimd.memset(KST[:, :, MROW:MROW + PARTS], 1.0))
                g(nc.gpsimd.memset(Vall[:, :, 0:KT - 1, DK:DK + 1], 1.0))
                g(nc.gpsimd.memset(Vall[0:TAIL, :, KT - 1:KT, DK:DK + 1], 1.0))
                nc.gpsimd.memset(KSall[:, :, S:SP], 0.0).then_inc(zeroed, 1)
                with pool.Fori(0, B) as b:
                    pool.wait_ge(k_split, b + 1)
                    pool.wait_ge(ks_turned[1], PRIME + b)
                    settle(pool)
                    for j in range(PARTS):
                        to = KST[:, :, 0:QK].rearrange("p t (j i d) -> p t j i d", i=PARTS, j=PARTS)[:, :, j, :, :]
                        last = nc.gpsimd.tensor_copy(to, bc(KPt[j], 2, PARTS))
                    last.then_inc(k_stacked, 1)

            @block.scalar
            def _(act):
                act.wait_ge(zeroed, 1)
                act.wait_ge(ln_vec, LN_STEPS)
                a = Steps(act, ln_act)
                a(nc.scalar.activation(st[:, 2, :], st[:, 1, :], ACT.Ln, bias=eps[:, :], scale=1.0 / D))
                a(nc.scalar.activation(st[:, 3, :], st[:, 2, :], ACT.Exp, scale=-0.5))
                with act.Fori(0, B // 2) as i:
                    for half in range(2):
                        b = 2 * i + half

                        act.wait_ge(xn_turned, PRIME + b + 1)
                        act.wait_ge(projected[1], PRIME + b)
                        nc.scalar.copy(xnT[:, :, :], bank(0)[:, 0:CH * P].rearrange("p (c t) -> p c t", c=CH))\
                            .then_inc(xnT_saved, 1)
                        for c in range(CH):
                            act.wait_ge(projected[c], PRIME + b + 1)
                            settle(act)
                            n = ds(2 * b + c, 1)
                            nc.scalar.copy(Z[:, n, :], bank(1 + 2 * c)[:, 0:DI].unsqueeze(1))
                            nc.scalar.copy(XS[:, n, :], bank(1 + 2 * c)[:, DI:2 * DI].unsqueeze(1)).then_inc(z_saved[c], 1)
                        if half == 0:
                            act.wait_ge(w_set, 16 * N_SMALL)
                        act.wait_ge(kv_made, PRIME + b + 1)
                        act.wait_ge(kv_turned, PRIME + b)
                        nc.scalar.activation(KVT[:, :], bank(7), ACT.Identity, bias=bkvS[:, :]).then_inc(kv_saved, 1)
                        act.wait_ge(ks_turned[0], PRIME + b + 1)
                        settle(act)
                        nc.scalar.copy(KSall[:, ds(b, 1), 0:8 * P], bankb(7).unsqueeze(1)).then_inc(ks_saved[0], 1)
                m = Steps(act, mid_act)
                act.wait_ge(mid_vec, MID_E)
                m(nc.scalar.activation(tm[:, 1, :], tm[:, 0, :], ACT.Exp))
                m(nc.scalar.activation(hb[:, 1, :], hb[:, 1, :], ACT.Exp))
                act.wait_ge(mid_vec, MID_U)
                m(nc.scalar.activation(tm[:, 3, :], tm[:, 2, :], ACT.Ln))
                act.wait_ge(mid_vec, MID_CUM)
                m(nc.scalar.activation(EC[:, :, :], CUM[:, 1, :, :], ACT.Exp, scale=-1.0))
                for n, to in enumerate((SIN, COS)):
                    act.wait_ge(trig_arg, n + 1)
                    nc.scalar.activation(to[:, :, :, :], T2, ACT.Sin).then_inc(sin_made, 1)
                nc.scalar.activation(Z[:, :, :], Z[:, :, :], ACT.Silu).then_inc(z_gated, 1)

            @block.vector
            def _(dve):
                dve.wait_ge(c_in, 16)
                nc.vector.tensor_copy(identb[:, :], ident)
                nc.vector.tensor_copy(selb[:, :, :], CST[0:PARTS * NE, CST_SEL:CST_SEL + (HT - 1) * P]
                                      .rearrange("p (k r) -> p k r", k=HT - 1))
                nc.vector.tensor_scalar(bigb[:, :, :], bc(mask_gt, 1, NH), 30000.0, None, ALU.mult).then_inc(consts_cast, 1)
                dve.wait_ge(x_in, 16)
                v = Steps(dve, ln_vec)
                layer_norm_sums(v, X[:, :, :], XC, SQ, st)
                assert v.k == LN_STEPS
                dve.wait_ge(ln_act, 2)
                with dve.Fori(0, B // 2) as i:
                    for half in range(2):
                        b = 2 * i + half
                        dve.wait_ge(xn_turned, PRIME + b)
                        n = ds(2 * b, CH)
                        nc.vector.tensor_tensor(xns[:, :, :], XC[:, n, :], bc(st[:, 3, n], 2, D), ALU.mult).then_inc(xn_made, 1)

                        def keep_ctxT(q, n):
                            dve.wait_ge(ctx_turned[q], b + 1)
                            dve.wait_ge(kv_made, PRIME + b)
                            nc.vector.tensor_copy(CTXT[:, 512 * q:512 * q + n], bank(5 + q % 2)[:, 0:n]).then_inc(ctxT_saved[q], 1)

                        def keep_bcd(c):
                            dve.wait_ge(projected[c], PRIME + b + 1)
                            settle(dve)
                            nc.vector.tensor_copy(BCD[:, ds(2 * b + c, 1), :], bank(2 + 2 * c)[:, 0:2 * NS + NH].unsqueeze(1))\
                                .then_inc(bcd_saved[c], 1)

                        keep_ctxT(0, 512)
                        keep_ctxT(1, 512)
                        keep_bcd(0)
                        keep_ctxT(2, 512)
                        keep_ctxT(3, P)
                        keep_bcd(1)
                        k = Steps(dve, k_steps, b, K_STEPS)
                        dve.wait_ge(kv_turned, PRIME + b + 1)
                        if half == 0:
                            dve.wait_ge(zeroed, 1)
                        kv = bank(7).rearrange("p (s j e) -> p j s e", s=4, j=4)
                        settle(dve)
                        k(nc.vector.tensor_copy(KF.rearrange("p (j s) d -> p j s d", j=4), kv[:, :, :, 0:DK]))
                        settle(dve)
                        for j in range(3):
                            nc.vector.tensor_copy(Vall[:, ds(b, 1), 4 * j:4 * j + 4, 0:DK], kv[:, j:j + 1, :, DK:2 * DK])
                        nc.vector.tensor_copy(Vall[0:TAIL, ds(b, 1), KT - 1:KT, 0:DK], kv[0:TAIL, 3:4, 0:1, DK:2 * DK])\
                            .then_inc(v_saved, 1)
                        dve.wait_ge(k_stacked, PRIME + b)
                        k(nc.vector.tensor_copy(KPt[0], KF))
                        k(nc.vector.tensor_tensor(KR, KF, KPt[0], ALU.subtract))
                        k(nc.vector.tensor_copy(KPt[1], KR))
                        k.end()
                        nc.vector.tensor_tensor(KPt[2], KR, KPt[1], ALU.subtract).then_inc(k_split, 1)
                        dve.wait_ge(k_split, b + 1)
                        dve.wait_ge(ks_turned[1], PRIME + b + 1)
                        settle(dve)
                        nc.vector.tensor_copy(KSall[:, ds(b, 1), 8 * P:S], bankb(7)[:, 0:S - 8 * P].unsqueeze(1))\
                            .then_inc(ks_saved[1], 1)
                m = Steps(dve, mid_vec)
                raw = DT[:, 0, :, :]
                flat = raw.rearrange("p n h -> p (n h)")
                dve.wait_ge(bcd_saved[0], PRIME + B)
                dve.wait_ge(bcd_saved[1], PRIME + B)
                m(nc.vector.tensor_tensor(raw, BCD[:, :, 2 * NS:], bc(hb[:, 0, :], 1, NT), ALU.add))
                m(nc.vector.scalar_tensor_tensor(tm[:, 0, :], flat, -1.0, flat, ALU.mult, ALU.min))
                assert m.k == MID_E
                dve.wait_ge(mid_act, 2)
                m(nc.vector.tensor_scalar(tm[:, 2, :], tm[:, 1, :], 1.0, None, ALU.add))
                assert m.k == MID_U
                m(nc.vector.tensor_scalar(tm[:, 4, :], tm[:, 2, :], -1.0, None, ALU.add))
                m(nc.vector.tensor_tensor(tm[:, 4, :], tm[:, 1, :], tm[:, 4, :], ALU.subtract))
                m(nc.vector.reciprocal(tm[:, 5, :], tm[:, 2, :]))
                m(nc.vector.tensor_tensor(tm[:, 4, :], tm[:, 4, :], tm[:, 5, :], ALU.mult))
                dve.wait_ge(mid_act, 3)
                m(nc.vector.tensor_tensor(tm[:, 3, :], tm[:, 3, :], tm[:, 4, :], ALU.add))
                m(nc.vector.scalar_tensor_tensor(flat, flat, 0.0, tm[:, 3, :], ALU.max, ALU.add))
                m(nc.vector.tensor_tensor(DT[:, 1, :, :], raw, bc(hb[:, 1, :], 1, NT), ALU.mult))
                m(nc.vector.tensor_scalar(DT[:, 1, :, :], DT[:, 1, :, :], LOGCAP, None, ALU.min))
                assert m.k == MID_DT
                dve.wait_ge(cum_made, 1)
                cum = bank(0)[:, 0:P].rearrange("p (c k b h) -> p c k b h", c=2, k=2, b=B)
                CV = CUM[:, :, :, :].rearrange("p k (b c) h -> p k b c h", c=2)
                m(nc.vector.tensor_scalar(CV[:, 0, :, 0, :], cum[:, 0, 0], -1.0, None, ALU.mult))
                m(nc.vector.tensor_copy(CV[:, 1, :, 0, :], cum[:, 0, 1]))
                m(nc.vector.tensor_copy(CV[:, 0, :, 1, :], cum[:, 1, 0]))
                m(nc.vector.tensor_copy(CV[:, 1, :, 1, :], cum[:, 1, 1]))
                assert m.k == MID_CUM
                shape = [P, NT, NH, PAIRS]
                fr = freq.unsqueeze(1).unsqueeze(1).to_broadcast(shape)
                m(nc.vector.tensor_tensor(ANG, bc(CUM[:, 0, :, :], 3, PAIRS), fr, ALU.mult))
                for n, (turn, shift) in enumerate(((0.0, 0.0), (0.25, np.pi / 2))):
                    if n:
                        dve.wait_ge(sin_made, 1)
                    m(nc.vector.tensor_scalar(TR, ANG, float(0.5 / np.pi), turn, ALU.mult, ALU.add))
                    m(nc.vector.tensor_scalar(TR, TR, ROUND, ROUND, ALU.add, ALU.subtract))
                    m(nc.vector.scalar_tensor_tensor(T2, TR, -TWO_PI_HI, ANG, ALU.mult, ALU.add))
                    m(nc.vector.scalar_tensor_tensor(T2, TR, -TWO_PI_LO, T2, ALU.mult, ALU.add))
                    m(nc.vector.tensor_scalar(T2, T2, float(shift), PI, ALU.add, ALU.min))
                    nc.vector.tensor_scalar(T2, T2, -PI, None, ALU.max).then_inc(trig_arg, 1)
                    dve.wait_ge(trig_arg, n + 1)
                for k in range(2):
                    m(nc.vector.tensor_scalar(Wout[:, k, :], Wout[:, k, :], nw[:, k:k + 1], None, ALU.mult))

            @block.tensor
            def _(pe):
                pe.wait_ge(c_in, 16)
                pe.wait_ge(w_in, 16)
                pe.wait_ge(consts_cast, 1)
                pe.wait_ge(zeroed, 1)
                with pe.Fori(0, B // 2) as i:
                    for half in range(2):
                        b = 2 * i + half

                        def turn_ctx(q, n):
                            if q < 2:
                                pe.wait_ge(ctxT_saved[q + 2], PRIME + b)
                            else:
                                pe.wait_ge(ctxT_saved[q - 2], PRIME + b + 1)
                            for t in range(n):
                                last = nc.tensor.transpose(bank(5 + q % 2)[:, t * P:(t + 1) * P], CTX[half][:, 4 * q + t, :], ident)
                            last.then_inc(ctx_turned[q], 1)

                        def project(c):
                            pe.wait_ge(xnT_saved, PRIME + b + 1)
                            pe.wait_ge(z_saved[c], PRIME + b)
                            pe.wait_ge(bcd_saved[c], PRIME + b)
                            nc.tensor.matmul(bank(1 + 2 * c), xnT[:, c, :], Win[:, 0:2 * DI], start=True, stop=True)
                            nc.tensor.matmul(bank(2 + 2 * c)[:, 0:2 * NS + NH], xnT[:, c, :], Win[:, 2 * DI:],
                                             start=True, stop=True).then_inc(projected[c], 1)

                        pe.wait_ge(xn_made, b + 1)
                        pe.wait_ge(xnT_saved, PRIME + b)
                        for c in range(CH):
                            last = nc.tensor.transpose(bank(0)[:, c * P:(c + 1) * P], xns[:, c, :], ident)
                        last.then_inc(xn_turned, 1)
                        pe.wait_ge(ctx_in[half], 32 * (i + 1))
                        turn_ctx(0, 4)
                        turn_ctx(1, 4)
                        project(0)
                        turn_ctx(2, 4)
                        turn_ctx(3, 1)
                        project(1)
                        if half == 0:
                            pe.wait_ge(w_set, 16 * N_SMALL)
                        for q in range(4):
                            pe.wait_ge(ctxT_saved[q], PRIME + b + 1)
                        pe.wait_ge(ks_saved[1], PRIME + b)
                        for j in range(4):
                            last = nc.tensor.matmul(PS[32 * j:32 * j + 32, 7, :], WkvS[:, :], CTXT[:, 512 * j:512 * j + 512],
                                                    start=True, stop=True)
                        last.then_inc(kv_made, 1)
                        pe.wait_ge(kv_saved, b + 1)
                        for t in range(4):
                            last = nc.tensor.transpose(bank(7)[:, t * P:(t + 1) * P], KVT[:, t * P:(t + 1) * P], ident)
                        last.then_inc(kv_turned, 1)
                        pe.wait_ge(k_stacked, PRIME + b + 1)
                        pe.wait_ge(v_saved, b + 1)
                        for t in range(8):
                            last = nc.tensor.transpose(bankb(7)[:, t * P:(t + 1) * P], KST[:, t, :], identb[:, :])
                        last.then_inc(ks_turned[0], 1)
                        pe.wait_ge(ks_saved[0], PRIME + b + 1)
                        for t in range(8, KT):
                            last = nc.tensor.transpose(bankb(7)[:, (t - 8) * P:(t - 7) * P], KST[:, t, :], identb[:, :])
                        last.then_inc(ks_turned[1], 1)
                pe.wait_ge(mid_vec, MID_DT)
                for c, mask in enumerate((mask_gt, mask_le)):
                    rhs = DT[:, :, :, :].rearrange("p k (b c) h -> p k b c h", c=2)[:, :, :, c, :]
                    last = nc.tensor.matmul(bank(0)[:, 64 * c:64 * c + 64], mask, rhs, start=True, stop=True)
                last.then_inc(cum_made, 1)

        with nc.Block() as block:
            main_zeroed = S_("main_zeroed")
            b_turned_in, b_plain, c_ready, dtx_made = S_("b_rotated"), S_("b_plain"), S_("c_ready"), S_("dtx_made")
            pool_steps, mix_steps, norm_steps, q_steps = (S_(n) for n in ("pool_steps", "mix_steps", "norm_steps", "q_steps"))
            seg_made = [S_("seg_made0"), S_("seg_made1")]
            btt_made, btt_saved, ctt_made, ctt_saved = S_("btt_made"), S_("btt_saved"), S_("ctt_made"), S_("ctt_saved")
            seg_summed = [S_("seg_summed0"), S_("seg_summed1")]
            decays_made = [S_("decays_made0"), S_("decays_made1")]
            products_made = [S_("products_made0"), S_("products_made1")]
            mixed = [S_("mixed0"), S_("mixed1")]
            state_made, state_saved = S_("state_made"), S_("state_saved")
            y_made, y_read, y_gated, y_squared = S_("y_made"), S_("y_read"), S_("y_gated"), S_("y_squared")
            yt_made, yt_saved, rms_steps, mix_out, x1_made = (S_(n) for n in ("yt_made", "yt_saved", "rms_steps", "mix_out", "x1_made"))
            norm_summed, norm_act, normed, normed_turned, normed_saved = (
                S_(n) for n in ("norm_summed", "norm_act", "normed", "normed_turned", "normed_saved"))
            q_in_dram = S_("q_in_dram")
            q_made, q_read, q_split = S_("q_made"), S_("q_read"), S_("q_split")
            q_stacked = [S_("q_stacked0"), S_("q_stacked1")]
            keys_max, keys_exp, values_ready = S_("keys_max"), S_("keys_exp"), S_("values_ready")
            unit_made = [S_("unit_made0"), S_("unit_made1")]
            unit_taken = [S_("unit_taken0"), S_("unit_taken1")]
            max_steps, max_split, max_turned, max_saved, max_stacked = (
                S_(n) for n in ("max_steps", "max_split", "max_turned", "max_saved", "max_stacked"))
            scored = [S_("scored0"), S_("scored1")]
            powered = [S_("powered0"), S_("powered1")]
            summed = [S_("summed0"), S_("summed1")]
            sums_saved, sums_turned, out_steps, heads_out = (
                S_(n) for n in ("sums_saved", "sums_turned", "out_steps", "heads_out"))

            def score_fill(b, g, kt, j):
                return ((2 * b + g) * KT + kt) * 2 + j // 2

            def sum_count(b, g, kt):
                return KT * b + (g * KT + kt) // 2

            def parity(g, kt):
                return (g * KT + kt) % 2

            def units(kt, g):
                first = 0 if g == 0 else LATE
                per = -(-2 * NQ // (KT - 1 - first))
                return range(min(2 * NQ, per * (kt - first)), min(2 * NQ, per * (kt - first + 1))) if kt >= first else range(0)

            def rotate(eng, step, src, to, t1, t2, n, sem=None):
                sh = [P, CH, NH, PAIRS]
                pair = src[:, :, 0:2 * PAIRS].rearrange("p n (i two) -> p n two i", two=2)
                one, two = (pair[:, :, k, :].unsqueeze(2).to_broadcast(sh) for k in range(2))
                a = t1.rearrange("p (n h) i -> p n h i", n=CH)
                c = t2.rearrange("p (n h) i -> p n h i", n=CH)
                dst = to[:, :, :, 0:2 * PAIRS].rearrange("p n h (i two) -> p n h i two", two=2)
                cos, sin = COS[:, n, :, :], SIN[:, n, :, :]
                step(eng.tensor_tensor(a, cos, one, ALU.mult))
                step(eng.tensor_tensor(c, sin, two, ALU.mult))
                step(eng.tensor_tensor(dst[:, :, :, :, 0], a, c, ALU.add))
                step(eng.tensor_tensor(a, cos, two, ALU.mult))
                step(eng.tensor_tensor(c, sin, one, ALU.mult))
                final = eng.tensor_tensor(dst[:, :, :, :, 1], a, c, ALU.subtract)
                if sem is None:
                    step(final)
                else:
                    final.then_inc(sem, 1)

            @block.sync
            def _(sp):
                def queries_to_dram(b):
                    sp.wait_ge(q_split, PRIME + b + 1)
                    for g in range(2):
                        sp.wait_ge(q_stacked[g], PRIME + 16 * PARTS * b)
                    for i in range(PARTS):
                        sp.dma_start(q_dram[:, i], QP[:, i, :]).then_inc(q_in_dram, 16)

                def stack_queries(b, g, b_before=None):
                    if b_before is not None:
                        sp.wait_ge(scored[1], PRIME + score_fill(b_before, g, KT, 1))
                    sp.wait_ge(q_in_dram, PRIME + 16 * PARTS * (b + 1))
                    src = q_dram[g * GH:(g + 1) * GH].rearrange("h i d t -> (i d) h t")
                    for j in range(PARTS):
                        r = j * PARTS * DK
                        sp.dma_start(Qg[g][r:r + PARTS * DK, :].rearrange("p (h t) -> p h t", h=GH), src)\
                            .then_inc(q_stacked[g], 16)

                def stack_maxima(b, g):
                    sp.wait_ge(max_saved, PRIME + 2 * b + g + 1)
                    sp.dma_start(Qg[g][MROW:MROW + PARTS, :].rearrange("i (q t) -> i q t", q=NQ), MT[0:PARTS * NQ, :])\
                        .then_inc(max_stacked, 16)

                def body(b, last=False):
                    stack_maxima(b, 1)
                    if not last:
                        queries_to_dram(b + 1)
                        stack_queries(b + 1, 0, b)
                        stack_maxima(b + 1, 0)
                        stack_queries(b + 1, 1, b)

                sp.wait_ge(main_zeroed, 1)
                queries_to_dram(0)
                stack_queries(0, 0)
                stack_queries(0, 1)
                stack_maxima(0, 0)
                body(0)
                with sp.Fori(1, B - 1) as b:
                    body(b)
                body(B - 1, last=True)
                sp.wait_ge(max_stacked, PRIME + 16 * 2 * B)

            @block.gpsimd
            def _(pool):
                g = Steps(pool, S_("main_zeroes"))
                for what in (Qg[0], Qg[1], KSa, CTZ, HZ):
                    g(nc.gpsimd.memset(what, 0.0))
                nc.gpsimd.memset(junk[0:1, 0:1], 0.0).then_inc(main_zeroed, 1)
                pool.wait_ge(main_zeroed, 1)

                def mixer(b):
                    p = Steps(pool, pool_steps, b, POOL_STEPS, settle)
                    n = ds(2 * b, CH)
                    Bp, Cp = BCD[:, n, PAIRS * 2:NS], BCD[:, n, NS + PAIRS * 2:2 * NS]
                    pool.wait_ge(btt_made, PRIME + b)
                    pool.wait_ge(state_made, PRIME + b)
                    settle(pool)
                    nc.gpsimd.tensor_copy(BT[:, :, :, PAIRS * 2:], bc(Bp, 2, NH)).then_inc(b_plain, 1)
                    pool.wait_ge(ctt_made, PRIME + b)
                    settle(pool)
                    p(nc.gpsimd.tensor_copy(CT[:, :, :, PAIRS * 2:], bc(Cp, 2, NH)))
                    rotate(pool, p, BCD[:, n, NS:2 * NS], CT, c1, c2, n)
                    xs4 = XS[:, n, :].rearrange("p n (h e) -> p n h e", h=NH)
                    nc.gpsimd.tensor_tensor(CE, CT[:, 1, :, :], bc(EC[:, ds(2 * b + 1, 1), :].rearrange("p n h -> p (n h)"), 2, NS),
                                            ALU.mult).then_inc(c_ready, 1)
                    pool.wait_ge(y_made, PRIME + b)
                    settle(pool)
                    p(nc.gpsimd.tensor_tensor(dtx, xs4, bc(DT[:, 0, n, :], 3, HD), ALU.mult))
                    nc.gpsimd.tensor_tensor(dtxe, dtx[:, 0], bc(EC[:, ds(2 * b, 1), :].rearrange("p n h -> p (n h)"), 2, HD),
                                            ALU.mult).then_inc(dtx_made, 1)
                    p.end()

                mixer(0)
                with pool.Fori(1, B) as b:
                    mixer(b)

            @block.scalar
            def _(act):
                def save_btt(b):
                    act.wait_ge(btt_made, PRIME + b + 1)
                    act.wait_ge(products_made[1], PRIME + b)
                    nc.scalar.copy(BTT, bank(AUX).rearrange("p (a t) -> p a t", t=P)).then_inc(btt_saved, 1)

                def save_ctt(b):
                    act.wait_ge(ctt_made, PRIME + b + 1)
                    act.wait_ge(products_made[1], PRIME + b)
                    v = bank(AUX).rearrange("p (c r t) -> p c r t", c=CH, r=2)
                    z = CTZ.rearrange("p c (r two) t -> p c r two t", two=2)
                    nc.scalar.copy(z[0:64, :, :, 0, :], v[0:64])
                    nc.scalar.copy(z[64:P, :, :, 1, :], v[64:P]).then_inc(ctt_saved, 1)

                def make_decays(b, c):
                    act.wait_ge(seg_summed[c], PRIME + b + 1)
                    act.wait_ge(y_made, PRIME + b)
                    nc.scalar.activation(LM[:, c], bank(AUX).rearrange("p (h t) -> p h t", h=NH), ACT.Exp, scale=-1.0)\
                        .then_inc(decays_made[c], 1)

                def save_state(b):
                    act.wait_ge(state_made, PRIME + b + 1)
                    act.wait_ge(y_made, PRIME + b)
                    z = HZ.rearrange("p (r two) e -> p r two e", two=2)
                    v = bank(AUX)[:, 0:2 * HD].rearrange("p (r e) -> p r e", r=2)
                    nc.scalar.copy(z[0:64, :, 0, :], v[0:64])
                    nc.scalar.copy(z[64:P, :, 1, :], v[64:P])
                    nc.scalar.copy(CET, bank(AUX)[:, 2 * HD:2 * HD + 2 * P].rearrange("p (r t) -> p r t", r=2))\
                        .then_inc(state_saved, 1)

                def square_y(b):
                    r = Steps(act, rms_steps, b, RMS_STEPS)
                    act.wait_ge(x1_made, PRIME + b)
                    act.wait_ge(y_gated, PRIME + b + 1)
                    for c in range(CH):
                        r(nc.scalar.activation(junk, Y[:, c, :], ACT.Square, accum_out=rms[:, c:c + 1]))
                    r(nc.scalar.activation(rms[:, 2:4], rms[:, 0:2], ACT.Ln, bias=eps[:, :], scale=1.0 / DI))
                    r(nc.scalar.activation(rms[:, 4:6], rms[:, 2:4], ACT.Exp, scale=-0.5))
                    r.end()

                def save_yt(b):
                    act.wait_ge(yt_made, PRIME + b + 1)
                    act.wait_ge(mix_out, PRIME + b)
                    nc.scalar.copy(YT, bank(AUX).rearrange("p (a t) -> p a t", t=P)).then_inc(yt_saved, 1)

                def norm_scale(b):
                    r = Steps(act, norm_act, b, 2)
                    act.wait_ge(norm_summed, PRIME + b + 1)
                    r(nc.scalar.activation(ln[:, 4:6], ln[:, 2:4], ACT.Ln, bias=eps[:, :], scale=1.0 / D))
                    r(nc.scalar.activation(ln[:, 6:8], ln[:, 4:6], ACT.Exp, scale=-0.5))
                    r.end()

                def save_normed(b):
                    act.wait_ge(normed_turned, PRIME + b + 1)
                    act.wait_ge(q_made, PRIME + b)
                    nc.scalar.copy(lnT, bank(AUX)[:, 0:L]).then_inc(normed_saved, 1)

                def save_maxima(b, g):
                    act.wait_ge(max_turned, PRIME + 2 * b + g + 1)
                    act.wait_ge(max_stacked, PRIME + 16 * (2 * b + g))
                    nc.scalar.copy(MT[0:PARTS * NQ, :], bankb(AUX)[0:PARTS * NQ, 0:P]).then_inc(max_saved, 1)

                def exponentials(b, g, kt, js):
                    for j in js:
                        act.wait_ge(scored[j % 2], PRIME + score_fill(b, g, kt, j) + 1)
                        if j == 0:
                            act.wait_ge(summed[parity(g, kt)], PRIME + sum_count(b, g, kt))
                        nc.scalar.activation(PE_[:, parity(g, kt), j, :], bank(RING + j % 2), ACT.Exp).then_inc(powered[j % 2], 1)

                def body(b, last=False):
                    for kt in range(KT):
                        exponentials(b, 0, kt, (0, 1))
                        if not last:
                            first, then = MIX_SLOTS.get(kt, ((), ()))
                            run(first, b + 1)
                            exponentials(b, 0, kt, (2,))
                            run(then, b + 1)
                            exponentials(b, 0, kt, (3,))
                        else:
                            exponentials(b, 0, kt, (2, 3))
                    save_maxima(b, 1)
                    for kt in range(KT):
                        exponentials(b, 1, kt, range(NB))
                    if not last:
                        save_maxima(b + 1, 0)

                def run(stages, b):
                    for s in stages:
                        if s == "btt":
                            save_btt(b)
                        elif s == "ctt":
                            save_ctt(b)
                        elif s in ("seg0", "seg1"):
                            make_decays(b, int(s[-1]))
                        elif s == "state":
                            save_state(b)
                        elif s == "yt":
                            square_y(b)
                            save_yt(b)
                        elif s == "norm":
                            norm_scale(b)
                            save_normed(b)

                act.wait_ge(main_zeroed, 1)
                run(MIX_ORDER, 0)
                save_maxima(0, 0)
                body(0)
                with act.Fori(1, B - 1) as b:
                    body(b)
                body(B - 1, last=True)

            @block.vector
            def _(dve):
                def rotate_b(b):
                    m = Steps(dve, mix_steps, b, MIX_STEPS)
                    dve.wait_ge(btt_made, PRIME + b)
                    dve.wait_ge(state_made, PRIME + b)
                    settle(dve)
                    n = ds(2 * b, CH)
                    rotate(dve, m, BCD[:, n, 0:NS], BT, r1, r2, n, b_turned_in)
                    m.end()
                    dve.wait_ge(b_turned_in, PRIME + b + 1)

                def make_seg(b, c):
                    if c:
                        dve.wait_ge(seg_summed[0], PRIME + b + 1)
                    else:
                        dve.wait_ge(seg_summed[1], PRIME + b)
                    settle(dve)
                    adt = DT[:, 1, ds(2 * b + c, 1), :].rearrange("p n h -> p (n h)")
                    nc.vector.tensor_tensor(SR, bc(mask_le, 1, NH), bc(adt, 2, P), ALU.mult).then_inc(seg_made[c], 1)

                def mix(b, c):
                    dve.wait_ge(decays_made[c], PRIME + b + 1)
                    dve.wait_ge(products_made[c], PRIME + b + 1)
                    nc.vector.tensor_tensor(LM[:, c], LM[:, c], bank(AUX).rearrange("p (h t) -> p h t", h=NH), ALU.mult)\
                        .then_inc(mixed[c], 1)

                def gate_y(b):
                    n = ds(2 * b, CH)
                    dve.wait_ge(yt_made, PRIME + b)
                    settle(dve)
                    m = Steps(dve, S_("skip_steps"), b, 1)
                    y4 = Y.rearrange("p n (h e) -> p n h e", h=NH)
                    dsk = hb[:, 2, :].unsqueeze(1).unsqueeze(3).to_broadcast([P, CH, NH, HD])
                    m(nc.vector.tensor_tensor(y4, XS[:, n, :].rearrange("p n (h e) -> p n h e", h=NH), dsk, ALU.mult))
                    m.end()
                    dve.wait_ge(y_made, PRIME + b + 1)
                    nc.vector.tensor_tensor(Y, Y, bank(AUX).rearrange("p (c e) -> p c e", c=CH), ALU.add).then_inc(y_read, 1)
                    dve.wait_ge(y_read, PRIME + b + 1)
                    nc.vector.tensor_tensor(Y, Y, Z[:, n, :], ALU.mult).then_inc(y_gated, 1)

                def add_mixer(b):
                    n = ds(2 * b, CH)
                    dve.wait_ge(mix_out, PRIME + b + 1)
                    dve.wait_ge(rms_steps, RMS_STEPS * (b + 1))
                    settle(dve)
                    m = Steps(dve, norm_steps, b, NORM_STEPS)
                    m(nc.vector.tensor_tensor(lx, bank(AUX)[:, 0:L].rearrange("p (c d) -> p c d", c=CH), bc(rms[:, 4:6], 2, D), ALU.mult))
                    nc.vector.tensor_tensor(X[:, n, :], X[:, n, :], lx, ALU.add).then_inc(x1_made, 1)
                    dve.wait_ge(x1_made, PRIME + b + 1)
                    settle(dve)
                    m(nc.vector.reduce_sum(ln[:, 0:2], X[:, n, :], axis=AX.X))
                    m(nc.vector.tensor_scalar(ln[:, 0:2], ln[:, 0:2], -1.0 / D, None, ALU.mult))
                    dve.wait_ge(normed_turned, PRIME + b)
                    settle(dve)
                    m(nc.vector.tensor_tensor(lx, X[:, n, :], bc(ln[:, 0:2], 2, D), ALU.add))
                    m(nc.vector.tensor_tensor(lq, lx, lx, ALU.mult))
                    m.end()
                    nc.vector.reduce_sum(ln[:, 2:4], lq, axis=AX.X).then_inc(norm_summed, 1)

                def make_normed(b):
                    dve.wait_ge(norm_act, 2 * b + 2)
                    nc.vector.tensor_tensor(lx, lx, bc(ln[:, 6:8], 2, D), ALU.mult).then_inc(normed, 1)

                def split_q(b):
                    m = Steps(dve, q_steps, b, Q_STEPS)
                    dve.wait_ge(q_made, PRIME + b + 1)
                    nc.vector.tensor_scalar(QF, bank(AUX)[:, 0:L], bqS[:, :], None, ALU.add).then_inc(q_read, 1)
                    dve.wait_ge(q_read, PRIME + b + 1)
                    dve.wait_ge(q_in_dram, PRIME + 16 * PARTS * b)
                    m(nc.vector.tensor_copy(QP[:, 0, :], QF))
                    m(nc.vector.tensor_tensor(QF, QF, QP[:, 0, :], ALU.subtract))
                    m(nc.vector.tensor_copy(QP[:, 1, :], QF))
                    m.end()
                    nc.vector.tensor_tensor(QP[:, 2, :], QF, QP[:, 1, :], ALU.subtract).then_inc(q_split, 1)

                def run(stages, b):
                    for s in stages:
                        if s == "btt":
                            rotate_b(b)
                        elif s in ("seg0", "seg1"):
                            make_seg(b, int(s[-1]))
                        elif s in ("mix0", "mix1"):
                            mix(b, int(s[-1]))
                        elif s == "y":
                            gate_y(b)
                        elif s == "out":
                            add_mixer(b)
                        elif s == "norm":
                            make_normed(b)
                        elif s == "q":
                            split_q(b)

                def take_max(b, g, u):
                    qt, par = u // 2, u % 2
                    dve.wait_ge(unit_made[par], PRIME + (2 * b + g) * NQ + qt + 1)
                    nc.vector.tensor_reduce(NMX[:, par, qt:qt + 1], PS[:, UNIT + 2 * par:UNIT + 2 * par + 2, 0:HALF],
                                            axis=AX.XY, op=ALU.max, negate=True).then_inc(unit_taken[par], 1)

                def split_maxima(b, g):
                    m = Steps(dve, max_steps, 2 * b + g, MAX_STEPS)
                    for par in range(2):
                        dve.wait_ge(unit_taken[par], PRIME + (2 * b + g + 1) * NQ)
                    dve.wait_ge(max_turned, PRIME + 2 * b + g)
                    m(nc.vector.tensor_tensor(NM, NMX[:, 0, :], NMX[:, 1, :], ALU.min))
                    m(nc.vector.tensor_copy(MP[:, 0, :], NM))
                    m(nc.vector.tensor_tensor(NR, NM, MP[:, 0, :], ALU.subtract))
                    m(nc.vector.tensor_copy(MP[:, 1, :], NR))
                    m.end()
                    nc.vector.tensor_tensor(MP[:, 2, :], NR, MP[:, 1, :], ALU.subtract).then_inc(max_split, 1)
                    dve.wait_ge(max_split, PRIME + 2 * b + g + 1)

                def keys_for_max(b):
                    for par in range(2):
                        dve.wait_ge(unit_taken[par], PRIME + 2 * b * NQ)
                    settle(dve)
                    nc.vector.tensor_copy(KSa[0:MROW, :], KSall[0:MROW, ds(b, 1), :].rearrange("p b s -> p (b s)"))\
                        .then_inc(keys_max, 1)

                def keys_for_exp(b):
                    dve.wait_ge(scored[1], PRIME + score_fill(b, 0, 0, 0))
                    settle(dve)
                    nc.vector.tensor_copy(KSb, KSall[:, ds(b, 1), :].rearrange("p b s -> p (b s)")).then_inc(keys_exp, 1)

                def values(b):
                    for par in range(2):
                        dve.wait_ge(summed[par], PRIME + KT * b)
                    settle(dve)
                    nc.vector.tensor_copy(Vc, Vall[:, ds(b, 1), :, :].rearrange("p b k e -> p (b k) e")).then_inc(values_ready, 1)

                def save_sums(b, g):
                    dve.wait_ge(summed[parity(g, KT - 1)], PRIME + sum_count(b, g, KT - 1) + 1)
                    dve.wait_ge(sums_turned, PRIME + 2 * b + g)
                    nc.vector.tensor_copy(OT, bank(ACC)).then_inc(sums_saved, 1)

                def finish(b, g):
                    m = Steps(dve, out_steps, 2 * b + g, 1)
                    v = bank(AUX).rearrange("p (s j e) -> p s j e", s=4, j=NB)
                    dve.wait_ge(sums_turned, PRIME + 2 * b + g + 1)
                    m(nc.vector.reciprocal(rdn.rearrange("p (s j) -> p s j", s=4), v[:, :, :, DK]))
                    m.end()
                    for s in range(4):
                        hh, c = s // 2, s % 2
                        to = ONall[:, ds(2 * b + c, 1), g * 64:g * 64 + 64].rearrange("p n (j hh d) -> p (n j) hh d", hh=2, d=DK)
                        last = nc.vector.tensor_tensor(to[:, :, hh, :], v[:, s, :, 0:DK], bc(rdn[:, 4 * s:4 * s + 4], 2, DK), ALU.mult)
                    last.then_inc(heads_out, 1)

                def body(b, first=False, last=False):
                    if not first:
                        keys_for_exp(b)
                        save_sums(b - 1, 1)
                        values(b)
                    for kt in range(KT):
                        if kt == 1 and not first:
                            finish(b - 1, 1)
                        todo = list(units(kt, 0))
                        slots = ((), ()) if last else MIX_SLOTS.get(kt, ((), ()))
                        for part, stages in ((todo[0:1], slots[0]), (todo[1:2], slots[1]), (todo[2:], ())):
                            for u in part:
                                take_max(b, 1, u)
                            run(stages, b + 1)
                    split_maxima(b, 1)
                    if not last:
                        keys_for_max(b + 1)
                    save_sums(b, 0)
                    for kt in range(KT):
                        if kt == 1:
                            finish(b, 0)
                        if not last:
                            for u in units(kt, 1):
                                take_max(b + 1, 0, u)
                    if not last:
                        split_maxima(b + 1, 0)

                dve.wait_ge(main_zeroed, 1)
                nc.vector.tensor_copy(KSa[0:MROW, :], KSall[0:MROW, 0, :]).then_inc(keys_max, 1)
                nc.vector.tensor_copy(KSb, KSall[:, 0, :]).then_inc(keys_exp, 1)
                nc.vector.tensor_copy(Vc, Vall[:, 0, :, :]).then_inc(values_ready, 1)
                run(MIX_ORDER, 0)
                for u in range(2 * NQ):
                    take_max(0, 0, u)
                split_maxima(0, 0)
                body(0, first=True)
                with dve.Fori(1, B - 1) as b:
                    body(b)
                body(B - 1, last=True)
                save_sums(B - 1, 1)
                finish(B - 1, 1)

            @block.tensor
            def _(pe):
                def turn_b(b, free):
                    pe.wait_ge(*free)
                    pe.wait_ge(b_turned_in, PRIME + b + 1)
                    pe.wait_ge(b_plain, PRIME + b + 1)
                    for c in range(CH):
                        for r in range(2):
                            at = (2 * c + r) * P
                            last = nc.tensor.transpose(bank(AUX)[:, at:at + P], BT[:, c, 2 * r:2 * r + 2, :].rearrange("p h n -> p (h n)"), ident)
                    last.then_inc(btt_made, 1)

                def turn_c(b, free):
                    pe.wait_ge(*free)
                    pe.wait_ge(c_ready, PRIME + b + 1)
                    for c in range(CH):
                        for r in range(2):
                            at = (2 * c + r) * P
                            last = nc.tensor.transpose(bank(AUX)[:, at:at + P], CT[:, c, 2 * r:2 * r + 2, :].rearrange("p h n -> p (h n)"), ident)
                    last.then_inc(ctt_made, 1)

                def sum_seg(b, c, free):
                    pe.wait_ge(*free)
                    pe.wait_ge(seg_made[c], PRIME + b + 1)
                    nc.tensor.matmul(bank(AUX), mask_gt, SR.rearrange("p h t -> p (h t)"), start=True, stop=False)
                    nc.tensor.matmul(bank(AUX), identb[:, :], bigb[:, :, :].rearrange("p h t -> p (h t)"), start=False, stop=True)\
                        .then_inc(seg_summed[c], 1)

                def products(b, c, free):
                    pe.wait_ge(*free)
                    if c == 0:
                        pe.wait_ge(btt_saved, PRIME + b + 1)
                        pe.wait_ge(ctt_saved, PRIME + b + 1)
                    for h in range(NH):
                        last = nc.tensor.matmul(bank(AUX)[:, h * P:(h + 1) * P], BTT[:, 2 * c + h // 2, :], CTZ[:, c, h, :],
                                                start=True, stop=True)
                    last.then_inc(products_made[c], 1)

                def state(b, free):
                    pe.wait_ge(*free)
                    pe.wait_ge(dtx_made, PRIME + b + 1)
                    for h in range(NH):
                        r = 64 * (h % 2)
                        nc.tensor.matmul(PS[r:r + 64, AUX, (h // 2) * HD:(h // 2 + 1) * HD], BT[:, 0, h, :], dtxe[:, h, :],
                                         start=True, stop=True)
                    for r in range(2):
                        at = 2 * HD + r * P
                        last = nc.tensor.transpose(bank(AUX)[:, at:at + P], CE[:, 2 * r:2 * r + 2, :].rearrange("p h n -> p (h n)"), ident)
                    last.then_inc(state_made, 1)

                def outputs(b, free):
                    pe.wait_ge(*free)
                    pe.wait_ge(mixed[0], PRIME + b + 1)
                    for c in range(CH):
                        for h in range(NH):
                            to = bank(AUX)[:, c * DI + h * HD:c * DI + (h + 1) * HD]
                            last = nc.tensor.matmul(to, LM[:, c, h, :], dtx[:, c, h, :], start=True, stop=c == 0)
                            if c:
                                last = nc.tensor.matmul(to, CET[:, h // 2, :], HZ[:, h, :], start=False, stop=True)
                    last.then_inc(y_made, 1)

                def turn_y(b, free):
                    pe.wait_ge(*free)
                    pe.wait_ge(y_gated, PRIME + b + 1)
                    for c in range(CH):
                        for r in range(2):
                            at = (2 * c + r) * P
                            last = nc.tensor.transpose(bank(AUX)[:, at:at + P], Y[:, c, r * P:(r + 1) * P], ident)
                    last.then_inc(yt_made, 1)

                def project_y(b, free):
                    pe.wait_ge(*free)
                    for c in range(CH):
                        for r in range(2):
                            last = nc.tensor.matmul(bank(AUX)[:, c * D:(c + 1) * D], YT[:, 2 * c + r, :], Wout[:, r, :],
                                                    start=r == 0, stop=r == 1)
                    last.then_inc(mix_out, 1)

                def turn_normed(b, free):
                    pe.wait_ge(*free)
                    pe.wait_ge(normed, PRIME + b + 1)
                    for c in range(CH):
                        last = nc.tensor.transpose(bank(AUX)[:, c * P:(c + 1) * P], lx[:, c, :], ident)
                    last.then_inc(normed_turned, 1)

                def project_q(b, free):
                    pe.wait_ge(*free)
                    nc.tensor.matmul(bank(AUX)[:, 0:L], WqS[:, :], lnT, start=True, stop=True).then_inc(q_made, 1)

                def run(stages, b, before):
                    one = PRIME + b + 1
                    for s in stages:
                        if s == "btt":
                            turn_b(b, before)
                            before = btt_saved, one
                        elif s == "ctt":
                            turn_c(b, before)
                            before = ctt_saved, one
                        elif s in ("seg0", "seg1"):
                            sum_seg(b, int(s[-1]), before)
                            before = decays_made[int(s[-1])], one
                        elif s in ("mix0", "mix1"):
                            products(b, int(s[-1]), before)
                            before = mixed[int(s[-1])], one
                        elif s == "state":
                            state(b, before)
                            before = state_saved, one
                        elif s == "y":
                            outputs(b, before)
                            before = y_read, one
                        elif s == "yt":
                            turn_y(b, before)
                            before = yt_saved, one
                        elif s == "out":
                            project_y(b, before)
                            before = x1_made, one
                        elif s == "norm":
                            turn_normed(b, before)
                            before = normed_saved, one
                        elif s == "q":
                            project_q(b, before)
                            before = q_read, one
                    return before

                def fill_unit(b, g, u):
                    qt, par = u // 2, u % 2
                    pe.wait_ge(unit_taken[par], PRIME + (2 * b + g) * NQ + qt)
                    if u == 0:
                        pe.wait_ge(q_stacked[g], PRIME + 16 * PARTS * (b + 1))
                        pe.wait_ge(keys_max, b + 1)
                    for k in range(2):
                        at = SPANS[par][k]
                        last = nc.tensor.matmul(PS[:, UNIT + 2 * par + k, 0:HALF], Qg[g][:, qt * P:(qt + 1) * P],
                                                KSa[:, at:at + HALF], start=True, stop=True)
                    last.then_inc(unit_made[par], 1)

                def turn_maxima(b, g, free):
                    pe.wait_ge(*free)
                    pe.wait_ge(max_split, PRIME + 2 * b + g + 1)
                    settle(pe)
                    nc.tensor.transpose(bankb(AUX)[0:PARTS * NQ, 0:P], MP.rearrange("p i q -> p (i q)"), identb[:, :])\
                        .then_inc(max_turned, 1)
                    return max_saved, PRIME + 2 * b + g + 1

                def score(b, g, kt, j):
                    pe.wait_ge(powered[j % 2], PRIME + score_fill(b, g, kt, j))
                    if kt == 0 and j == 0:
                        pe.wait_ge(max_stacked, PRIME + 16 * (2 * b + g + 1))
                        if g == 0:
                            pe.wait_ge(keys_exp, b + 1)
                    nc.tensor.matmul(bank(RING + j % 2), KSb[:, kt * P:(kt + 1) * P], Qg[g][:, j * 512:(j + 1) * 512],
                                     start=True, stop=True).then_inc(scored[j % 2], 1)

                def weigh(b, g, kt):
                    for r in range(2):
                        pe.wait_ge(powered[r], PRIME + score_fill(b, g, kt, 2) + 1)
                    if kt == 0:
                        pe.wait_ge(sums_saved, PRIME + 2 * b + g)
                        if g == 0:
                            pe.wait_ge(values_ready, b + 1)
                    for j in range(NB):
                        last = nc.tensor.matmul(PS[32 * j:32 * j + 32, ACC, :], Vc[:, kt, :], PE_[:, parity(g, kt), j, :],
                                                start=kt == 0, stop=kt == KT - 1)
                    last.then_inc(summed[parity(g, kt)], 1)

                def finish(b, g, free):
                    pe.wait_ge(*free)
                    pe.wait_ge(sums_saved, PRIME + 2 * b + g + 1)
                    for s in range(4):
                        last = nc.tensor.transpose(bank(AUX)[:, s * P:(s + 1) * P], OT[:, s * P:(s + 1) * P], ident)
                    last.then_inc(sums_turned, 1)
                    return heads_out, PRIME + 2 * b + g + 1

                def body(b, first=False, last=False):
                    aux = max_saved, PRIME + 2 * b + 1
                    for g in range(2):
                        more = not (g == 1 and last)
                        for kt in range(KT):
                            slots = MIX_SLOTS.get(kt, ((), ())) if g == 0 and not last else ((), ())
                            todo = list(units(kt, g)) if more else []
                            to = (b, 1) if g == 0 else (b + 1, 0)
                            score(b, g, kt, 0)
                            for u in todo[0:1]:
                                fill_unit(*to, u)
                            score(b, g, kt, 1)
                            if kt:
                                weigh(b, g, kt - 1)
                            elif g:
                                weigh(b, 0, KT - 1)
                            elif not first:
                                weigh(b - 1, 1, KT - 1)
                            if kt == 1 and (g or not first):
                                aux = finish(*((b, 0) if g else (b - 1, 1)), aux)
                            aux = run(slots[0], b + 1, aux)
                            score(b, g, kt, 2)
                            for u in todo[1:2]:
                                fill_unit(*to, u)
                            aux = run(slots[1], b + 1, aux)
                            score(b, g, kt, 3)
                            for u in todo[2:]:
                                fill_unit(*to, u)
                        if more:
                            aux = turn_maxima(*to, aux)
                    return aux

                pe.wait_ge(main_zeroed, 1)
                aux = run(MIX_ORDER, 0, (main_zeroed, 1))
                for u in range(2 * NQ):
                    fill_unit(0, 0, u)
                turn_maxima(0, 0, aux)
                body(0, first=True)
                with pe.Fori(1, B - 1) as b:
                    body(b)
                aux = body(B - 1, last=True)
                weigh(B - 1, 1, KT - 1)
                finish(B - 1, 1, aux)

        with nc.Block() as block:
            copied, on_turned, onT_saved, o_made, x2_made = (S_(n) for n in ("on_copied", "on_turned", "onT_saved", "o_made", "x2_made"))
            bias_added = S_("bias_added")
            ln3_vec, ln3_act = S_("ln3_vec"), S_("ln3_act")
            xn3_made, x3_turned, x3_saved, lg_made, lg_saved = (S_(n) for n in ("xn3_made", "x3_turned", "x3_saved", "lg_made", "lg_saved"))
            top_steps, lg_exp, coef_split, coef_turned, coef_saved = (S_(n) for n in ("top_steps", "lg_exp", "coef_split", "coef_turned", "coef_saved"))
            gate_made = [S_("gate_made0"), S_("gate_made1")]
            gate_used = [S_("gate_used0"), S_("gate_used1")]
            up_made = [S_("up_made0"), S_("up_made1")]
            up_used = [S_("up_used0"), S_("up_used1")]
            gated, down_made, out_made, stored = S_("gated"), S_("down_made"), S_("out_made"), S_("stored")
            TB = 512
            fills = [len(range(par, HT, 2)) for par in range(2)]

            def count(q, k):
                return fills[k % 2] * q + k // 2

            @block.sync
            def _(sp):
                o = out.rearrange("b (c p) d -> p (b c) d", p=P)
                with sp.Fori(0, NT * P // TB) as q:
                    sp.wait_ge(out_made, PRIME + q + 1)
                    sp.dma_start(o[:, ds(4 * q, 4), :], X[:, ds(4 * q, 4), :]).then_inc(stored, 16)
                sp.wait_ge(stored, 16 * (NT * P // TB))

            @block.scalar
            def _(act):
                with act.Fori(0, B) as b:
                    act.wait_ge(on_turned, PRIME + b)
                    settle(act)
                    nc.scalar.copy(xns[:, :, :], ONall[:, ds(2 * b, CH), :]).then_inc(copied, 1)
                    act.wait_ge(on_turned, PRIME + b + 1)
                    act.wait_ge(o_made, PRIME + b)
                    nc.scalar.copy(xnT[:, :, :], bank(0)[:, 0:CH * P].rearrange("p (c t) -> p c t", c=CH)).then_inc(onT_saved, 1)
                act.wait_ge(ln3_vec, LN_STEPS)
                a = Steps(act, ln3_act)
                a(nc.scalar.activation(st[:, 2, :], st[:, 1, :], ACT.Ln, bias=eps[:, :], scale=1.0 / D))
                a(nc.scalar.activation(st[:, 3, :], st[:, 2, :], ACT.Exp, scale=-0.5))
                with act.Fori(0, B) as b:
                    act.wait_ge(x3_turned, PRIME + b + 1)
                    act.wait_ge(lg_made, PRIME + b)
                    settle(act)
                    v = bank(2)[:, 0:L]
                    nc.scalar.copy(X3T[:, ds(L * b, L)], v)
                    nc.scalar.copy(xnT.rearrange("p c t -> p (c t)"), v).then_inc(x3_saved, 1)
                act.wait_ge(top_steps, TOP_SHIFT)
                nc.scalar.activation(SH, SH, ACT.Exp).then_inc(lg_exp, 1)
                act.wait_ge(coef_turned, 2)
                nc.scalar.copy(CTs[:, :].rearrange("p (k t) -> p k t", k=2),
                               PS[0:PARTS * NE, 4:6, :].bitcast(bf16)).then_inc(coef_saved, 1)
                with act.Fori(0, NT * P // TB) as q:
                    for k in range(HT):
                        act.wait_ge(gate_made[k % 2], PRIME + count(q, k) + 1)
                        act.wait_ge(up_used[k % 2], PRIME + count(q, k))
                        nc.scalar.activation(SG[:, k % 2, :], bank(k % 2), ACT.Silu).then_inc(gate_used[k % 2], 1)

            @block.vector
            def _(dve):
                nc.vector.tensor_tensor(X[:, :, :], X[:, :, :], bc(boS[:, :], 1, NT), ALU.add).then_inc(bias_added, 1)
                dve.wait_ge(bias_added, 1)
                with dve.Fori(0, B) as b:
                    dve.wait_ge(o_made, PRIME + b + 1)
                    settle(dve)
                    n = ds(2 * b, CH)
                    nc.vector.tensor_tensor(X[:, n, :], X[:, n, :], bank(1)[:, 0:L].rearrange("p (c d) -> p c d", c=CH), ALU.add)\
                        .then_inc(x2_made, 1)
                dve.wait_ge(x2_made, PRIME + B)
                v = Steps(dve, ln3_vec)
                layer_norm_sums(v, X[:, :, :], XC, SQ, st)
                dve.wait_ge(ln3_act, 2)
                with dve.Fori(0, B) as b:
                    dve.wait_ge(x3_turned, PRIME + b)
                    settle(dve)
                    n = ds(2 * b, CH)
                    nc.vector.tensor_tensor(xns[:, :, :], XC[:, n, :], bc(st[:, 3, n], 2, D), ALU.mult).then_inc(xn3_made, 1)
                    dve.wait_ge(lg_made, PRIME + b + 1)
                    settle(dve)
                    nc.vector.tensor_copy(LG[:, n, :], bank(3)[:, 0:CH * NE].rearrange("p (c e) -> p c e", c=CH)).then_inc(lg_saved, 1)
                t = Steps(dve, top_steps)
                dve.wait_ge(lg_saved, PRIME + B)
                t(nc.vector.tensor_reduce(red, LG, axis=AX.X, op=ALU.max))
                t(nc.vector.tensor_tensor(SH, LG, bc(red, 2, NE), ALU.subtract))
                assert t.k == TOP_SHIFT
                dve.wait_ge(lg_exp, 1)
                t(nc.vector.reduce_sum(red, SH, axis=AX.X))
                t(nc.vector.reciprocal(rcp, red))
                t(nc.vector.tensor_tensor(PB, SH, bc(rcp, 2, NE), ALU.mult))
                t(nc.vector.tensor_copy(SH, PB))
                for picked in (S1, S2_):
                    t(nc.vector.tensor_reduce(red, SH, axis=AX.X, op=ALU.max))
                    t(nc.vector.tensor_tensor(KY, SH, bc(red, 2, NE), ALU.is_equal))
                    t(nc.vector.tensor_tensor(KY, KY, bc(rank, 1, NT), ALU.mult))
                    t(nc.vector.tensor_reduce(red, KY, axis=AX.X, op=ALU.max))
                    t(nc.vector.tensor_tensor(picked, KY, bc(red, 2, NE), ALU.is_equal))
                    t(nc.vector.scalar_tensor_tensor(SH, picked, -2.0, SH, ALU.mult, ALU.add))
                t(nc.vector.tensor_tensor(S1, S1, S2_, ALU.add))
                t(nc.vector.tensor_tensor(CR, PB, S1, ALU.mult))
                part = [CP[:, :, i * NE:(i + 1) * NE] for i in range(PARTS)]
                t(nc.vector.tensor_copy(part[0], CR))
                t(nc.vector.tensor_tensor(CR, CR, part[0], ALU.subtract))
                t(nc.vector.tensor_copy(part[1], CR))
                nc.vector.tensor_tensor(part[2], CR, part[1], ALU.subtract).then_inc(coef_split, 1)
                with dve.Fori(0, NT * P // TB) as q:
                    dve.wait_ge(down_made, PRIME + q)
                    for k in range(HT):
                        par = k % 2
                        dve.wait_ge(gate_used[par], PRIME + count(q, k) + 1)
                        dve.wait_ge(up_made[par], PRIME + count(q, k) + 1)
                        if k < HT - 1:
                            g = Steps(dve, gated, q, HT - 1)
                            g.k = k
                            g(nc.vector.tensor_tensor(Hb[:, k, :], SG[:, par, :], bank(2 + par), ALU.mult))
                            nc.vector.tensor_tensor(Hb[:, k, :], Hb[:, k, :], bank(4 + par), ALU.mult).then_inc(up_used[par], 1)
                        else:
                            nc.vector.tensor_tensor(Hb[:, k, :], SG[:, par, :], bank(2 + par), ALU.mult).then_inc(up_used[par], 1)
                    dve.wait_ge(down_made, PRIME + q + 1)
                    settle(dve)
                    n = ds(4 * q, 4)
                    nc.vector.tensor_tensor(X[:, n, :], X[:, n, :], bank(6).rearrange("p (n d) -> p n d", n=4), ALU.add)\
                        .then_inc(out_made, 1)

            @block.tensor
            def _(pe):
                with pe.Fori(0, B) as b:
                    pe.wait_ge(copied, PRIME + b + 1)
                    pe.wait_ge(onT_saved, PRIME + b)
                    for c in range(CH):
                        last = nc.tensor.transpose(bank(0)[:, c * P:(c + 1) * P], xns[:, c, :], ident)
                    last.then_inc(on_turned, 1)
                    pe.wait_ge(onT_saved, PRIME + b + 1)
                    pe.wait_ge(x2_made, PRIME + b)
                    for c in range(CH):
                        last = nc.tensor.matmul(bank(1)[:, c * D:(c + 1) * D], xnT[:, c, :], WoS[:, :], start=True, stop=True)
                    last.then_inc(o_made, 1)
                with pe.Fori(0, B) as b:
                    pe.wait_ge(xn3_made, PRIME + b + 1)
                    pe.wait_ge(x3_saved, PRIME + b)
                    for c in range(CH):
                        last = nc.tensor.transpose(bank(2)[:, c * P:(c + 1) * P], xns[:, c, :], ident)
                    last.then_inc(x3_turned, 1)
                    pe.wait_ge(x3_saved, PRIME + b + 1)
                    pe.wait_ge(lg_saved, PRIME + b)
                    for c in range(CH):
                        last = nc.tensor.matmul(bank(3)[:, c * NE:(c + 1) * NE], xnT[:, c, :], RT[:, :], start=True, stop=True)
                    last.then_inc(lg_made, 1)
                pe.wait_ge(coef_split, 1)
                for n in range(NT):
                    last = nc.tensor.transpose(bankb(4 + n // 8)[0:PARTS * NE, (n % 8) * P:(n % 8 + 1) * P],
                                               CP[:, n, 0:PARTS * NE], identb[:, :])
                    if n % 8 == 7:
                        last.then_inc(coef_turned, 1)
                pe.wait_ge(coef_saved, 1)
                with pe.Fori(0, NT * P // TB) as q:
                    tok = ds(TB * q, TB)
                    for k in range(HT):
                        par = k % 2
                        pe.wait_ge(gate_used[par], PRIME + count(q, k))
                        nc.tensor.matmul(bank(par), WG[:, k * P:(k + 1) * P], X3T[:, tok], start=True, stop=True)\
                            .then_inc(gate_made[par], 1)
                        pe.wait_ge(up_used[par], PRIME + count(q, k))
                        last = nc.tensor.matmul(bank(2 + par), WU[:, k * P:(k + 1) * P], X3T[:, tok], start=True, stop=True)
                        if k < HT - 1:
                            last = nc.tensor.matmul(bank(4 + par), selb[:, k, :], CTs[:, tok], start=True, stop=True)
                        last.then_inc(up_made[par], 1)
                    for par in range(2):
                        pe.wait_ge(up_used[par], PRIME + fills[par] * (q + 1))
                    pe.wait_ge(out_made, PRIME + q)
                    for t in range(TB // P):
                        for k in range(HT):
                            last = nc.tensor.matmul(bank(6)[:, t * D:(t + 1) * D], Hb[:, k, t * P:(t + 1) * P], WD[:, k, :],
                                                    start=k == 0, stop=k == HT - 1)
                    last.then_inc(down_made, 1)


def kernel(**inputs):
    import concourse.bacc as bacc
    from concourse.bass_utils import run_bass_kernel_spmd

    names = ["x", "ctx_1024", "L0_attn_W_in", "L0_attn_W_out", "L0_attn_dt_bias", "L0_attn_A_log", "L0_attn_D_skip",
             "L0_attn_norm_weight", "L0_xattn_Wq", "L0_xattn_bq", "L0_xattn_Wk", "L0_xattn_bk", "L0_xattn_Wv",
             "L0_xattn_bv", "L0_xattn_Wo", "L0_xattn_bo", "L0_ffn_router", "L0_ffn_experts_gate",
             "L0_ffn_experts_up", "L0_ffn_experts_down", "L0_ffn_shared_gate", "L0_ffn_shared_up",
             "L0_ffn_shared_down"]
    nc = bacc.Bacc("TRN2", target_bir_lowering=False, num_devices=1)
    arrays, args = {}, []
    for name in names + ["shape_constants"]:
        a = np.ascontiguousarray(inputs[name] if name in inputs else shape_constants())
        arrays[f"in_{name}"] = a
        args.append(nc.dram_tensor(f"in_{name}", a.shape, mybir.dt.from_np(a.dtype), kind="ExternalInput").ap())
    out = nc.dram_tensor("out_0", (B, L, D), mybir.dt.float32, kind="ExternalOutput").ap()
    build(nc, *args, out)
    r = run_bass_kernel_spmd(nc, [arrays], core_ids=[0])
    return r.results[0]["out_0"]
```

```python
from contextlib import ExitStack

import numpy as np

import concourse.bass as bass
from concourse import mybir

B, L, D = 8, 256, 128
P = 128
CH = L // P
NT = B * CH
NH, HD, NS = 4, 64, 64
DI = NH * HD
PAIRS = 16
XH, DK = 16, 8
S = 1601
KT = -(-S // P)
SP = KT * P
TAIL = S - (KT - 1) * P
NE, ED, SD = 8, 64, 128
HT = (NE * ED + SD) // P
EPS = 1e-5
PARTS = 3
QK = PARTS * PARTS * DK
MROW = 96
GH = XH // 2
GC = GH * L
NB = GC // 512
NQ = GC // P
SPANS = 4
SPAN = -(-S // SPANS)
LOGCAP = 200.0
ROUND = 1.5 * 2.0 ** 23
TWO_PI_HI = float(np.float32(6.28125))
TWO_PI_LO = float(np.float32(2 * np.pi - 6.28125))
PI = float(np.nextafter(np.float32(np.pi), np.float32(0)))
SCRATCH = 18200
CST_IDENT, CST_GT, CST_LE, CST_FREQ, CST_RANK, CST_SEL, CST_W = 0, 128, 256, 384, 400, 408, 408 + 4 * 128


def shape_constants():
    c = np.zeros((P, CST_W), np.float32)
    r = np.arange(P)
    c[:, CST_IDENT:CST_IDENT + P] = np.eye(P)
    c[:, CST_GT:CST_GT + P] = r[:, None] > r[None, :]
    c[:, CST_LE:CST_LE + P] = r[:, None] <= r[None, :]
    freq = np.float32(1.0) / np.power(np.float32(10000.0), np.arange(PAIRS, dtype=np.float32) / np.float32(PAIRS))
    c[:, CST_FREQ:CST_FREQ + PAIRS] = freq.astype(np.float32)
    c[:, CST_RANK:CST_RANK + NE] = NE - np.arange(NE)
    for k in range(HT - 1):
        for row in range(PARTS * NE):
            e = row % NE
            if e // 2 == k:
                at = CST_SEL + k * P + (e % 2) * ED
                c[row, at:at + ED] = 1.0
    return c


class Steps:

    def __init__(self, eng, sem, index=0, per=0, settle=None):
        self.eng, self.sem, self.base, self.per, self.k, self.settle = eng, sem, index * per, per, 0, settle

    def __call__(self, ins):
        self.k += 1
        ins.then_inc(self.sem, 1)
        self.eng.wait_ge(self.sem, self.base + self.k)
        if self.settle:
            self.settle(self.eng)

    def end(self):
        assert self.k == self.per, (self.sem, self.k, self.per)


PRIME = 2
PRIMED = (("projected", 2), ("z_saved", 2), ("bcd_saved", 2), ("xnT_saved", 0), ("xn_turned", 0), ("ctxT_saved", 4),
          ("kv_made", 0), ("kv_turned", 0), ("v_saved", 0), ("k_stacked", 0), ("ks_turned", 2), ("ks_saved", 2),
          ("b_rotated", 0), ("b_plain", 0), ("c_ready", 0), ("dtx_made", 0), ("seg_made", 2), ("btt_made", 0),
          ("btt_saved", 0), ("ctt_made", 0), ("ctt_saved", 0), ("seg_summed", 2), ("decays_made", 2),
          ("products_made", 2), ("mixed", 2), ("state_made", 0), ("state_saved", 0), ("y_made", 0), ("y_read", 0),
          ("y_gated", 0), ("yt_made", 0), ("yt_saved", 0), ("mix_out", 0), ("raw_saved", 0), ("squared", 0),
          ("q_stacked", 4), ("keys_max", 0), ("keys_exp", 0), ("values_ready", 0),
          ("unit_made", SPANS), ("unit_taken", SPANS), ("max_split", 0), ("max_turned", 0),
          ("max_saved", 0), ("max_stacked", 0), ("scored", 2), ("powered", 2), ("summed", 2), ("sums_saved", 0),
          ("sums_turned", 0), ("heads_out", 0),
          ("gate_made", 2), ("gate_used", 2),
          ("up_made", 2), ("up_used", 2), ("down_made", 0), ("out_made", 0))
TOP_SHIFT = 3
EB = 2
AHEAD = 10
UNITS_AT = (5, 4, 5, 5, 5, 5, 5, 5, 5, 6, 4, 5, 5)
POOL_STEPS, MIX_STEPS, SQUARE_STEPS, MAX_STEPS = 8, 5, 1, 4
N_SMALL = 21
LN_STEPS, MID_E, MID_U, MID_DT, MID_CUM, K_STEPS = 5, 2, 3, 11, 15, 4


def layer_norm_sums(step, X, XC, SQ, st):
    ALU, AX = mybir.AluOpType, mybir.AxisListType
    v = step.eng
    step(v.reduce_sum(st[:, 0, :], X, axis=AX.X))
    step(v.tensor_scalar(st[:, 0, :], st[:, 0, :], -1.0 / D, None, ALU.mult))
    step(v.tensor_tensor(XC, X, bc(st[:, 0, :], 2, D), ALU.add))
    step(v.tensor_tensor(SQ, XC, XC, ALU.mult))
    step(v.reduce_sum(st[:, 1, :], SQ, axis=AX.X))


def bc(ap, axis, n):
    v = ap.unsqueeze(axis)
    shape = list(v.shape)
    shape[axis] = n
    return v.to_broadcast(shape)


def build(nc, x, ctx_1024, W_in, W_out, dt_bias, A_log, D_skip, norm_weight, Wq, bq, Wk, bk, Wv, bv, Wo, bo,
          router, e_gate, e_up, e_down, s_gate, s_up, s_down, consts, out):
    f32, bf16 = mybir.dt.float32, mybir.dt.bfloat16
    ALU, ACT, AX = mybir.AluOpType, mybir.ActivationFunctionType, mybir.AxisListType
    ds = bass.ds
    es = ExitStack()
    with es:
        def sb(name, shape, dt=f32):
            return es.enter_context(nc.sbuf_tensor(name, shape, dt))

        def sem(name):
            return es.enter_context(nc.semaphore(name))

        X = sb("X", [P, NT, D])
        Z = sb("Z", [P, NT, DI])
        XS = sb("XS", [P, NT, DI])
        BCD = sb("BCD", [P, NT, 2 * NS + NH])
        COS = sb("COS", [P, NT, NH, PAIRS])
        SIN = sb("SIN", [P, NT, NH, PAIRS])
        KSall = sb("KSall", [P, B, SP], bf16)
        Vall = sb("Vall", [P, B, KT, 32])
        ONall = sb("ONall", [P, NT, D])
        CST = sb("CST", [P, CST_W])
        identb = sb("identb", [P, P], bf16)
        selb = sb("selb", [PARTS * NE, HT - 1, P], bf16)
        bigb = sb("bigb", [P, NH, P], bf16)
        Win = sb("Win", [P, 2 * DI + 2 * NS + NH])
        Wout = sb("Wout", [P, 2, D])
        nw = sb("nw", [P, 2])
        eps = sb("eps", [P, 1])
        hb = sb("hb", [P, 3, NH])
        WqS = sb("WqS", [P, D])
        bqS = sb("bqS", [P, 1])
        WkvS = sb("WkvS", [P, 32])
        bkvS = sb("bkvS", [P, 1])
        WoS = sb("WoS", [P, D])
        boS = sb("boS", [P, D])
        RT = sb("RT", [P, NE])
        WG = sb("WG", [P, HT * P])
        WU = sb("WU", [P, HT * P])
        WD = sb("WD", [P, HT, D])
        ident = CST[:, CST_IDENT:CST_IDENT + P]
        mask_gt = CST[:, CST_GT:CST_GT + P]
        mask_le = CST[:, CST_LE:CST_LE + P]
        freq = CST[:, CST_FREQ:CST_FREQ + PAIRS]
        rank = CST[:, CST_RANK:CST_RANK + NE]
        st = sb("st", [P, 4, NT])
        DT = sb("DT", [P, 2, NT, NH])
        CUM = sb("CUM", [P, 2, NT, NH])
        EC = sb("EC", [P, NT, NH])
        tm = sb("tm", [P, 6, NT * NH])
        rs = sb("rs", [P, 3, NT])

        SCR = sb("SCR", [P, SCRATCH])
        taken = [0]

        def scr(shape, dt=f32):
            n = int(np.prod(shape)) * (2 if dt == bf16 else 4) // 4
            v = SCR[:, taken[0]:taken[0] + n]
            taken[0] += n
            assert taken[0] <= SCRATCH, taken[0]
            if dt == bf16:
                v = v.bitcast(bf16)
            if len(shape) == 2:
                v = v.rearrange("p (a b) -> p a b", b=shape[1])
            if len(shape) == 3:
                v = v.rearrange("p (a b c) -> p a b c", b=shape[1], c=shape[2])
            return v

        XC = scr([NT, D])
        SQ = scr([NT, D])
        CTX = [scr([KT, D]) for _ in range(2)]
        CTXT = scr([2048])
        xns = scr([CH, D])
        xnT = scr([CH, P])
        KVT = scr([512])
        KF = scr([16, DK])
        KR = scr([16, DK])
        KPt = [scr([16, DK], bf16) for _ in range(PARTS)]
        KST = scr([16, P], bf16)
        first_top = taken[0]
        ANG = CTX[0][:, 0:8, :].rearrange("p a b -> p (a b)").rearrange("p (n h i) -> p n h i", n=NT, h=NH)
        TR = CTX[1][:, 0:8, :].rearrange("p a b -> p (a b)").rearrange("p (n h i) -> p n h i", n=NT, h=NH)
        T2 = CTXT[:, 0:1024].rearrange("p (n h i) -> p n h i", n=NT, h=NH)
        taken[0] = 2 * NT * D
        BT = [scr([CH, NH, NS]) for _ in range(2)]
        CT = [scr([CH, NH, NS]) for _ in range(2)]
        CE = [scr([NH, NS]) for _ in range(2)]
        BTT = [scr([CH * 2, P]) for _ in range(2)]
        CTZ = [scr([CH, NH, P]) for _ in range(2)]
        LM = [scr([CH, NH, P]) for _ in range(2)]
        dtx = [scr([CH, NH, HD]) for _ in range(2)]
        dtxe = [scr([NH, HD]) for _ in range(2)]
        SR = [scr([NH, P]) for _ in range(CH)]
        r1 = scr([CH * NH, PAIRS])
        r2 = scr([CH * NH, PAIRS])
        c1 = scr([CH * NH, PAIRS])
        c2 = scr([CH * NH, PAIRS])
        CET = scr([2, P])
        HZ = scr([NH, HD])
        Y = scr([CH, DI])
        YT = scr([CH * 2, P])
        junk = scr([DI])
        rms = scr([2])
        taken[0] = 2 * NT * D
        xqT = scr([B * L])
        QF = scr([512])
        QP = scr([PARTS, B * L], bf16)
        Qg = [[scr([GC], bf16) for _ in range(2)] for _ in range(2)]
        KSa = [scr([SP], bf16) for _ in range(2)]
        attention_top = taken[0]
        taken[0] = 0
        PE_ = scr([EB, NB, 512])
        KSb = [scr([SP], bf16) for _ in range(2)]
        Vc = [scr([KT, 32]) for _ in range(2)]
        NMX = scr([SPANS, NQ])
        NM = scr([NQ])
        NR = scr([NQ])
        MP = scr([PARTS, NQ], bf16)
        MT = scr([P], bf16)
        OT = scr([512])
        rdn = scr([16])
        assert taken[0] <= 2 * NT * D + B * L + 512 + PARTS * B * L // 2
        X3T = Z[:, 0:8, :].rearrange("p a b -> p (a b)")
        SG = Z[:, 8:12, :].rearrange("p a b -> p (a b)").rearrange("p (a b) -> p a b", b=512)
        Hb = XS[:, 0:10, :].rearrange("p a b -> p (a b)").rearrange("p (a b) -> p a b", b=512)
        T8 = XS[:, 10:16, :].rearrange("p a b -> p (a b)")
        LG, SH, KY, S1, S2_, PB = [T8[:, k * 128:(k + 1) * 128].rearrange("p (n e) -> p n e", e=NE) for k in range(6)]
        CP = T8[:, 768:768 + 256].bitcast(bf16).rearrange("p (n e) -> p n e", e=32)
        red = T8[:, 1024:1024 + 16]
        rcp = T8[:, 1040:1040 + 16]
        CR = T8[:, 1056:1056 + 128].rearrange("p (n e) -> p n e", e=NE)
        CTs = Z[:, 12:16, :].rearrange("p a b -> p (a b)")[0:PARTS * NE, :].bitcast(bf16)

        PS = es.enter_context(nc.psum_tensor("PS", [P, 8, 512], f32))
        UNIT, RING, ACC, AUX = 0, 4, 6, 7


        sems = {}

        def S_(name):
            if name not in sems:
                sems[name] = es.enter_context(nc.semaphore(name))
            return sems[name]

        primed = []
        for name, n in PRIMED:
            primed += [S_(f"{name}{k}") for k in range(n)] if n else [S_(name)]
        with nc.Block() as block:
            @block.sync
            def _(sp):
                for p in primed[0::4]:
                    sp.sem_inc(p, PRIME)

            @block.gpsimd
            def _(pool):
                for p in primed[1::4]:
                    pool.sem_inc(p, PRIME)

            @block.scalar
            def _(act):
                for p in primed[2::4]:
                    act.sem_inc(p, PRIME)

            @block.vector
            def _(dve):
                for p in primed[3::4]:
                    dve.sem_inc(p, PRIME)

        def settle(eng):
            eng.sem_inc(S_("settled"), 1)

        q_dram = nc.dram_tensor("q_parts", (XH, PARTS, DK, B * L), bf16, kind="Internal").ap()

        def row(v):
            return v.rearrange("(o a) -> o a", o=1).to_broadcast([P, v.shape[0]])

        def col(v):
            return v.rearrange("(a o) -> a o", o=1)

        def bank(k):
            return PS[:, k, :]

        def bankb(k):
            return PS[:, k, :].bitcast(bf16)

        with nc.Block() as block:
            x_in, w_in, c_in, w_set = S_("x_in"), S_("w_in"), S_("c_in"), S_("w_set")
            zeroed, consts_cast = S_("zeroed"), S_("consts_cast")
            ctx_in = [S_("ctx_in0"), S_("ctx_in1")]
            ln_vec, ln_act = S_("ln_vec"), S_("ln_act")
            xn_made, xn_turned, xnT_saved = S_("xn_made"), S_("xn_turned"), S_("xnT_saved")
            projected = [S_("projected0"), S_("projected1")]
            z_saved = [S_("z_saved0"), S_("z_saved1")]
            bcd_saved = [S_("bcd_saved0"), S_("bcd_saved1")]
            ctx_turned = [S_(f"ctx_turned{q}") for q in range(4)]
            ctxT_saved = [S_(f"ctxT_saved{q}") for q in range(4)]
            kv_made, kv_saved, kv_turned, v_saved = S_("kv_made"), S_("kv_saved"), S_("kv_turned"), S_("v_saved")
            k_split, k_steps, k_stacked = S_("k_split"), S_("k_steps"), S_("k_stacked")
            ks_turned = [S_("ks_turned0"), S_("ks_turned1")]
            ks_saved = [S_("ks_saved0"), S_("ks_saved1")]
            mid_vec, mid_act, cum_made = S_("mid_vec"), S_("mid_act"), S_("cum_made")
            trig_arg, sin_made, z_gated = S_("trig_arg"), S_("sin_made"), S_("z_gated")

            XN, ZX, STACK, CTXB, KV = 0, (1, 2), 4, (5, 6), 7
            BC = [bank(3)[:, 0:2 * NS + NH], bank(XN)[:, CH * P:CH * P + 2 * NS + NH]]

            @block.sync
            def _(sp):
                sp.dma_start(X[:, :, :], x.rearrange("b (c p) d -> p (b c) d", p=P)).then_inc(x_in, 16)
                sp.dma_start(CST[:, :], consts).then_inc(c_in, 16)
                sp.dma_start(Win[:, :], W_in).then_inc(w_in, 16)
                sp.wait_ge(zeroed, 1)

                def load_context(b, half):
                    main = ctx_1024[:, 0:(KT - 1) * P, :].rearrange("b (p j) d -> p b j d", p=P)
                    tail = ctx_1024[:, (KT - 1) * P:S, :].rearrange("b p d -> p b d")
                    sp.dma_start(CTX[half][:, 0:KT - 1, :].unsqueeze(1), main[:, ds(b, 1)]).then_inc(ctx_in[half], 16)
                    sp.dma_start(CTX[half][0:TAIL, KT - 1:KT, :], tail[:, ds(b, 1)]).then_inc(ctx_in[half], 16)

                load_context(0, 0)
                small = [(WkvS[:, 0:DK], Wk), (WkvS[:, DK:2 * DK], Wv)]
                small += [(bkvS[32 * j:32 * j + DK, :], col(bk)) for j in range(4)]
                small += [(bkvS[32 * j + DK:32 * j + 2 * DK, :], col(bv)) for j in range(4)]
                small += [(hb[:, 0, :], row(dt_bias)), (hb[:, 1, :], row(A_log)), (hb[:, 2, :], row(D_skip))]
                small += [(Wout[:, :, :], W_out.rearrange("(k p) d -> p k d", p=P)),
                          (nw[:, 0:1], col(norm_weight[0:P])), (nw[:, 1:2], col(norm_weight[P:2 * P])),
                          (WqS[:, :], Wq), (bqS[:, :], col(bq)), (WoS[:, :], Wo), (boS[:, :], row(bo)),
                          (RT[:, :], router)]
                for n, (to, what) in enumerate(small):
                    sp.dma_start(to, what).then_inc(w_set, 16)
                assert len(small) == N_SMALL
                load_context(1, 1)
                with sp.Fori(1, B // 2) as i:
                    for half in range(2):
                        sp.wait_ge(ctx_turned[3], 2 * i + half - 1)
                        load_context(2 * i + half, half)
                for k, (gate, up) in enumerate(((e_gate, e_up),)):
                    for to, what in ((WG, gate), (WU, up)):
                        sp.dma_start(to[:, 0:NE * ED].rearrange("p (e d) -> p e d", e=NE),
                                     what.rearrange("e h d -> h e d")).then_inc(w_set, 16)
                sp.dma_start(WG[:, NE * ED:], s_gate).then_inc(w_set, 16)
                sp.dma_start(WU[:, NE * ED:], s_up).then_inc(w_set, 16)
                sp.dma_start(WD[:, 0:HT - 1, :], e_down.rearrange("(k e) d h -> (e d) k h", e=2)).then_inc(w_set, 16)
                sp.dma_start(WD[:, HT - 1, :], s_down).then_inc(w_set, 16)
                sp.wait_ge(w_set, 16 * (N_SMALL + 6))

            @block.gpsimd
            def _(pool):
                g = Steps(pool, S_("pool_zeroes"))
                g(nc.gpsimd.memset(WkvS[:, :], 0.0))
                g(nc.gpsimd.memset(bkvS[:, :], 0.0))
                g(nc.gpsimd.memset(eps[:, :], EPS))
                for half in range(2):
                    g(nc.gpsimd.memset(CTX[half][64:P, KT - 1, :], 0.0))
                g(nc.gpsimd.memset(CTXT[:, SP:2048], 0.0))
                g(nc.gpsimd.memset(KST[:, :, :], 0.0))
                g(nc.gpsimd.memset(Vall[:, :, :, :], 0.0))
                g(nc.gpsimd.memset(KST[:, :, MROW:MROW + PARTS], 1.0))
                g(nc.gpsimd.memset(Vall[:, :, 0:KT - 1, DK:DK + 1], 1.0))
                g(nc.gpsimd.memset(Vall[0:TAIL, :, KT - 1:KT, DK:DK + 1], 1.0))
                nc.gpsimd.memset(KSall[:, :, S:SP], 0.0).then_inc(zeroed, 1)
                with pool.Fori(0, B) as b:
                    pool.wait_ge(k_split, b + 1)
                    pool.wait_ge(ks_turned[1], PRIME + b)
                    settle(pool)
                    for j in range(PARTS):
                        to = KST[:, :, 0:QK].rearrange("p t (j i d) -> p t j i d", i=PARTS, j=PARTS)[:, :, j, :, :]
                        last = nc.gpsimd.tensor_copy(to, bc(KPt[j], 2, PARTS))
                    last.then_inc(k_stacked, 1)

            @block.scalar
            def _(act):
                act.wait_ge(zeroed, 1)
                act.wait_ge(ln_vec, LN_STEPS)
                a = Steps(act, ln_act)
                a(nc.scalar.activation(st[:, 2, :], st[:, 1, :], ACT.Ln, bias=eps[:, :], scale=1.0 / D))
                a(nc.scalar.activation(st[:, 3, :], st[:, 2, :], ACT.Exp, scale=-0.5))

                def keep_stack(b):
                    act.wait_ge(ks_turned[0], PRIME + b + 1)
                    settle(act)
                    nc.scalar.copy(KSall[:, ds(b, 1), 0:8 * P], bankb(STACK).unsqueeze(1)).then_inc(ks_saved[0], 1)

                def body(b, first=False):
                    act.wait_ge(xn_turned, PRIME + b + 1)
                    act.wait_ge(projected[1], PRIME + b)
                    nc.scalar.copy(xnT[:, :, :], bank(XN)[:, 0:CH * P].rearrange("p (c t) -> p c t", c=CH)).then_inc(xnT_saved, 1)
                    for c in range(CH):
                        act.wait_ge(projected[c], PRIME + b + 1)
                        settle(act)
                        n = ds(2 * b + c, 1)
                        nc.scalar.copy(Z[:, n, :], bank(ZX[c])[:, 0:DI].unsqueeze(1))
                        nc.scalar.copy(XS[:, n, :], bank(ZX[c])[:, DI:2 * DI].unsqueeze(1)).then_inc(z_saved[c], 1)
                    if first:
                        act.wait_ge(w_set, 16 * N_SMALL)
                    else:
                        keep_stack(b - 1)
                    act.wait_ge(kv_made, PRIME + b + 1)
                    act.wait_ge(kv_turned, PRIME + b)
                    nc.scalar.activation(KVT[:, :], bank(KV), ACT.Identity, bias=bkvS[:, :]).then_inc(kv_saved, 1)

                body(0, first=True)
                with act.Fori(1, B) as b:
                    body(b)
                keep_stack(B - 1)
                m = Steps(act, mid_act)
                act.wait_ge(mid_vec, MID_E)
                m(nc.scalar.activation(tm[:, 1, :], tm[:, 0, :], ACT.Exp))
                m(nc.scalar.activation(hb[:, 1, :], hb[:, 1, :], ACT.Exp))
                act.wait_ge(mid_vec, MID_U)
                m(nc.scalar.activation(tm[:, 3, :], tm[:, 2, :], ACT.Ln))
                act.wait_ge(mid_vec, MID_CUM)
                m(nc.scalar.activation(EC[:, :, :], CUM[:, 1, :, :], ACT.Exp, scale=-1.0))
                for n, to in enumerate((SIN, COS)):
                    act.wait_ge(trig_arg, n + 1)
                    nc.scalar.activation(to[:, :, :, :], T2, ACT.Sin).then_inc(sin_made, 1)
                nc.scalar.activation(Z[:, :, :], Z[:, :, :], ACT.Silu).then_inc(z_gated, 1)

            @block.vector
            def _(dve):
                dve.wait_ge(c_in, 16)
                nc.vector.tensor_copy(identb[:, :], ident)
                nc.vector.tensor_copy(selb[:, :, :], CST[0:PARTS * NE, CST_SEL:CST_SEL + (HT - 1) * P]
                                      .rearrange("p (k r) -> p k r", k=HT - 1))
                nc.vector.tensor_scalar(bigb[:, :, :], bc(mask_gt, 1, NH), 30000.0, None, ALU.mult).then_inc(consts_cast, 1)
                dve.wait_ge(x_in, 16)
                v = Steps(dve, ln_vec)
                layer_norm_sums(v, X[:, :, :], XC, SQ, st)
                assert v.k == LN_STEPS
                dve.wait_ge(ln_act, 2)

                def make_xn(b):
                    dve.wait_ge(xn_turned, PRIME + b)
                    n = ds(2 * b, CH)
                    nc.vector.tensor_tensor(xns[:, :, :], XC[:, n, :], bc(st[:, 3, n], 2, D), ALU.mult).then_inc(xn_made, 1)

                def keep_ctxT(b, q, n):
                    dve.wait_ge(ctx_turned[q], b + 1)
                    dve.wait_ge(kv_made, PRIME + b)
                    nc.vector.tensor_copy(CTXT[:, 512 * q:512 * q + n], bank(CTXB[q % 2])[:, 0:n]).then_inc(ctxT_saved[q], 1)

                def keep_bcd(b, c):
                    dve.wait_ge(projected[c], PRIME + b + 1)
                    settle(dve)
                    nc.vector.tensor_copy(BCD[:, ds(2 * b + c, 1), :], BC[c].unsqueeze(1))\
                        .then_inc(bcd_saved[c], 1)

                def keep_stack(b):
                    dve.wait_ge(ks_turned[1], PRIME + b + 1)
                    settle(dve)
                    nc.vector.tensor_copy(KSall[:, ds(b, 1), 8 * P:S], bankb(STACK)[:, 0:S - 8 * P].unsqueeze(1))\
                        .then_inc(ks_saved[1], 1)

                def body(b, first=False, last=False):
                    keep_ctxT(b, 0, 512)
                    keep_ctxT(b, 1, 512)
                    keep_bcd(b, 0)
                    keep_ctxT(b, 2, 512)
                    keep_ctxT(b, 3, P)
                    keep_bcd(b, 1)
                    if not first:
                        keep_stack(b - 1)
                    if not last:
                        make_xn(b + 1)
                    k = Steps(dve, k_steps, b, K_STEPS)
                    dve.wait_ge(kv_turned, PRIME + b + 1)
                    if first:
                        dve.wait_ge(zeroed, 1)
                    kv = bank(KV).rearrange("p (s j e) -> p j s e", s=4, j=4)
                    settle(dve)
                    k(nc.vector.tensor_copy(KF.rearrange("p (j s) d -> p j s d", j=4), kv[:, :, :, 0:DK]))
                    settle(dve)
                    for j in range(3):
                        nc.vector.tensor_copy(Vall[:, ds(b, 1), 4 * j:4 * j + 4, 0:DK], kv[:, j:j + 1, :, DK:2 * DK])
                    nc.vector.tensor_copy(Vall[0:TAIL, ds(b, 1), KT - 1:KT, 0:DK], kv[0:TAIL, 3:4, 0:1, DK:2 * DK])\
                        .then_inc(v_saved, 1)
                    dve.wait_ge(k_stacked, PRIME + b)
                    k(nc.vector.tensor_copy(KPt[0], KF))
                    k(nc.vector.tensor_tensor(KR, KF, KPt[0], ALU.subtract))
                    k(nc.vector.tensor_copy(KPt[1], KR))
                    k.end()
                    nc.vector.tensor_tensor(KPt[2], KR, KPt[1], ALU.subtract).then_inc(k_split, 1)
                    dve.wait_ge(k_split, b + 1)

                make_xn(0)
                body(0, first=True)
                with dve.Fori(1, B - 1) as b:
                    body(b)
                body(B - 1, last=True)
                keep_stack(B - 1)
                m = Steps(dve, mid_vec)
                raw = DT[:, 0, :, :]
                flat = raw.rearrange("p n h -> p (n h)")
                dve.wait_ge(bcd_saved[0], PRIME + B)
                dve.wait_ge(bcd_saved[1], PRIME + B)
                m(nc.vector.tensor_tensor(raw, BCD[:, :, 2 * NS:], bc(hb[:, 0, :], 1, NT), ALU.add))
                m(nc.vector.scalar_tensor_tensor(tm[:, 0, :], flat, -1.0, flat, ALU.mult, ALU.min))
                assert m.k == MID_E
                dve.wait_ge(mid_act, 2)
                m(nc.vector.tensor_scalar(tm[:, 2, :], tm[:, 1, :], 1.0, None, ALU.add))
                assert m.k == MID_U
                m(nc.vector.tensor_scalar(tm[:, 4, :], tm[:, 2, :], -1.0, None, ALU.add))
                m(nc.vector.tensor_tensor(tm[:, 4, :], tm[:, 1, :], tm[:, 4, :], ALU.subtract))
                m(nc.vector.reciprocal(tm[:, 5, :], tm[:, 2, :]))
                m(nc.vector.tensor_tensor(tm[:, 4, :], tm[:, 4, :], tm[:, 5, :], ALU.mult))
                dve.wait_ge(mid_act, 3)
                m(nc.vector.tensor_tensor(tm[:, 3, :], tm[:, 3, :], tm[:, 4, :], ALU.add))
                m(nc.vector.scalar_tensor_tensor(flat, flat, 0.0, tm[:, 3, :], ALU.max, ALU.add))
                m(nc.vector.tensor_tensor(DT[:, 1, :, :], raw, bc(hb[:, 1, :], 1, NT), ALU.mult))
                m(nc.vector.tensor_scalar(DT[:, 1, :, :], DT[:, 1, :, :], LOGCAP, None, ALU.min))
                assert m.k == MID_DT
                dve.wait_ge(cum_made, 1)
                cum = bank(0)[:, 0:P].rearrange("p (c k b h) -> p c k b h", c=2, k=2, b=B)
                CV = CUM[:, :, :, :].rearrange("p k (b c) h -> p k b c h", c=2)
                m(nc.vector.tensor_scalar(CV[:, 0, :, 0, :], cum[:, 0, 0], -1.0, None, ALU.mult))
                m(nc.vector.tensor_copy(CV[:, 1, :, 0, :], cum[:, 0, 1]))
                m(nc.vector.tensor_copy(CV[:, 0, :, 1, :], cum[:, 1, 0]))
                m(nc.vector.tensor_copy(CV[:, 1, :, 1, :], cum[:, 1, 1]))
                assert m.k == MID_CUM
                shape = [P, NT, NH, PAIRS]
                fr = freq.unsqueeze(1).unsqueeze(1).to_broadcast(shape)
                m(nc.vector.tensor_tensor(ANG, bc(CUM[:, 0, :, :], 3, PAIRS), fr, ALU.mult))
                for n, (turn, shift) in enumerate(((0.0, 0.0), (0.25, np.pi / 2))):
                    if n:
                        dve.wait_ge(sin_made, 1)
                    m(nc.vector.tensor_scalar(TR, ANG, float(0.5 / np.pi), turn, ALU.mult, ALU.add))
                    m(nc.vector.tensor_scalar(TR, TR, ROUND, ROUND, ALU.add, ALU.subtract))
                    m(nc.vector.scalar_tensor_tensor(T2, TR, -TWO_PI_HI, ANG, ALU.mult, ALU.add))
                    m(nc.vector.scalar_tensor_tensor(T2, TR, -TWO_PI_LO, T2, ALU.mult, ALU.add))
                    m(nc.vector.tensor_scalar(T2, T2, float(shift), PI, ALU.add, ALU.min))
                    nc.vector.tensor_scalar(T2, T2, -PI, None, ALU.max).then_inc(trig_arg, 1)
                    dve.wait_ge(trig_arg, n + 1)
                for k in range(2):
                    m(nc.vector.tensor_scalar(Wout[:, k, :], Wout[:, k, :], nw[:, k:k + 1], None, ALU.mult))

            @block.tensor
            def _(pe):
                pe.wait_ge(c_in, 16)
                pe.wait_ge(w_in, 16)
                pe.wait_ge(consts_cast, 1)
                pe.wait_ge(zeroed, 1)

                def turn_ctx(b, half, q, n):
                    if q < 2:
                        pe.wait_ge(ctxT_saved[q + 2], PRIME + b)
                    else:
                        pe.wait_ge(ctxT_saved[q - 2], PRIME + b + 1)
                    for t in range(n):
                        last = nc.tensor.transpose(bank(CTXB[q % 2])[:, t * P:(t + 1) * P], CTX[half][:, 4 * q + t, :], ident)
                    last.then_inc(ctx_turned[q], 1)

                def project(b, c):
                    pe.wait_ge(xnT_saved, PRIME + b + 1)
                    pe.wait_ge(z_saved[c], PRIME + b)
                    pe.wait_ge(bcd_saved[c], PRIME + b)
                    nc.tensor.matmul(bank(ZX[c]), xnT[:, c, :], Win[:, 0:2 * DI], start=True, stop=True)
                    nc.tensor.matmul(BC[c], xnT[:, c, :], Win[:, 2 * DI:], start=True, stop=True)\
                        .then_inc(projected[c], 1)

                def turn_stack(b, part):
                    if part == 0:
                        pe.wait_ge(k_stacked, PRIME + b + 1)
                        pe.wait_ge(ks_saved[1], PRIME + b)
                    else:
                        pe.wait_ge(ks_saved[0], PRIME + b + 1)
                    for t in (range(8), range(8, KT))[part]:
                        last = nc.tensor.transpose(bankb(STACK)[:, (t % 8) * P:(t % 8 + 1) * P], KST[:, t, :], identb[:, :])
                    last.then_inc(ks_turned[part], 1)

                def body(b, half, turn, first=False):
                    pe.wait_ge(xn_made, b + 1)
                    pe.wait_ge(xnT_saved, PRIME + b)
                    pe.wait_ge(bcd_saved[1], PRIME + b)
                    for c in range(CH):
                        last = nc.tensor.transpose(bank(XN)[:, c * P:(c + 1) * P], xns[:, c, :], ident)
                    last.then_inc(xn_turned, 1)
                    pe.wait_ge(ctx_in[half], 32 * (turn + 1))
                    turn_ctx(b, half, 0, 4)
                    turn_ctx(b, half, 1, 4)
                    project(b, 0)
                    turn_ctx(b, half, 2, 4)
                    turn_ctx(b, half, 3, 1)
                    project(b, 1)
                    if not first:
                        turn_stack(b - 1, 0)
                    if first:
                        pe.wait_ge(w_set, 16 * N_SMALL)
                    for q in range(4):
                        pe.wait_ge(ctxT_saved[q], PRIME + b + 1)
                    pe.wait_ge(v_saved, PRIME + b)
                    for j in range(4):
                        last = nc.tensor.matmul(PS[32 * j:32 * j + 32, KV, :], WkvS[:, :], CTXT[:, 512 * j:512 * j + 512],
                                                start=True, stop=True)
                    last.then_inc(kv_made, 1)
                    if not first:
                        turn_stack(b - 1, 1)
                    pe.wait_ge(kv_saved, b + 1)
                    for t in range(4):
                        last = nc.tensor.transpose(bank(KV)[:, t * P:(t + 1) * P], KVT[:, t * P:(t + 1) * P], ident)
                    last.then_inc(kv_turned, 1)

                body(0, 0, 0, first=True)
                with pe.Fori(0, B // 2 - 1) as i:
                    for k in range(2):
                        body(2 * i + 1 + k, 1 - k, i + k)
                body(B - 1, 1, B // 2 - 1)
                for part in range(2):
                    turn_stack(B - 1, part)
                pe.wait_ge(mid_vec, MID_DT)
                for c, mask in enumerate((mask_gt, mask_le)):
                    rhs = DT[:, :, :, :].rearrange("p k (b c) h -> p k b c h", c=2)[:, :, :, c, :]
                    last = nc.tensor.matmul(bank(0)[:, 64 * c:64 * c + 64], mask, rhs, start=True, stop=True)
                last.then_inc(cum_made, 1)

        with nc.Block() as block:
            mixer_zeroed = S_("mixer_zeroed")
            b_turned_in, b_plain, c_ready, dtx_made = S_("b_rotated"), S_("b_plain"), S_("c_ready"), S_("dtx_made")
            pool_steps, mix_steps, square_steps = S_("pool_steps"), S_("mix_steps"), S_("square_steps")
            seg_made = [S_("seg_made0"), S_("seg_made1")]
            btt_made, btt_saved, ctt_made, ctt_saved = S_("btt_made"), S_("btt_saved"), S_("ctt_made"), S_("ctt_saved")
            seg_summed = [S_("seg_summed0"), S_("seg_summed1")]
            decays_made = [S_("decays_made0"), S_("decays_made1")]
            products_made = [S_("products_made0"), S_("products_made1")]
            mixed = [S_("mixed0"), S_("mixed1")]
            state_made, state_saved = S_("state_made"), S_("state_saved")
            y_made, y_read, y_gated, squared = S_("y_made"), S_("y_read"), S_("y_gated"), S_("squared")
            yt_made, yt_saved, mix_out, raw_saved = S_("yt_made"), S_("yt_saved"), S_("mix_out"), S_("raw_saved")
            B_TURN, C_TURN, SEG, PRODUCTS, STATE, OUTPUT = 0, 1, 2, 4, 6, 7

            def rotate(eng, step, src, to, t1, t2, n, sem=None):
                sh = [P, CH, NH, PAIRS]
                pair = src[:, :, 0:2 * PAIRS].rearrange("p n (i two) -> p n two i", two=2)
                one, two = (pair[:, :, k, :].unsqueeze(2).to_broadcast(sh) for k in range(2))
                a = t1.rearrange("p (n h) i -> p n h i", n=CH)
                c = t2.rearrange("p (n h) i -> p n h i", n=CH)
                dst = to[:, :, :, 0:2 * PAIRS].rearrange("p n h (i two) -> p n h i two", two=2)
                cos, sin = COS[:, n, :, :], SIN[:, n, :, :]
                step(eng.tensor_tensor(a, cos, one, ALU.mult))
                step(eng.tensor_tensor(c, sin, two, ALU.mult))
                step(eng.tensor_tensor(dst[:, :, :, :, 0], a, c, ALU.add))
                step(eng.tensor_tensor(a, cos, two, ALU.mult))
                step(eng.tensor_tensor(c, sin, one, ALU.mult))
                final = eng.tensor_tensor(dst[:, :, :, :, 1], a, c, ALU.subtract)
                if sem is None:
                    step(final)
                else:
                    final.then_inc(sem, 1)

            @block.gpsimd
            def _(pool):
                g = Steps(pool, S_("mixer_zeroes"))
                for what in (CTZ[0], CTZ[1]):
                    g(nc.gpsimd.memset(what, 0.0))
                nc.gpsimd.memset(HZ, 0.0).then_inc(mixer_zeroed, 1)
                pool.wait_ge(mixer_zeroed, 1)

                def mixer(b, h):
                    p = Steps(pool, pool_steps, b, POOL_STEPS, settle)
                    n = ds(2 * b, CH)
                    Bp, Cp = BCD[:, n, PAIRS * 2:NS], BCD[:, n, NS + PAIRS * 2:2 * NS]
                    pool.wait_ge(state_made, PRIME + b - 1)
                    pool.wait_ge(btt_made, PRIME + b - 1)
                    settle(pool)
                    nc.gpsimd.tensor_copy(BT[h][:, :, :, PAIRS * 2:], bc(Bp, 2, NH)).then_inc(b_plain, 1)
                    pool.wait_ge(ctt_made, PRIME + b - 1)
                    settle(pool)
                    p(nc.gpsimd.tensor_copy(CT[h][:, :, :, PAIRS * 2:], bc(Cp, 2, NH)))
                    rotate(pool, p, BCD[:, n, NS:2 * NS], CT[h], c1, c2, n)
                    xs4 = XS[:, n, :].rearrange("p n (h e) -> p n h e", h=NH)
                    nc.gpsimd.tensor_tensor(CE[h], CT[h][:, 1, :, :], bc(EC[:, ds(2 * b + 1, 1), :].rearrange("p n h -> p (n h)"), 2, NS),
                                            ALU.mult).then_inc(c_ready, 1)
                    pool.wait_ge(y_made, PRIME + b - 1)
                    settle(pool)
                    p(nc.gpsimd.tensor_tensor(dtx[h], xs4, bc(DT[:, 0, n, :], 3, HD), ALU.mult))
                    nc.gpsimd.tensor_tensor(dtxe[h], dtx[h][:, 0], bc(EC[:, ds(2 * b, 1), :].rearrange("p n h -> p (n h)"), 2, HD),
                                            ALU.mult).then_inc(dtx_made, 1)
                    p.end()

                with pool.Fori(0, B // 2) as i:
                    for h in range(2):
                        mixer(2 * i + h, h)

            @block.scalar
            def _(act):
                def save_btt(b, h):
                    act.wait_ge(btt_made, PRIME + b + 1)
                    act.wait_ge(products_made[1], PRIME + b - 1)
                    nc.scalar.copy(BTT[h], bank(B_TURN).rearrange("p (a t) -> p a t", t=P)).then_inc(btt_saved, 1)

                def save_ctt(b, h):
                    act.wait_ge(ctt_made, PRIME + b + 1)
                    act.wait_ge(products_made[1], PRIME + b - 1)
                    v = bank(C_TURN).rearrange("p (c r t) -> p c r t", c=CH, r=2)
                    z = CTZ[h].rearrange("p c (r two) t -> p c r two t", two=2)
                    nc.scalar.copy(z[0:64, :, :, 0, :], v[0:64])
                    nc.scalar.copy(z[64:P, :, :, 1, :], v[64:P]).then_inc(ctt_saved, 1)

                def make_decays(b, h, c):
                    act.wait_ge(seg_summed[c], PRIME + b + 1)
                    act.wait_ge(y_made, PRIME + b - 1)
                    nc.scalar.activation(LM[h][:, c], bank(SEG + c).rearrange("p (h t) -> p h t", h=NH), ACT.Exp, scale=-1.0)\
                        .then_inc(decays_made[c], 1)

                def save_state(b):
                    act.wait_ge(state_made, PRIME + b + 1)
                    act.wait_ge(y_made, PRIME + b)
                    z = HZ.rearrange("p (r two) e -> p r two e", two=2)
                    v = bank(STATE)[:, 0:2 * HD].rearrange("p (r e) -> p r e", r=2)
                    nc.scalar.copy(z[0:64, :, 0, :], v[0:64])
                    nc.scalar.copy(z[64:P, :, 1, :], v[64:P])
                    nc.scalar.copy(CET, bank(STATE)[:, 2 * HD:2 * HD + 2 * P].rearrange("p (r t) -> p r t", r=2))\
                        .then_inc(state_saved, 1)

                def square_y(b):
                    r = Steps(act, square_steps, b, SQUARE_STEPS)
                    act.wait_ge(raw_saved, PRIME + b)
                    act.wait_ge(y_gated, PRIME + b + 1)
                    r(nc.scalar.activation(junk, Y[:, 0, :], ACT.Square, accum_out=rms[:, 0:1]))
                    nc.scalar.activation(junk, Y[:, 1, :], ACT.Square, accum_out=rms[:, 1:2]).then_inc(squared, 1)
                    act.wait_ge(squared, PRIME + b + 1)
                    r.end()

                def save_yt(b):
                    act.wait_ge(yt_made, PRIME + b + 1)
                    act.wait_ge(mix_out, PRIME + b)
                    nc.scalar.copy(YT, bank(B_TURN).rearrange("p (a t) -> p a t", t=P)).then_inc(yt_saved, 1)

                def ahead(b, h):
                    save_btt(b, h)
                    save_ctt(b, h)

                def body(b, h, first=False, last=False):
                    if not first:
                        save_yt(b - 1)
                    save_state(b)
                    if not last:
                        ahead(b + 1, 1 - h)
                        for c in range(CH):
                            make_decays(b + 1, 1 - h, c)
                    square_y(b)

                act.wait_ge(mixer_zeroed, 1)
                ahead(0, 0)
                for c in range(CH):
                    make_decays(0, 0, c)
                body(0, 0, first=True)
                with act.Fori(0, B // 2 - 1) as i:
                    for k in range(2):
                        body(2 * i + 1 + k, 1 - k)
                body(B - 1, 1, last=True)
                save_yt(B - 1)

            @block.vector
            def _(dve):
                def rotate_b(b, h):
                    m = Steps(dve, mix_steps, b, MIX_STEPS)
                    dve.wait_ge(btt_made, PRIME + b - 1)
                    dve.wait_ge(state_made, PRIME + b - 1)
                    settle(dve)
                    n = ds(2 * b, CH)
                    rotate(dve, m, BCD[:, n, 0:NS], BT[h], r1, r2, n, b_turned_in)
                    m.end()
                    dve.wait_ge(b_turned_in, PRIME + b + 1)

                def make_seg(b, c):
                    dve.wait_ge(seg_summed[c], PRIME + b)
                    settle(dve)
                    adt = DT[:, 1, ds(2 * b + c, 1), :].rearrange("p n h -> p (n h)")
                    nc.vector.tensor_tensor(SR[c], bc(mask_le, 1, NH), bc(adt, 2, P), ALU.mult).then_inc(seg_made[c], 1)

                def mix(b, h, c):
                    dve.wait_ge(decays_made[c], PRIME + b + 1)
                    dve.wait_ge(products_made[c], PRIME + b + 1)
                    nc.vector.tensor_tensor(LM[h][:, c], LM[h][:, c], bank(PRODUCTS + c).rearrange("p (h t) -> p h t", h=NH), ALU.mult)\
                        .then_inc(mixed[c], 1)

                def gate_y(b):
                    n = ds(2 * b, CH)
                    dve.wait_ge(yt_made, PRIME + b)
                    settle(dve)
                    m = Steps(dve, S_("skip_steps"), b, 1)
                    y4 = Y.rearrange("p n (h e) -> p n h e", h=NH)
                    dsk = hb[:, 2, :].unsqueeze(1).unsqueeze(3).to_broadcast([P, CH, NH, HD])
                    m(nc.vector.tensor_tensor(y4, XS[:, n, :].rearrange("p n (h e) -> p n h e", h=NH), dsk, ALU.mult))
                    m.end()
                    dve.wait_ge(y_made, PRIME + b + 1)
                    nc.vector.tensor_tensor(Y, Y, bank(OUTPUT).rearrange("p (c e) -> p c e", c=CH), ALU.add).then_inc(y_read, 1)
                    dve.wait_ge(y_read, PRIME + b + 1)
                    nc.vector.tensor_tensor(Y, Y, Z[:, n, :], ALU.mult).then_inc(y_gated, 1)

                def keep_raw(b):
                    n = ds(2 * b, CH)
                    dve.wait_ge(mix_out, PRIME + b + 1)
                    dve.wait_ge(squared, PRIME + b + 1)
                    settle(dve)
                    nc.vector.tensor_copy(rs[:, 0, n], rms)
                    nc.vector.tensor_copy(XC[:, n, :], bank(SEG)[:, 0:L].rearrange("p (c d) -> p c d", c=CH)).then_inc(raw_saved, 1)

                def body(b, h, first=False, last=False):
                    if not last:
                        rotate_b(b + 1, 1 - h)
                    for c in range(CH):
                        mix(b, h, c)
                    if not first:
                        keep_raw(b - 1)
                    if not last:
                        for c in range(CH):
                            make_seg(b + 1, c)
                    gate_y(b)

                dve.wait_ge(mixer_zeroed, 1)
                rotate_b(0, 0)
                for c in range(CH):
                    make_seg(0, c)
                body(0, 0, first=True)
                with dve.Fori(0, B // 2 - 1) as i:
                    for k in range(2):
                        body(2 * i + 1 + k, 1 - k)
                body(B - 1, 1, last=True)
                keep_raw(B - 1)

            @block.tensor
            def _(pe):
                def turned_by(b):
                    return B if isinstance(b, int) and b == B - 1 else b + 2

                def turn_b(b, h):
                    pe.wait_ge(btt_saved, PRIME + b)
                    pe.wait_ge(yt_saved, PRIME + b - 1)
                    pe.wait_ge(b_turned_in, PRIME + b + 1)
                    pe.wait_ge(b_plain, PRIME + b + 1)
                    for c in range(CH):
                        for r in range(2):
                            at = (2 * c + r) * P
                            last = nc.tensor.transpose(bank(B_TURN)[:, at:at + P], BT[h][:, c, 2 * r:2 * r + 2, :].rearrange("p h n -> p (h n)"), ident)
                    last.then_inc(btt_made, 1)

                def turn_c(b, h):
                    pe.wait_ge(ctt_saved, PRIME + b)
                    pe.wait_ge(c_ready, PRIME + b + 1)
                    for c in range(CH):
                        for r in range(2):
                            at = (2 * c + r) * P
                            last = nc.tensor.transpose(bank(C_TURN)[:, at:at + P], CT[h][:, c, 2 * r:2 * r + 2, :].rearrange("p h n -> p (h n)"), ident)
                    last.then_inc(ctt_made, 1)

                def sum_seg(b, c):
                    pe.wait_ge(decays_made[c], PRIME + b)
                    if c == 0:
                        pe.wait_ge(raw_saved, PRIME + b - 1)
                    pe.wait_ge(seg_made[c], PRIME + b + 1)
                    nc.tensor.matmul(bank(SEG + c), mask_gt, SR[c].rearrange("p h t -> p (h t)"), start=True, stop=False)
                    nc.tensor.matmul(bank(SEG + c), identb[:, :], bigb[:, :, :].rearrange("p h t -> p (h t)"), start=False, stop=True)\
                        .then_inc(seg_summed[c], 1)

                def products(b, h, c):
                    pe.wait_ge(mixed[c], PRIME + b)
                    if c == 0:
                        pe.wait_ge(btt_saved, PRIME + b + 1)
                        pe.wait_ge(ctt_saved, PRIME + b + 1)
                    for k in range(NH):
                        last = nc.tensor.matmul(bank(PRODUCTS + c)[:, k * P:(k + 1) * P], BTT[h][:, 2 * c + k // 2, :], CTZ[h][:, c, k, :],
                                                start=True, stop=True)
                    last.then_inc(products_made[c], 1)

                def state(b, h):
                    pe.wait_ge(state_saved, PRIME + b)
                    pe.wait_ge(dtx_made, PRIME + b + 1)
                    for k in range(NH):
                        r = 64 * (k % 2)
                        nc.tensor.matmul(PS[r:r + 64, STATE, (k // 2) * HD:(k // 2 + 1) * HD], BT[h][:, 0, k, :], dtxe[h][:, k, :],
                                         start=True, stop=True)
                    for r in range(2):
                        at = 2 * HD + r * P
                        last = nc.tensor.transpose(bank(STATE)[:, at:at + P], CE[h][:, 2 * r:2 * r + 2, :].rearrange("p h n -> p (h n)"), ident)
                    last.then_inc(state_made, 1)

                def outputs(b, h):
                    pe.wait_ge(y_read, PRIME + b)
                    pe.wait_ge(state_saved, PRIME + b + 1)
                    for c in range(CH):
                        pe.wait_ge(mixed[c], PRIME + b + 1)
                        for k in range(NH):
                            to = bank(OUTPUT)[:, c * DI + k * HD:c * DI + (k + 1) * HD]
                            last = nc.tensor.matmul(to, LM[h][:, c, k, :], dtx[h][:, c, k, :], start=True, stop=c == 0)
                            if c:
                                last = nc.tensor.matmul(to, CET[:, k // 2, :], HZ[:, k, :], start=False, stop=True)
                    last.then_inc(y_made, 1)

                def turn_y(b):
                    pe.wait_ge(btt_saved, PRIME + turned_by(b))
                    pe.wait_ge(y_gated, PRIME + b + 1)
                    for c in range(CH):
                        for r in range(2):
                            at = (2 * c + r) * P
                            last = nc.tensor.transpose(bank(B_TURN)[:, at:at + P], Y[:, c, r * P:(r + 1) * P], ident)
                    last.then_inc(yt_made, 1)

                def project_y(b):
                    pe.wait_ge(decays_made[0], PRIME + turned_by(b))
                    pe.wait_ge(yt_saved, PRIME + b + 1)
                    for c in range(CH):
                        for r in range(2):
                            last = nc.tensor.matmul(bank(SEG)[:, c * D:(c + 1) * D], YT[:, 2 * c + r, :], Wout[:, r, :],
                                                    start=r == 0, stop=r == 1)
                    last.then_inc(mix_out, 1)

                def body(b, h, first=False, last=False):
                    for c in range(CH):
                        products(b, h, c)
                    if not first:
                        turn_y(b - 1)
                    state(b, h)
                    if not first:
                        project_y(b - 1)
                    if not last:
                        turn_b(b + 1, 1 - h)
                        turn_c(b + 1, 1 - h)
                    outputs(b, h)
                    if not last:
                        for c in range(CH):
                            sum_seg(b + 1, c)

                pe.wait_ge(mixer_zeroed, 1)
                turn_b(0, 0)
                turn_c(0, 0)
                for c in range(CH):
                    sum_seg(0, c)
                body(0, 0, first=True)
                with pe.Fori(0, B // 2 - 1) as i:
                    for k in range(2):
                        body(2 * i + 1 + k, 1 - k)
                body(B - 1, 1, last=True)
                turn_y(B - 1)
                project_y(B - 1)

        TB = 512
        with nc.Block() as block:
            scale_act, scaled, res_vec, res_act = S_("scale_act"), S_("scaled"), S_("res_vec"), S_("res_act")
            normed, normed_turned, normed_saved, q_made, q_parts_made, q_in_dram, q_steps = (
                S_(n) for n in ("normed", "normed_turned", "normed_saved", "q_made", "q_parts_made", "q_in_dram", "q_steps"))
            blocks = range(NT * P // TB)

            @block.sync
            def _(sp):
                for r in blocks:
                    sp.wait_ge(q_parts_made, r + 1)
                    for i in range(PARTS):
                        sp.dma_start(q_dram[:, i, :, r * TB:(r + 1) * TB], QP[:, i, r * TB:(r + 1) * TB]).then_inc(q_in_dram, 16)
                sp.wait_ge(q_in_dram, 16 * PARTS * len(blocks))

            @block.gpsimd
            def _(pool):
                g = Steps(pool, S_("queries_zeroes"))
                for par in range(2):
                    g(nc.gpsimd.memset(KSa[par], 0.0))
                    for what in Qg[par]:
                        g(nc.gpsimd.memset(what, 0.0))
                g(nc.gpsimd.tensor_copy(KSa[0][0:MROW, :], KSall[0:MROW, 0, :]))

            @block.scalar
            def _(act):
                a = Steps(act, scale_act)
                a(nc.scalar.activation(rs[:, 1, :], rs[:, 0, :], ACT.Ln, bias=eps[:, :], scale=1.0 / DI))
                a(nc.scalar.activation(rs[:, 2, :], rs[:, 1, :], ACT.Exp, scale=-0.5))
                act.wait_ge(res_vec, LN_STEPS)
                a = Steps(act, res_act)
                a(nc.scalar.activation(st[:, 2, :], st[:, 1, :], ACT.Ln, bias=eps[:, :], scale=1.0 / D))
                a(nc.scalar.activation(st[:, 3, :], st[:, 2, :], ACT.Exp, scale=-0.5))
                for r in blocks:
                    act.wait_ge(normed_turned, r + 1)
                    nc.scalar.copy(xqT[:, r * TB:(r + 1) * TB], bank(r)).then_inc(normed_saved, 1)

            @block.vector
            def _(dve):
                dve.wait_ge(scale_act, 2)
                s = Steps(dve, scaled)
                s(nc.vector.tensor_tensor(XC, XC, bc(rs[:, 2, :], 2, D), ALU.mult))
                s(nc.vector.tensor_tensor(X[:, :, :], X[:, :, :], XC, ALU.add))
                layer_norm_sums(Steps(dve, res_vec), X[:, :, :], XC, SQ, st)
                dve.wait_ge(res_act, 2)
                for r in blocks:
                    n = slice(4 * r, 4 * r + 4)
                    nc.vector.tensor_tensor(XC[:, n, :], XC[:, n, :], bc(st[:, 3, n], 2, D), ALU.mult).then_inc(normed, 1)
                m = Steps(dve, q_steps)
                for r in blocks:
                    tok = slice(r * TB, (r + 1) * TB)
                    dve.wait_ge(q_made, r + 1)
                    m(nc.vector.tensor_scalar(QF, bank(4 + r), bqS[:, :], None, ALU.add))
                    m(nc.vector.tensor_copy(QP[:, 0, tok], QF))
                    m(nc.vector.tensor_tensor(QF, QF, QP[:, 0, tok], ALU.subtract))
                    m(nc.vector.tensor_copy(QP[:, 1, tok], QF))
                    nc.vector.tensor_tensor(QP[:, 2, tok], QF, QP[:, 1, tok], ALU.subtract).then_inc(q_parts_made, 1)
                    dve.wait_ge(q_parts_made, r + 1)

            @block.tensor
            def _(pe):
                for r in blocks:
                    pe.wait_ge(normed, r + 1)
                    for t in range(TB // P):
                        last = nc.tensor.transpose(bank(r)[:, t * P:(t + 1) * P], XC[:, 4 * r + t, :], ident)
                    last.then_inc(normed_turned, 1)
                for r in blocks:
                    pe.wait_ge(normed_saved, r + 1)
                    nc.tensor.matmul(bank(4 + r), WqS[:, :], xqT[:, r * TB:(r + 1) * TB], start=True, stop=True).then_inc(q_made, 1)

        with nc.Block() as block:
            q_stacked = [[S_(f"q_stacked{2 * par + g}") for g in range(2)] for par in range(2)]
            keys_max, keys_exp, values_ready = S_("keys_max"), S_("keys_exp"), S_("values_ready")
            unit_made = [S_(f"unit_made{k}") for k in range(SPANS)]
            unit_taken = [S_(f"unit_taken{k}") for k in range(SPANS)]
            max_steps, max_split, max_turned, max_saved, max_stacked = (
                S_(n) for n in ("max_steps", "max_split", "max_turned", "max_saved", "max_stacked"))
            scored = [S_("scored0"), S_("scored1")]
            powered = [S_("powered0"), S_("powered1")]
            summed = [S_("summed0"), S_("summed1")]
            sums_saved, sums_turned, out_steps, heads_out = (
                S_(n) for n in ("sums_saved", "sums_turned", "out_steps", "heads_out"))

            def score_fill(b, g, kt, j):
                return ((2 * b + g) * KT + kt) * 2 + j // 2

            def sum_count(b, g, kt):
                return KT * b + (g * KT + kt) // 2

            def parity(g, kt):
                return (g * KT + kt) % 2

            def units(b, g, kt, last):
                if kt >= AHEAD:
                    target, at = (b + 1, g), sum(UNITS_AT[AHEAD:kt])
                else:
                    target, at = following(b, g), sum(UNITS_AT[AHEAD:]) + sum(UNITS_AT[:kt])
                none = last and (kt >= AHEAD or g)
                return target, range(at, at + UNITS_AT[kt] * (not none))

            def following(b, g):
                return (b, 1) if g == 0 else (b + 1, 0)

            first_units = range(sum(UNITS_AT[AHEAD:]))

            @block.sync
            def _(sp):
                def stack_queries(b, g, par, b_before=None):
                    if b_before is not None:
                        sp.wait_ge(scored[1], PRIME + score_fill(b_before, g, KT, 1))
                    src = q_dram[g * GH:(g + 1) * GH, :, :, ds(L * b, L)].rearrange("h i d t -> (i d) h t")
                    for j in range(PARTS):
                        r = j * PARTS * DK
                        sp.dma_start(Qg[par][g][r:r + PARTS * DK, :].rearrange("p (h t) -> p h t", h=GH), src)\
                            .then_inc(q_stacked[par][g], 16)

                def stack_maxima(b, g, par):
                    sp.wait_ge(max_saved, PRIME + 2 * b + g + 1)
                    sp.dma_start(Qg[par][g][MROW:MROW + PARTS, :].rearrange("i (q t) -> i q t", q=NQ), MT[0:PARTS * NQ, :])\
                        .then_inc(max_stacked, 16)

                def body(b, par, last=False, queries=True):
                    stack_maxima(b, 1, par)
                    if queries:
                        stack_queries(b + 2, 0, par, b)
                    if not last:
                        stack_maxima(b + 1, 0, 1 - par)
                    if queries:
                        stack_queries(b + 2, 1, par, b)

                for par in range(2):
                    for g in range(2):
                        stack_queries(par, g, par)
                stack_maxima(0, 0, 0)
                with sp.Fori(0, B // 2 - 1) as i:
                    for par in range(2):
                        body(2 * i + par, par)
                body(B - 2, 0, queries=False)
                body(B - 1, 1, last=True, queries=False)
                sp.wait_ge(max_stacked, PRIME + 16 * 2 * B)

            @block.scalar
            def _(act):
                def save_maxima(b, g):
                    act.wait_ge(max_turned, PRIME + 2 * b + g + 1)
                    act.wait_ge(max_stacked, PRIME + 16 * (2 * b + g))
                    nc.scalar.copy(MT[0:PARTS * NQ, :], bankb(AUX)[0:PARTS * NQ, 0:P]).then_inc(max_saved, 1)

                def save_sums(b, g):
                    act.wait_ge(summed[parity(g, KT - 1)], PRIME + sum_count(b, g, KT - 1) + 1)
                    act.wait_ge(sums_turned, PRIME + 2 * b + g)
                    nc.scalar.copy(OT, bank(ACC)).then_inc(sums_saved, 1)

                def exponentials(b, g, kt, js):
                    for j in js:
                        act.wait_ge(scored[j % 2], PRIME + score_fill(b, g, kt, j) + 1)
                        if j == 0:
                            act.wait_ge(summed[parity(g, kt)], PRIME + sum_count(b, g, kt))
                        nc.scalar.activation(PE_[:, parity(g, kt), j, :], bank(RING + j % 2), ACT.Exp).then_inc(powered[j % 2], 1)

                def body(b, first=False, last=False):
                    for g in range(2):
                        for kt in range(KT):
                            exponentials(b, g, kt, (0, 1))
                            exponentials(b, g, kt, (2,))
                            if kt == 0 and (g or not first):
                                save_sums(*((b, 0) if g else (b - 1, 1)))
                            exponentials(b, g, kt, (3,))
                            if kt == AHEAD + 1 and not (last and g):
                                save_maxima(*following(b, g))

                save_maxima(0, 0)
                body(0, first=True)
                with act.Fori(1, B - 1) as b:
                    body(b)
                body(B - 1, last=True)
                save_sums(B - 1, 1)

            @block.vector
            def _(dve):
                def take_max(b, g, u):
                    qt, k = u // SPANS, u % SPANS
                    dve.wait_ge(unit_made[k], PRIME + (2 * b + g) * NQ + qt + 1)
                    nc.vector.tensor_reduce(NMX[:, k, qt:qt + 1], bank(UNIT + k)[:, 0:SPAN], axis=AX.X, op=ALU.max, negate=True)\
                        .then_inc(unit_taken[k], 1)

                def split_maxima(b, g, target=None, todo=()):
                    done = MAX_STEPS * (2 * b + g)
                    for k in range(SPANS):
                        dve.wait_ge(unit_taken[k], PRIME + (2 * b + g + 1) * NQ)
                    dve.wait_ge(max_turned, PRIME + 2 * b + g)
                    nc.vector.tensor_reduce(NM, NMX.rearrange("p k q -> p q k"), axis=AX.X, op=ALU.min).then_inc(max_steps, 1)
                    dve.wait_ge(max_steps, done + 1)
                    nc.vector.tensor_copy(MP[:, 0, :], NM).then_inc(max_steps, 1)
                    for u in todo[0:1]:
                        take_max(*target, u)
                    dve.wait_ge(max_steps, done + 2)
                    nc.vector.tensor_tensor(NR, NM, MP[:, 0, :], ALU.subtract).then_inc(max_steps, 1)
                    for u in todo[1:2]:
                        take_max(*target, u)
                    dve.wait_ge(max_steps, done + 3)
                    nc.vector.tensor_copy(MP[:, 1, :], NR).then_inc(max_steps, 1)
                    for u in todo[2:3]:
                        take_max(*target, u)
                    dve.wait_ge(max_steps, done + 4)
                    nc.vector.tensor_tensor(MP[:, 2, :], NR, MP[:, 1, :], ALU.subtract).then_inc(max_split, 1)
                    for u in todo[3:]:
                        take_max(*target, u)

                def finish(b, g):
                    m = Steps(dve, out_steps, 2 * b + g, 1)
                    v = bank(AUX).rearrange("p (s j e) -> p s j e", s=4, j=NB)
                    dve.wait_ge(sums_turned, PRIME + 2 * b + g + 1)
                    m(nc.vector.reciprocal(rdn.rearrange("p (s j) -> p s j", s=4), v[:, :, :, DK]))
                    m.end()
                    for s in range(4):
                        hh, c = s // 2, s % 2
                        to = ONall[:, ds(2 * b + c, 1), g * 64:g * 64 + 64].rearrange("p n (j hh d) -> p (n j) hh d", hh=2, d=DK)
                        last = nc.vector.tensor_tensor(to[:, :, hh, :], v[:, s, :, 0:DK], bc(rdn[:, 4 * s:4 * s + 4], 2, DK), ALU.mult)
                    last.then_inc(heads_out, 1)

                def body(b, first=False, last=False):
                    for g in range(2):
                        for kt in range(KT):
                            target, todo = units(b, g, kt, last)
                            if kt == AHEAD and not (last and g):
                                split_maxima(*following(b, g), target, todo)
                            else:
                                for u in todo:
                                    take_max(*target, u)
                            if kt == 1 and (g or not first):
                                finish(*((b, 0) if g else (b - 1, 1)))

                for u in range(SPANS * NQ):
                    take_max(0, 0, u)
                split_maxima(0, 0)
                for u in first_units:
                    take_max(0, 1, u)
                body(0, first=True)
                with dve.Fori(1, B - 1) as b:
                    body(b)
                body(B - 1, last=True)
                finish(B - 1, 1)

            @block.gpsimd
            def _(pool):
                def keys_for_max(b, par):
                    for k in range(SPANS):
                        pool.wait_ge(unit_taken[k], PRIME + 2 * (b - 1) * NQ)
                    settle(pool)
                    nc.gpsimd.tensor_copy(KSa[par][0:MROW, :], KSall[0:MROW, ds(b, 1), :].rearrange("p b s -> p (b s)"))\
                        .then_inc(keys_max, 1)

                def keys_for_exp(b, par):
                    pool.wait_ge(scored[1], PRIME + score_fill(b - 1, 0, 0, 0))
                    settle(pool)
                    nc.gpsimd.tensor_copy(KSb[par], KSall[:, ds(b, 1), :].rearrange("p b s -> p (b s)")).then_inc(keys_exp, 1)

                def values(b, par):
                    for r in range(2):
                        pool.wait_ge(summed[r], PRIME + KT * (b - 1))
                    settle(pool)
                    nc.gpsimd.tensor_copy(Vc[par], Vall[:, ds(b, 1), :, :].rearrange("p b k e -> p (b k) e")).then_inc(values_ready, 1)

                def copies(b, par):
                    keys_for_max(b, par)
                    keys_for_exp(b, par)
                    values(b, par)

                nc.gpsimd.tensor_copy(KSb[0], KSall[:, 0, :]).then_inc(keys_exp, 1)
                nc.gpsimd.tensor_copy(Vc[0], Vall[:, 0, :, :]).then_inc(values_ready, 1)
                with pool.Fori(0, B // 2 - 1) as i:
                    for k in range(2):
                        copies(2 * i + 1 + k, 1 - k)
                copies(B - 1, 1)

            @block.tensor
            def _(pe):
                def fill_unit(b, g, par, turn, u):
                    qt, k = u // SPANS, u % SPANS
                    pe.wait_ge(unit_taken[k], PRIME + (2 * b + g) * NQ + qt)
                    if u == 0:
                        pe.wait_ge(q_stacked[par][g], PRIME + 16 * PARTS * (turn + 1))
                        if g == 0:
                            pe.wait_ge(keys_max, PRIME + b)
                    at = min(k * SPAN, S - SPAN)
                    nc.tensor.matmul(bank(UNIT + k)[:, 0:SPAN], Qg[par][g][:, qt * P:(qt + 1) * P], KSa[par][:, at:at + SPAN],
                                     start=True, stop=True).then_inc(unit_made[k], 1)

                def turn_maxima(b, g):
                    pe.wait_ge(heads_out, PRIME + 2 * b + g - 1)
                    pe.wait_ge(max_split, PRIME + 2 * b + g + 1)
                    settle(pe)
                    nc.tensor.transpose(bankb(AUX)[0:PARTS * NQ, 0:P], MP.rearrange("p i q -> p (i q)"), identb[:, :])\
                        .then_inc(max_turned, 1)

                def score(b, g, par, kt, j):
                    pe.wait_ge(powered[j % 2], PRIME + score_fill(b, g, kt, j))
                    if kt == 0 and j == 0:
                        pe.wait_ge(max_stacked, PRIME + 16 * (2 * b + g + 1))
                        if g == 0:
                            pe.wait_ge(keys_exp, PRIME + b + 1)
                    nc.tensor.matmul(bank(RING + j % 2), KSb[par][:, kt * P:(kt + 1) * P], Qg[par][g][:, j * 512:(j + 1) * 512],
                                     start=True, stop=True).then_inc(scored[j % 2], 1)

                def weigh(b, g, par, kt):
                    for r in range(2):
                        pe.wait_ge(powered[r], PRIME + score_fill(b, g, kt, 2) + 1)
                    if kt == 0:
                        pe.wait_ge(sums_saved, PRIME + 2 * b + g)
                        if g == 0:
                            pe.wait_ge(values_ready, PRIME + b + 1)
                    for j in range(NB):
                        last = nc.tensor.matmul(PS[32 * j:32 * j + 32, ACC, :], Vc[par][:, kt, :], PE_[:, parity(g, kt), j, :],
                                                start=kt == 0, stop=kt == KT - 1)
                    last.then_inc(summed[parity(g, kt)], 1)

                def finish(b, g):
                    pe.wait_ge(max_saved, PRIME + 2 * b + g + 2)
                    pe.wait_ge(sums_saved, PRIME + 2 * b + g + 1)
                    for s in range(4):
                        last = nc.tensor.transpose(bank(AUX)[:, s * P:(s + 1) * P], OT[:, s * P:(s + 1) * P], ident)
                    last.then_inc(sums_turned, 1)

                def body(b, par, turn, first=False, last=False):
                    for g in range(2):
                        for kt in range(KT):
                            target, todo = units(b, g, kt, last)
                            same = g == 0 and kt < AHEAD
                            place = (par, turn) if same else (1 - par, turn + par)

                            def maxima(first, n):
                                for u in todo[first:first + n]:
                                    fill_unit(*target, *place, u)

                            maxima(0, 1)
                            score(b, g, par, kt, 0)
                            maxima(1, 2)
                            score(b, g, par, kt, 1)
                            if kt:
                                weigh(b, g, par, kt - 1)
                            elif g:
                                weigh(b, 0, par, KT - 1)
                            elif not first:
                                weigh(b - 1, 1, 1 - par, KT - 1)
                            score(b, g, par, kt, 2)
                            maxima(3, 2)
                            if kt == AHEAD + 1 and not (last and g):
                                turn_maxima(*following(b, g))
                            score(b, g, par, kt, 3)
                            maxima(5, len(todo))
                            if kt == 1 and (g or not first):
                                finish(*((b, 0) if g else (b - 1, 1)))
                for u in range(SPANS * NQ):
                    fill_unit(0, 0, 0, 0, u)
                for u in first_units:
                    fill_unit(0, 1, 0, 0, u)
                turn_maxima(0, 0)
                body(0, 0, 0, first=True)
                with pe.Fori(0, B // 2 - 1) as i:
                    for k in range(2):
                        body(2 * i + 1 + k, 1 - k, i + k)
                body(B - 1, 1, B // 2 - 1, last=True)
                weigh(B - 1, 1, 1, KT - 1)
                pe.wait_ge(sums_saved, PRIME + 2 * B)
                pe.wait_ge(heads_out, PRIME + 2 * B - 1)
                for s in range(4):
                    last = nc.tensor.transpose(bank(AUX)[:, s * P:(s + 1) * P], OT[:, s * P:(s + 1) * P], ident)
                last.then_inc(sums_turned, 1)

        with nc.Block() as block:
            on_turned, onT_saved, o_made, x2_made = (S_(n) for n in ("on_turned", "onT_saved", "o_made", "x2_made"))
            bias_added = S_("bias_added")
            ln3_vec, ln3_act = S_("ln3_vec"), S_("ln3_act")
            xn3_made, x3_turned, x3_saved, lg_made = (S_(n) for n in ("xn3_made", "x3_turned", "x3_saved", "lg_made"))
            top_steps, lg_exp, coef_split, coef_turned, coef_saved = (S_(n) for n in ("top_steps", "lg_exp", "coef_split", "coef_turned", "coef_saved"))
            gate_made = [S_("gate_made0"), S_("gate_made1")]
            gate_used = [S_("gate_used0"), S_("gate_used1")]
            up_made = [S_("up_made0"), S_("up_made1")]
            up_used = [S_("up_used0"), S_("up_used1")]
            gated, down_made, out_made, stored = S_("gated"), S_("down_made"), S_("out_made"), S_("stored")
            fills = [len(range(par, HT, 2)) for par in range(2)]

            def count(q, k):
                return fills[k % 2] * q + k // 2

            @block.sync
            def _(sp):
                o = out.rearrange("b (c p) d -> p (b c) d", p=P)
                with sp.Fori(0, NT * P // TB) as q:
                    sp.wait_ge(out_made, PRIME + q + 1)
                    sp.dma_start(o[:, ds(4 * q, 4), :], X[:, ds(4 * q, 4), :]).then_inc(stored, 16)
                sp.wait_ge(stored, 16 * (NT * P // TB))

            @block.scalar
            def _(act):
                for r in blocks:
                    act.wait_ge(on_turned, r + 1)
                    nc.scalar.copy(X3T[:, r * TB:(r + 1) * TB], bank(r)).then_inc(onT_saved, 1)
                act.wait_ge(ln3_vec, LN_STEPS)
                a = Steps(act, ln3_act)
                a(nc.scalar.activation(st[:, 2, :], st[:, 1, :], ACT.Ln, bias=eps[:, :], scale=1.0 / D))
                a(nc.scalar.activation(st[:, 3, :], st[:, 2, :], ACT.Exp, scale=-0.5))
                for r in blocks:
                    act.wait_ge(x3_turned, r + 1)
                    nc.scalar.copy(X3T[:, r * TB:(r + 1) * TB], bank(r)).then_inc(x3_saved, 1)
                act.wait_ge(top_steps, TOP_SHIFT)
                nc.scalar.activation(SH, SH, ACT.Exp).then_inc(lg_exp, 1)
                act.wait_ge(coef_turned, 2)
                nc.scalar.copy(CTs[:, :].rearrange("p (k t) -> p k t", k=2),
                               PS[0:PARTS * NE, 4:6, :].bitcast(bf16)).then_inc(coef_saved, 1)
                with act.Fori(0, NT * P // TB) as q:
                    for k in range(HT):
                        act.wait_ge(gate_made[k % 2], PRIME + count(q, k) + 1)
                        act.wait_ge(up_used[k % 2], PRIME + count(q, k))
                        nc.scalar.activation(SG[:, k % 2, :], bank(k % 2), ACT.Silu).then_inc(gate_used[k % 2], 1)

            @block.vector
            def _(dve):
                nc.vector.tensor_tensor(X[:, :, :], X[:, :, :], bc(boS[:, :], 1, NT), ALU.add).then_inc(bias_added, 1)
                dve.wait_ge(bias_added, 1)
                for r in blocks:
                    n = slice(4 * r, 4 * r + 4)
                    dve.wait_ge(o_made, r + 1)
                    nc.vector.tensor_tensor(X[:, n, :], X[:, n, :], bank(4 + r).rearrange("p (n d) -> p n d", n=4), ALU.add)\
                        .then_inc(x2_made, 1)
                dve.wait_ge(x2_made, len(blocks))
                v = Steps(dve, ln3_vec)
                layer_norm_sums(v, X[:, :, :], XC, SQ, st)
                dve.wait_ge(ln3_act, 2)
                for r in blocks:
                    n = slice(4 * r, 4 * r + 4)
                    nc.vector.tensor_tensor(XC[:, n, :], XC[:, n, :], bc(st[:, 3, n], 2, D), ALU.mult).then_inc(xn3_made, 1)
                t = Steps(dve, top_steps)
                dve.wait_ge(lg_made, 1)
                t(nc.vector.tensor_copy(LG, bank(7)[:, 0:NT * NE].rearrange("p (n e) -> p n e", e=NE)))
                t(nc.vector.tensor_reduce(red, LG, axis=AX.X, op=ALU.max))
                t(nc.vector.tensor_tensor(SH, LG, bc(red, 2, NE), ALU.subtract))
                assert t.k == TOP_SHIFT
                dve.wait_ge(lg_exp, 1)
                t(nc.vector.reduce_sum(red, SH, axis=AX.X))
                t(nc.vector.reciprocal(rcp, red))
                t(nc.vector.tensor_tensor(PB, SH, bc(rcp, 2, NE), ALU.mult))
                t(nc.vector.tensor_copy(SH, PB))
                for picked in (S1, S2_):
                    t(nc.vector.tensor_reduce(red, SH, axis=AX.X, op=ALU.max))
                    t(nc.vector.tensor_tensor(KY, SH, bc(red, 2, NE), ALU.is_equal))
                    t(nc.vector.tensor_tensor(KY, KY, bc(rank, 1, NT), ALU.mult))
                    t(nc.vector.tensor_reduce(red, KY, axis=AX.X, op=ALU.max))
                    t(nc.vector.tensor_tensor(picked, KY, bc(red, 2, NE), ALU.is_equal))
                    t(nc.vector.scalar_tensor_tensor(SH, picked, -2.0, SH, ALU.mult, ALU.add))
                t(nc.vector.tensor_tensor(S1, S1, S2_, ALU.add))
                t(nc.vector.tensor_tensor(CR, PB, S1, ALU.mult))
                part = [CP[:, :, i * NE:(i + 1) * NE] for i in range(PARTS)]
                t(nc.vector.tensor_copy(part[0], CR))
                t(nc.vector.tensor_tensor(CR, CR, part[0], ALU.subtract))
                t(nc.vector.tensor_copy(part[1], CR))
                nc.vector.tensor_tensor(part[2], CR, part[1], ALU.subtract).then_inc(coef_split, 1)
                with dve.Fori(0, NT * P // TB) as q:
                    dve.wait_ge(down_made, PRIME + q)
                    for k in range(HT):
                        par = k % 2
                        dve.wait_ge(gate_used[par], PRIME + count(q, k) + 1)
                        dve.wait_ge(up_made[par], PRIME + count(q, k) + 1)
                        if k < HT - 1:
                            g = Steps(dve, gated, q, HT - 1)
                            g.k = k
                            g(nc.vector.tensor_tensor(Hb[:, k, :], SG[:, par, :], bank(2 + par), ALU.mult))
                            nc.vector.tensor_tensor(Hb[:, k, :], Hb[:, k, :], bank(4 + par), ALU.mult).then_inc(up_used[par], 1)
                        else:
                            nc.vector.tensor_tensor(Hb[:, k, :], SG[:, par, :], bank(2 + par), ALU.mult).then_inc(up_used[par], 1)
                    dve.wait_ge(down_made, PRIME + q + 1)
                    settle(dve)
                    n = ds(4 * q, 4)
                    nc.vector.tensor_tensor(X[:, n, :], X[:, n, :], bank(6).rearrange("p (n d) -> p n d", n=4), ALU.add)\
                        .then_inc(out_made, 1)

            @block.tensor
            def _(pe):
                for r in blocks:
                    for t in range(TB // P):
                        last = nc.tensor.transpose(bank(r)[:, t * P:(t + 1) * P], ONall[:, 4 * r + t, :], ident)
                    last.then_inc(on_turned, 1)
                for r in blocks:
                    pe.wait_ge(onT_saved, r + 1)
                    for t in range(TB // P):
                        at = r * TB + t * P
                        last = nc.tensor.matmul(bank(4 + r)[:, t * P:(t + 1) * P], X3T[:, at:at + P], WoS[:, :], start=True, stop=True)
                    last.then_inc(o_made, 1)
                for r in blocks:
                    pe.wait_ge(xn3_made, r + 1)
                    for t in range(TB // P):
                        last = nc.tensor.transpose(bank(r)[:, t * P:(t + 1) * P], XC[:, 4 * r + t, :], ident)
                    last.then_inc(x3_turned, 1)
                for r in blocks:
                    pe.wait_ge(x3_saved, r + 1)
                    for t in range(TB // P):
                        n = 4 * r + t
                        last = nc.tensor.matmul(bank(7)[:, n * NE:(n + 1) * NE], X3T[:, n * P:(n + 1) * P], RT[:, :], start=True, stop=True)
                last.then_inc(lg_made, 1)
                pe.wait_ge(coef_split, 1)
                for n in range(NT):
                    last = nc.tensor.transpose(bankb(4 + n // 8)[0:PARTS * NE, (n % 8) * P:(n % 8 + 1) * P],
                                               CP[:, n, 0:PARTS * NE], identb[:, :])
                    if n % 8 == 7:
                        last.then_inc(coef_turned, 1)
                pe.wait_ge(coef_saved, 1)
                with pe.Fori(0, NT * P // TB) as q:
                    tok = ds(TB * q, TB)
                    for k in range(HT):
                        par = k % 2
                        pe.wait_ge(gate_used[par], PRIME + count(q, k))
                        nc.tensor.matmul(bank(par), WG[:, k * P:(k + 1) * P], X3T[:, tok], start=True, stop=True)\
                            .then_inc(gate_made[par], 1)
                        pe.wait_ge(up_used[par], PRIME + count(q, k))
                        last = nc.tensor.matmul(bank(2 + par), WU[:, k * P:(k + 1) * P], X3T[:, tok], start=True, stop=True)
                        if k < HT - 1:
                            last = nc.tensor.matmul(bank(4 + par), selb[:, k, :], CTs[:, tok], start=True, stop=True)
                        last.then_inc(up_made[par], 1)
                    for par in range(2):
                        pe.wait_ge(up_used[par], PRIME + fills[par] * (q + 1))
                    pe.wait_ge(out_made, PRIME + q)
                    for t in range(TB // P):
                        for k in range(HT):
                            last = nc.tensor.matmul(bank(6)[:, t * D:(t + 1) * D], Hb[:, k, t * P:(t + 1) * P], WD[:, k, :],
                                                    start=k == 0, stop=k == HT - 1)
                    last.then_inc(down_made, 1)


def kernel(**inputs):
    import concourse.bacc as bacc
    from concourse.bass_utils import run_bass_kernel_spmd

    names = ["x", "ctx_1024", "L0_attn_W_in", "L0_attn_W_out", "L0_attn_dt_bias", "L0_attn_A_log", "L0_attn_D_skip",
             "L0_attn_norm_weight", "L0_xattn_Wq", "L0_xattn_bq", "L0_xattn_Wk", "L0_xattn_bk", "L0_xattn_Wv",
             "L0_xattn_bv", "L0_xattn_Wo", "L0_xattn_bo", "L0_ffn_router", "L0_ffn_experts_gate",
             "L0_ffn_experts_up", "L0_ffn_experts_down", "L0_ffn_shared_gate", "L0_ffn_shared_up",
             "L0_ffn_shared_down"]
    nc = bacc.Bacc("TRN2", target_bir_lowering=False, num_devices=1)
    arrays, args = {}, []
    for name in names + ["shape_constants"]:
        a = np.ascontiguousarray(inputs[name] if name in inputs else shape_constants())
        arrays[f"in_{name}"] = a
        args.append(nc.dram_tensor(f"in_{name}", a.shape, mybir.dt.from_np(a.dtype), kind="ExternalInput").ap())
    out = nc.dram_tensor("out_0", (B, L, D), mybir.dt.float32, kind="ExternalOutput").ap()
    build(nc, *args, out)
    r = run_bass_kernel_spmd(nc, [arrays], core_ids=[0])
    return r.results[0]["out_0"]
```

```python
from contextlib import ExitStack

import numpy as np

import concourse.bass as bass
from concourse import mybir

B, L, D = 8, 256, 128
P = 128
CH = L // P
NT = B * CH
NH, HD, NS = 4, 64, 64
DI = NH * HD
PAIRS = 16
XH, DK = 16, 8
S = 1601
KT = -(-S // P)
SP = KT * P
TAIL = S - (KT - 1) * P
NE, ED, SD = 8, 64, 128
HT = (NE * ED + SD) // P
EPS = 1e-5
PARTS = 3
QK = PARTS * PARTS * DK
MROW = 96
GH = XH // 2
GC = GH * L
NB = GC // 512
NQ = GC // P
SPANS = 4
SPAN = -(-S // SPANS)
LOGCAP = 200.0
ROUND = 1.5 * 2.0 ** 23
TWO_PI_HI = float(np.float32(6.28125))
TWO_PI_LO = float(np.float32(2 * np.pi - 6.28125))
PI = float(np.nextafter(np.float32(np.pi), np.float32(0)))
SCRATCH = 15700
CST_IDENT, CST_GT, CST_LE, CST_FREQ, CST_RANK, CST_SEL, CST_W = 0, 128, 256, 384, 400, 408, 408 + 4 * 128


def shape_constants():
    c = np.zeros((P, CST_W), np.float32)
    r = np.arange(P)
    c[:, CST_IDENT:CST_IDENT + P] = np.eye(P)
    c[:, CST_GT:CST_GT + P] = r[:, None] > r[None, :]
    c[:, CST_LE:CST_LE + P] = r[:, None] <= r[None, :]
    freq = np.float32(1.0) / np.power(np.float32(10000.0), np.arange(PAIRS, dtype=np.float32) / np.float32(PAIRS))
    c[:, CST_FREQ:CST_FREQ + PAIRS] = freq.astype(np.float32)
    c[:, CST_RANK:CST_RANK + NE] = NE - np.arange(NE)
    for k in range(HT - 1):
        for row in range(PARTS * NE):
            e = row % NE
            if e // 2 == k:
                at = CST_SEL + k * P + (e % 2) * ED
                c[row, at:at + ED] = 1.0
    return c


class Steps:

    def __init__(self, eng, sem, index=0, per=0, settle=None):
        self.eng, self.sem, self.base, self.per, self.k, self.settle = eng, sem, index * per, per, 0, settle

    def __call__(self, ins):
        self.k += 1
        ins.then_inc(self.sem, 1)
        self.eng.wait_ge(self.sem, self.base + self.k)
        if self.settle:
            self.settle(self.eng)

    def end(self):
        assert self.k == self.per, (self.sem, self.k, self.per)


PRIME = 2
PRIMED = (("projected", 2), ("z_saved", 2), ("bcd_saved", 2), ("xnT_saved", 0), ("xn_turned", 0), ("ctxT_saved", 4),
          ("kv_made", 0), ("kv_turned", 0), ("v_saved", 0), ("k_split", 0), ("k_stacked", 0), ("ks_turned", 2), ("ks_saved", 2),
          ("b_rotated", 0), ("b_plain", 0), ("c_ready", 0), ("dtx_made", 0), ("seg_made", 2), ("btt_made", 0),
          ("btt_saved", 0), ("ctt_made", 0), ("ctt_saved", 0), ("seg_summed", 2), ("decays_made", 2),
          ("products_made", 2), ("mixed", 2), ("state_made", 0), ("state_saved", 0), ("y_made", 0), ("y_read", 0),
          ("y_gated", 0), ("yt_made", 0), ("yt_saved", 0), ("mix_out", 0), ("raw_saved", 0), ("squared", 0),
          ("q_stacked", 4), ("keys_max", 0), ("keys_exp", 0), ("values_ready", 0),
          ("unit_made", SPANS), ("unit_taken", SPANS), ("max_split", 0), ("max_turned", 0),
          ("max_saved", 0), ("max_stacked", 0), ("scored", 2), ("powered", 2), ("summed", 2), ("sums_saved", 0),
          ("sums_turned", 0), ("heads_out", 0),
          ("gate_made", 2), ("gate_used", 2),
          ("up_made", 2), ("up_used", 2), ("down_made", 0), ("out_made", 0))
TOP_SHIFT = 2
AHEAD = 10
UNITS_AT = (5, 4, 5, 5, 5, 5, 5, 5, 5, 6, 4, 5, 5)
POOL_STEPS, MIX_STEPS, SQUARE_STEPS, MAX_STEPS = 8, 5, 1, 4
N_KEYS, N_SMALL = 10, 11
NORM_STEPS = 3
QUARTERS = 4
MID_E, MID_U, MID_DT, MID_CUM, K_STEPS = 2, 3, 11, 15, 3


def moments(eng, sems, k, X, BS, MV, st, arrived=None):
    ALU = mybir.AluOpType
    steps, inverse = sems[0:2]
    step = Steps(eng, steps, k, NORM_STEPS)
    for n in range(NT):
        if arrived and n % (NT // 2) == 0:
            eng.wait_ge(arrived[n // (NT // 2)], 16)
        last = eng.bn_stats(BS[:, n, :], X[:, n, :])
    step(last)
    for n in range(NT):
        last = eng.bn_aggr(MV[:, n, :], BS[:, n, :])
    step(last)
    step(eng.tensor_scalar(st[:, 0, :], MV[:, :, 1], EPS, None, ALU.add))
    step.end()
    eng.reciprocal(st[:, 1, :], st[:, 0, :]).then_inc(inverse, 1)


def deviations(eng, sems, k, st, warm):
    ACT = mybir.ActivationFunctionType
    inverse, deviated = sems[1:3]
    warm(ACT.Sqrt)
    eng.wait_ge(inverse, k + 1)
    eng.activation(st[:, 2, :], st[:, 1, :], ACT.Sqrt).then_inc(deviated, 1)


def normalise(eng, sems, k, X, XC, MV, st, done):
    ALU = mybir.AluOpType
    eng.wait_ge(sems[2], k + 1)
    for n in range(NT):
        last = eng.tensor_scalar(XC[:, n, :], X[:, n, :], MV[:, n, 0:1], st[:, 2, n:n + 1], ALU.subtract, ALU.mult)
        if n % (NT // QUARTERS) == NT // QUARTERS - 1:
            last.then_inc(done, 1)


def bc(ap, axis, n):
    v = ap.unsqueeze(axis)
    shape = list(v.shape)
    shape[axis] = n
    return v.to_broadcast(shape)


def build(nc, x, ctx_1024, W_in, W_out, dt_bias, A_log, D_skip, norm_weight, Wq, bq, Wk, bk, Wv, bv, Wo, bo,
          router, e_gate, e_up, e_down, s_gate, s_up, s_down, consts, out):
    f32, bf16 = mybir.dt.float32, mybir.dt.bfloat16
    ALU, ACT, AX = mybir.AluOpType, mybir.ActivationFunctionType, mybir.AxisListType
    ds = bass.ds
    es = ExitStack()
    with es:
        def sb(name, shape, dt=f32):
            return es.enter_context(nc.sbuf_tensor(name, shape, dt))

        def sem(name):
            return es.enter_context(nc.semaphore(name))

        X = sb("X", [P, NT, D])
        Z = sb("Z", [P, NT, DI])
        XS = sb("XS", [P, NT, DI])
        BCD = sb("BCD", [P, NT, 2 * NS + NH])
        COS = sb("COS", [P, NT, NH, PAIRS])
        SIN = sb("SIN", [P, NT, NH, PAIRS])
        KSall = sb("KSall", [P, B, SP], bf16)
        Vall = sb("Vall", [P, B, KT, 32])
        ONall = sb("ONall", [P, NT, D])
        CST = sb("CST", [P, CST_W])
        identb = sb("identb", [P, P], bf16)
        selb = sb("selb", [PARTS * NE, HT - 1, P], bf16)
        bigb = sb("bigb", [P, NH, P], bf16)
        Win = sb("Win", [P, 2 * DI + 2 * NS + NH])
        Wout = sb("Wout", [P, 2, D])
        nw = sb("nw", [P, 2])
        eps = sb("eps", [P, 1])
        half_pi = sb("half_pi", [P, 1])
        hb = sb("hb", [P, 3, NH])
        WqS = sb("WqS", [P, D])
        bqS = sb("bqS", [P, 1])
        WkvS = sb("WkvS", [P, 32])
        bkvS = sb("bkvS", [P, 1])
        WoS = sb("WoS", [P, D])
        boS = sb("boS", [P, D])
        RT = sb("RT", [P, NE])
        WG = sb("WG", [P, HT * P])
        WU = sb("WU", [P, HT * P])
        WD = sb("WD", [P, HT, D])
        ident = CST[:, CST_IDENT:CST_IDENT + P]
        mask_gt = CST[:, CST_GT:CST_GT + P]
        mask_le = CST[:, CST_LE:CST_LE + P]
        freq = CST[:, CST_FREQ:CST_FREQ + PAIRS]
        rank = CST[:, CST_RANK:CST_RANK + NE]
        BS = sb("BS", [P, NT, 6])
        MV = sb("MV", [P, NT, 2])
        st = sb("st", [P, 3, NT])
        DT = sb("DT", [P, 2, NT, NH])
        CUM = sb("CUM", [P, 2, NT, NH])
        EC = sb("EC", [P, NT, NH])
        tm = sb("tm", [P, 6, NT * NH])
        rs = sb("rs", [P, 3, NT])
        warmth = sb("warmth", [P, 16])

        SCR = sb("SCR", [P, SCRATCH])
        taken = [0]

        def scr(shape, dt=f32):
            n = int(np.prod(shape)) * (2 if dt == bf16 else 4) // 4
            v = SCR[:, taken[0]:taken[0] + n]
            taken[0] += n
            assert taken[0] <= SCRATCH, taken[0]
            if dt == bf16:
                v = v.bitcast(bf16)
            if len(shape) == 2:
                v = v.rearrange("p (a b) -> p a b", b=shape[1])
            if len(shape) == 3:
                v = v.rearrange("p (a b c) -> p a b c", b=shape[1], c=shape[2])
            return v

        XC = scr([NT, D])
        CTX = [scr([KT, D]) for _ in range(2)]
        CTXT = scr([2048])
        xns = scr([CH, D])
        xnT = scr([CH, P])
        KVT = scr([512])
        KF = scr([16, DK])
        KR = scr([16, DK])
        KPt = [scr([16, DK], bf16) for _ in range(PARTS)]
        KST = scr([16, P], bf16)
        ANG = CTX[0][:, 0:8, :].rearrange("p a b -> p (a b)").rearrange("p (n h i) -> p n h i", n=NT, h=NH)
        TR = CTX[1][:, 0:8, :].rearrange("p a b -> p (a b)").rearrange("p (n h i) -> p n h i", n=NT, h=NH)
        T2 = CTXT[:, 0:1024].rearrange("p (n h i) -> p n h i", n=NT, h=NH)
        taken[0] = NT * D
        BT = [scr([CH, NH, NS]) for _ in range(2)]
        CT = [scr([CH, NH, NS]) for _ in range(2)]
        CE = [scr([NH, NS]) for _ in range(2)]
        BTT = [scr([CH * 2, P]) for _ in range(2)]
        CTZ = [scr([CH, NH, P]) for _ in range(2)]
        LM = [scr([CH, NH, P]) for _ in range(2)]
        dtx = [scr([CH, NH, HD]) for _ in range(2)]
        dtxe = [scr([NH, HD]) for _ in range(2)]
        SR = [scr([NH, P]) for _ in range(CH)]
        r1 = scr([CH * NH, PAIRS])
        r2 = scr([CH * NH, PAIRS])
        c1 = scr([CH * NH, PAIRS])
        c2 = scr([CH * NH, PAIRS])
        CET = scr([2, P])
        HZ = scr([NH, HD])
        Y = scr([CH, DI])
        YT = scr([CH * 2, P])
        junk = scr([DI])
        rms = scr([2])
        taken[0] = NT * D
        xqT = scr([B * L])
        QF = scr([B * L])
        QP = scr([PARTS, B * L], bf16)
        Qg = [[scr([GC], bf16) for _ in range(2)] for _ in range(2)]
        KSa = [scr([SP], bf16) for _ in range(2)]
        PE_ = Z[:, :, :].rearrange("p a b -> p (a b)").rearrange("p (k j c) -> p k j c", k=2, j=NB)
        SCR, taken[0] = XS[:, :, :].rearrange("p a b -> p (a b)"), 0
        KSb = [scr([SP], bf16) for _ in range(2)]
        Vc = [scr([KT, 32]) for _ in range(2)]
        NMX = scr([SPANS, NQ])
        NM = scr([NQ])
        NR = scr([NQ])
        MP = scr([PARTS, NQ], bf16)
        MT = scr([P], bf16)
        OT = scr([512])
        rdn = scr([16])
        assert taken[0] <= NT * DI
        X3T = Z[:, 0:8, :].rearrange("p a b -> p (a b)")
        SG = Z[:, 8:12, :].rearrange("p a b -> p (a b)").rearrange("p (a b) -> p a b", b=512)
        Hb = XS[:, 0:10, :].rearrange("p a b -> p (a b)").rearrange("p (a b) -> p a b", b=512)
        T8 = XS[:, 10:16, :].rearrange("p a b -> p (a b)")
        SH, KY, S1, S2_, PB = [T8[:, k * 128:(k + 1) * 128].rearrange("p (n e) -> p n e", e=NE) for k in range(5)]
        CP = T8[:, 768:768 + 256].bitcast(bf16).rearrange("p (n e) -> p n e", e=32)
        red = T8[:, 1024:1024 + 16]
        rcp = T8[:, 1040:1040 + 16]
        CR = T8[:, 1056:1056 + 128].rearrange("p (n e) -> p n e", e=NE)
        CTs = Z[:, 12:16, :].rearrange("p a b -> p (a b)")[0:PARTS * NE, :].bitcast(bf16)

        PS = es.enter_context(nc.psum_tensor("PS", [P, 8, 512], f32))
        UNIT, RING, ACC, AUX = 0, 4, 6, 7


        sems = {}

        def S_(name):
            if name not in sems:
                sems[name] = es.enter_context(nc.semaphore(name))
            return sems[name]

        primed = []
        for name, n in PRIMED:
            primed += [S_(f"{name}{k}") for k in range(n)] if n else [S_(name)]
        with nc.Block() as block:
            @block.sync
            def _(sp):
                for p in primed[0::4]:
                    sp.sem_inc(p, PRIME)

            @block.gpsimd
            def _(pool):
                for p in primed[1::4]:
                    pool.sem_inc(p, PRIME)

            @block.scalar
            def _(act):
                for p in primed[2::4]:
                    act.sem_inc(p, PRIME)

            @block.vector
            def _(dve):
                for p in primed[3::4]:
                    dve.sem_inc(p, PRIME)

        norms = [S_(f"norm_{what}") for what in ("steps", "inverse", "deviated")]
        tokens_normed = S_("tokens_normed")

        warmed = []

        def warm(function):
            warmed.append(function)
            k = len(warmed)
            nc.scalar.activation(warmth[:, k:k + 1], eps[:, :], function)

        def settle(eng):
            eng.sem_inc(S_("settled"), 1)

        q_dram = nc.dram_tensor("q_parts", (XH, PARTS, DK, B * L), bf16, kind="Internal").ap()

        def row(v):
            return v.rearrange("(o a) -> o a", o=1).to_broadcast([P, v.shape[0]])

        def col(v):
            return v.rearrange("(a o) -> a o", o=1)

        def bank(k):
            return PS[:, k, :]

        def bankb(k):
            return PS[:, k, :].bitcast(bf16)

        with nc.Block() as block:
            x_in, w_in, c_in, w_set = [S_("x_in0"), S_("x_in1")], S_("w_in"), S_("c_in"), S_("w_set")
            kv_set, experts_set = S_("kv_set"), S_("experts_set")
            zeroed, consts_cast = S_("zeroed"), S_("consts_cast")
            ctx_in = [S_("ctx_in0"), S_("ctx_in1")]
            xn_made, xn_turned, xnT_saved = S_("xn_made"), S_("xn_turned"), S_("xnT_saved")
            projected = [S_("projected0"), S_("projected1")]
            z_saved = [S_("z_saved0"), S_("z_saved1")]
            bcd_saved = [S_("bcd_saved0"), S_("bcd_saved1")]
            ctx_turned = [S_(f"ctx_turned{q}") for q in range(4)]
            ctxT_saved = [S_(f"ctxT_saved{q}") for q in range(4)]
            kv_made, kv_saved, kv_turned, v_saved = S_("kv_made"), S_("kv_saved"), S_("kv_turned"), S_("v_saved")
            k_split, k_steps, k_stacked = S_("k_split"), S_("k_steps"), S_("k_stacked")
            ks_turned = [S_("ks_turned0"), S_("ks_turned1")]
            ks_saved = [S_("ks_saved0"), S_("ks_saved1")]
            mid_vec, mid_act, cum_made = S_("mid_vec"), S_("mid_act"), S_("cum_made")
            trig_arg = S_("trig_arg")

            XN, ZX, STACK, CTXB, KV = 0, (1, 2), 4, (5, 6), 7
            BC = [bank(3)[:, 0:2 * NS + NH], bank(XN)[:, CH * P:CH * P + 2 * NS + NH]]

            @block.sync
            def _(sp):
                for h in range(2):
                    n = slice(h * NT // 2, (h + 1) * NT // 2)
                    sp.dma_start(X[:, n, :], x.rearrange("b (c p) d -> p (b c) d", p=P)[:, n, :]).then_inc(x_in[h], 16)
                sp.dma_start(CST[:, :], consts).then_inc(c_in, 16)
                sp.dma_start(Win[:, :], W_in).then_inc(w_in, 16)
                sp.wait_ge(zeroed, 1)

                def load_context(b, half):
                    main = ctx_1024[:, 0:(KT - 1) * P, :].rearrange("b (p j) d -> p b j d", p=P)
                    tail = ctx_1024[:, (KT - 1) * P:S, :].rearrange("b p d -> p b d")
                    sp.dma_start(CTX[half][:, 0:KT - 1, :].unsqueeze(1), main[:, ds(b, 1)]).then_inc(ctx_in[half], 16)
                    sp.dma_start(CTX[half][0:TAIL, KT - 1:KT, :], tail[:, ds(b, 1)]).then_inc(ctx_in[half], 16)

                load_context(0, 0)
                keys = [(WkvS[:, 0:DK], Wk), (WkvS[:, DK:2 * DK], Wv)]
                keys += [(bkvS[32 * j:32 * j + DK, :], col(bk)) for j in range(4)]
                keys += [(bkvS[32 * j + DK:32 * j + 2 * DK, :], col(bv)) for j in range(4)]
                for to, what in keys:
                    sp.dma_start(to, what).then_inc(kv_set, 16)
                assert len(keys) == N_KEYS
                load_context(1, 1)
                small = [(hb[:, 0, :], row(dt_bias)), (hb[:, 1, :], row(A_log)), (hb[:, 2, :], row(D_skip))]
                small += [(Wout[:, :, :], W_out.rearrange("(k p) d -> p k d", p=P)),
                          (nw[:, 0:1], col(norm_weight[0:P])), (nw[:, 1:2], col(norm_weight[P:2 * P])),
                          (WqS[:, :], Wq), (bqS[:, :], col(bq)), (WoS[:, :], Wo), (boS[:, :], row(bo)),
                          (RT[:, :], router)]
                for n, (to, what) in enumerate(small):
                    sp.dma_start(to, what).then_inc(w_set, 16)
                assert len(small) == N_SMALL
                with sp.Fori(1, B // 2) as i:
                    for half in range(2):
                        sp.wait_ge(ctx_turned[3], 2 * i + half - 1)
                        load_context(2 * i + half, half)
                for to, what in ((WG, e_gate), (WU, e_up)):
                    sp.dma_start(to[:, 0:NE * ED].rearrange("p (e d) -> p e d", e=NE),
                                 what.rearrange("e h d -> h e d")).then_inc(experts_set, 16)
                sp.dma_start(WG[:, NE * ED:], s_gate).then_inc(experts_set, 16)
                sp.dma_start(WU[:, NE * ED:], s_up).then_inc(experts_set, 16)
                sp.dma_start(WD[:, 0:HT - 1, :], e_down.rearrange("(k e) d h -> (e d) k h", e=2)).then_inc(experts_set, 16)
                sp.dma_start(WD[:, HT - 1, :], s_down).then_inc(experts_set, 16)
                sp.wait_ge(experts_set, 16 * 6)

            @block.gpsimd
            def _(pool):
                g = Steps(pool, S_("pool_zeroes"))
                g(nc.gpsimd.memset(WkvS[:, :], 0.0))
                g(nc.gpsimd.memset(bkvS[:, :], 0.0))
                g(nc.gpsimd.memset(eps[:, :], EPS))
                g(nc.gpsimd.memset(half_pi[:, :], float(np.pi / 2)))
                for half in range(2):
                    g(nc.gpsimd.memset(CTX[half][64:P, KT - 1, :], 0.0))
                g(nc.gpsimd.memset(CTXT[:, SP:2048], 0.0))
                g(nc.gpsimd.memset(KST[:, :, :], 0.0))
                g(nc.gpsimd.memset(Vall[:, :, :, :], 0.0))
                g(nc.gpsimd.memset(KST[:, :, MROW:MROW + PARTS], 1.0))
                g(nc.gpsimd.memset(Vall[:, :, 0:KT - 1, DK:DK + 1], 1.0))
                g(nc.gpsimd.memset(Vall[0:TAIL, :, KT - 1:KT, DK:DK + 1], 1.0))
                nc.gpsimd.memset(KSall[:, :, S:SP], 0.0).then_inc(zeroed, 1)

            @block.scalar
            def _(act):
                act.wait_ge(zeroed, 1)
                deviations(act, norms, 0, st, warm)

                def keep_stack(b):
                    act.wait_ge(ks_turned[0], PRIME + b + 1)
                    settle(act)
                    nc.scalar.copy(KSall[:, ds(b, 1), 0:8 * P], bankb(STACK).unsqueeze(1)).then_inc(ks_saved[0], 1)

                def keep_xnT(b):
                    act.wait_ge(xn_turned, PRIME + b + 1)
                    act.wait_ge(projected[1], PRIME + b)
                    nc.scalar.copy(xnT[:, :, :], bank(XN)[:, 0:CH * P].rearrange("p (c t) -> p c t", c=CH)).then_inc(xnT_saved, 1)

                def keep_projected(b, c):
                    act.wait_ge(projected[c], PRIME + b + 1)
                    settle(act)
                    n = ds(2 * b + c, 1)
                    nc.scalar.copy(Z[:, n, :], bank(ZX[c])[:, 0:DI].unsqueeze(1))
                    nc.scalar.copy(XS[:, n, :], bank(ZX[c])[:, DI:2 * DI].unsqueeze(1)).then_inc(z_saved[c], 1)

                def stack(b):
                    act.wait_ge(k_split, PRIME + b + 1)
                    act.wait_ge(ks_turned[1], PRIME + b)
                    for j in range(PARTS):
                        to = KST[:, :, 0:QK].rearrange("p t (j i d) -> p t j i d", i=PARTS, j=PARTS)[:, :, j, :, :]
                        last = nc.scalar.copy(to, bc(KPt[j], 2, PARTS))
                    last.then_inc(k_stacked, 1)

                def body(b, before, last=False):
                    keep_projected(b, 0)
                    if before == 2:
                        keep_stack(b - 2)
                    keep_projected(b, 1)
                    if before == 0:
                        act.wait_ge(kv_set, 16 * N_KEYS)
                    act.wait_ge(kv_made, PRIME + b + 1)
                    act.wait_ge(kv_turned, PRIME + b)
                    nc.scalar.activation(KVT[:, :], bank(KV), ACT.Identity, bias=bkvS[:, :]).then_inc(kv_saved, 1)
                    if not last:
                        keep_xnT(b + 1)
                    if before:
                        stack(b - 1)

                keep_xnT(0)
                body(0, 0)
                body(1, 1)
                with act.Fori(2, B - 1) as b:
                    body(b, 2)
                body(B - 1, 2, last=True)
                keep_stack(B - 2)
                stack(B - 1)
                warm(ACT.Exp)
                act.wait_ge(w_set, 16 * N_SMALL)
                m = Steps(act, mid_act)
                act.wait_ge(mid_vec, MID_E)
                m(nc.scalar.activation(tm[:, 1, :], tm[:, 0, :], ACT.Exp))
                m(nc.scalar.activation(hb[:, 1, :], hb[:, 1, :], ACT.Exp))
                warm(ACT.Ln)
                act.wait_ge(mid_vec, MID_U)
                m(nc.scalar.activation(tm[:, 3, :], tm[:, 2, :], ACT.Ln))
                keep_stack(B - 1)
                nc.scalar.activation(Z[:, :, :], Z[:, :, :], ACT.Silu)
                warm(ACT.Exp)
                act.wait_ge(mid_vec, MID_CUM)
                m(nc.scalar.activation(EC[:, :, :], CUM[:, 1, :, :], ACT.Exp, scale=-1.0))
                warm(ACT.Sin)
                act.wait_ge(trig_arg, 1)
                nc.scalar.activation(SIN[:, :, :, :], T2, ACT.Sin)
                act.wait_ge(trig_arg, 2)
                nc.scalar.activation(COS[:, :, :, :], TR, ACT.Sin, bias=half_pi[:, :])

            @block.vector
            def _(dve):
                moments(dve, norms, 0, X, BS, MV, st, x_in)
                dve.wait_ge(c_in, 16)
                nc.vector.tensor_copy(identb[:, :], ident)
                nc.vector.tensor_copy(selb[:, :, :], CST[0:PARTS * NE, CST_SEL:CST_SEL + (HT - 1) * P]
                                      .rearrange("p (k r) -> p k r", k=HT - 1))
                nc.vector.tensor_scalar(bigb[:, :, :], bc(mask_gt, 1, NH), 30000.0, None, ALU.mult).then_inc(consts_cast, 1)
                normalise(dve, norms, 0, X, XC, MV, st, tokens_normed)
                dve.wait_ge(tokens_normed, QUARTERS)

                def make_xn(b):
                    dve.wait_ge(xn_turned, PRIME + b)
                    n = ds(2 * b, CH)
                    settle(dve)
                    nc.vector.tensor_copy(xns[:, :, :], XC[:, n, :]).then_inc(xn_made, 1)

                def keep_ctxT(b, q, n):
                    dve.wait_ge(ctx_turned[q], b + 1)
                    dve.wait_ge(kv_made, PRIME + b)
                    nc.vector.tensor_copy(CTXT[:, 512 * q:512 * q + n], bank(CTXB[q % 2])[:, 0:n]).then_inc(ctxT_saved[q], 1)

                def keep_bcd(b, c):
                    dve.wait_ge(projected[c], PRIME + b + 1)
                    settle(dve)
                    nc.vector.tensor_copy(BCD[:, ds(2 * b + c, 1), :], BC[c].unsqueeze(1))\
                        .then_inc(bcd_saved[c], 1)

                def keep_stack(b):
                    dve.wait_ge(ks_turned[1], PRIME + b + 1)
                    settle(dve)
                    nc.vector.tensor_copy(KSall[:, ds(b, 1), 8 * P:S], bankb(STACK)[:, 0:S - 8 * P].unsqueeze(1))\
                        .then_inc(ks_saved[1], 1)

                def read_keys(b, first=False):
                    dve.wait_ge(kv_turned, PRIME + b + 1)
                    dve.wait_ge(k_steps, K_STEPS * b + 1)
                    if first:
                        dve.wait_ge(zeroed, 1)
                    kv = bank(KV).rearrange("p (s j e) -> p j s e", s=4, j=4)
                    settle(dve)
                    nc.vector.tensor_copy(KF.rearrange("p (j s) d -> p j s d", j=4), kv[:, :, :, 0:DK])
                    for j in range(3):
                        nc.vector.tensor_copy(Vall[:, ds(b, 1), 4 * j:4 * j + 4, 0:DK], kv[:, j:j + 1, :, DK:2 * DK])
                    nc.vector.tensor_copy(Vall[0:TAIL, ds(b, 1), KT - 1:KT, 0:DK], kv[0:TAIL, 3:4, 0:1, DK:2 * DK])\
                        .then_inc(v_saved, 1)

                def split_keys(b):
                    k = Steps(dve, k_steps, b, K_STEPS)
                    k.base += 1
                    dve.wait_ge(v_saved, PRIME + b + 1)
                    dve.wait_ge(k_stacked, PRIME + b)
                    k(nc.vector.tensor_copy(KPt[0], KF))
                    k(nc.vector.tensor_tensor(KR, KF, KPt[0], ALU.subtract))
                    k(nc.vector.tensor_copy(KPt[1], KR))
                    k.end()
                    nc.vector.tensor_tensor(KPt[2], KR, KPt[1], ALU.subtract).then_inc(k_split, 1)
                    dve.wait_ge(k_split, PRIME + b + 1)

                def body(b, before, last=False):
                    keep_ctxT(b, 0, 512)
                    keep_ctxT(b, 1, 512)
                    if before:
                        read_keys(b - 1, first=before == 1)
                    keep_ctxT(b, 2, 512)
                    keep_ctxT(b, 3, P)
                    keep_bcd(b, 0)
                    keep_bcd(b, 1)
                    if not last:
                        make_xn(b + 1)
                    if before == 2:
                        keep_stack(b - 2)
                    if before:
                        split_keys(b - 1)

                dve.sem_inc(k_steps, 1)
                make_xn(0)
                body(0, 0)
                body(1, 1)
                with dve.Fori(2, B - 1) as b:
                    body(b, 2)
                body(B - 1, 2, last=True)
                read_keys(B - 1)
                keep_stack(B - 2)
                split_keys(B - 1)
                m = Steps(dve, mid_vec)
                dve.wait_ge(w_set, 16 * N_SMALL)
                raw = DT[:, 0, :, :]
                flat = raw.rearrange("p n h -> p (n h)")
                dve.wait_ge(bcd_saved[0], PRIME + B)
                dve.wait_ge(bcd_saved[1], PRIME + B)
                m(nc.vector.tensor_tensor(raw, BCD[:, :, 2 * NS:], bc(hb[:, 0, :], 1, NT), ALU.add))
                m(nc.vector.scalar_tensor_tensor(tm[:, 0, :], flat, -1.0, flat, ALU.mult, ALU.min))
                assert m.k == MID_E
                dve.wait_ge(mid_act, 2)
                m(nc.vector.tensor_scalar(tm[:, 2, :], tm[:, 1, :], 1.0, None, ALU.add))
                assert m.k == MID_U
                m(nc.vector.tensor_scalar(tm[:, 4, :], tm[:, 2, :], -1.0, None, ALU.add))
                m(nc.vector.tensor_tensor(tm[:, 4, :], tm[:, 1, :], tm[:, 4, :], ALU.subtract))
                m(nc.vector.reciprocal(tm[:, 5, :], tm[:, 2, :]))
                m(nc.vector.tensor_tensor(tm[:, 4, :], tm[:, 4, :], tm[:, 5, :], ALU.mult))
                dve.wait_ge(mid_act, 3)
                m(nc.vector.tensor_tensor(tm[:, 3, :], tm[:, 3, :], tm[:, 4, :], ALU.add))
                m(nc.vector.scalar_tensor_tensor(flat, flat, 0.0, tm[:, 3, :], ALU.max, ALU.add))
                m(nc.vector.tensor_tensor(DT[:, 1, :, :], raw, bc(hb[:, 1, :], 1, NT), ALU.mult))
                m(nc.vector.tensor_scalar(DT[:, 1, :, :], DT[:, 1, :, :], LOGCAP, None, ALU.min))
                assert m.k == MID_DT
                dve.wait_ge(cum_made, 1)
                cum = bank(0)[:, 0:P].rearrange("p (c k b h) -> p c k b h", c=2, k=2, b=B)
                CV = CUM[:, :, :, :].rearrange("p k (b c) h -> p k b c h", c=2)
                m(nc.vector.tensor_scalar(CV[:, 0, :, 0, :], cum[:, 0, 0], -1.0, None, ALU.mult))
                m(nc.vector.tensor_copy(CV[:, 1, :, 0, :], cum[:, 0, 1]))
                m(nc.vector.tensor_copy(CV[:, 0, :, 1, :], cum[:, 1, 0]))
                m(nc.vector.tensor_copy(CV[:, 1, :, 1, :], cum[:, 1, 1]))
                assert m.k == MID_CUM
                shape = [P, NT, NH, PAIRS]
                fr = freq.unsqueeze(1).unsqueeze(1).to_broadcast(shape)
                m(nc.vector.tensor_tensor(ANG, bc(CUM[:, 0, :, :], 3, PAIRS), fr, ALU.mult))
                m(nc.vector.tensor_scalar(TR, ANG, float(0.5 / np.pi), ROUND, ALU.mult, ALU.add))
                m(nc.vector.tensor_scalar(TR, TR, ROUND, None, ALU.subtract))
                m(nc.vector.scalar_tensor_tensor(T2, TR, -TWO_PI_HI, ANG, ALU.mult, ALU.add))
                m(nc.vector.scalar_tensor_tensor(T2, TR, -TWO_PI_LO, T2, ALU.mult, ALU.add))
                nc.vector.tensor_scalar(T2, T2, PI, -PI, ALU.min, ALU.max).then_inc(trig_arg, 1)
                dve.wait_ge(trig_arg, 1)
                nc.vector.scalar_tensor_tensor(TR, T2, -1.0, T2, ALU.mult, ALU.min).then_inc(trig_arg, 1)
                keep_stack(B - 1)
                for k in range(2):
                    m(nc.vector.tensor_scalar(Wout[:, k, :], Wout[:, k, :], nw[:, k:k + 1], None, ALU.mult))

            @block.tensor
            def _(pe):
                pe.wait_ge(c_in, 16)
                pe.wait_ge(w_in, 16)
                pe.wait_ge(consts_cast, 1)
                pe.wait_ge(zeroed, 1)

                def turn_ctx(b, half, q, n):
                    if q < 2:
                        pe.wait_ge(ctxT_saved[q + 2], PRIME + b)
                    else:
                        pe.wait_ge(ctxT_saved[q - 2], PRIME + b + 1)
                    for t in range(n):
                        last = nc.tensor.transpose(bank(CTXB[q % 2])[:, t * P:(t + 1) * P], CTX[half][:, 4 * q + t, :], ident)
                    last.then_inc(ctx_turned[q], 1)

                def project(b, c):
                    pe.wait_ge(xnT_saved, PRIME + b + 1)
                    pe.wait_ge(z_saved[c], PRIME + b)
                    pe.wait_ge(bcd_saved[c], PRIME + b)
                    nc.tensor.matmul(bank(ZX[c]), xnT[:, c, :], Win[:, 0:2 * DI], start=True, stop=True)
                    nc.tensor.matmul(BC[c], xnT[:, c, :], Win[:, 2 * DI:], start=True, stop=True)\
                        .then_inc(projected[c], 1)

                def turn_stack(b, part):
                    if part == 0:
                        pe.wait_ge(k_stacked, PRIME + b + 1)
                        pe.wait_ge(ks_saved[1], PRIME + b)
                    else:
                        pe.wait_ge(ks_saved[0], PRIME + b + 1)
                    for t in (range(8), range(8, KT))[part]:
                        last = nc.tensor.transpose(bankb(STACK)[:, (t % 8) * P:(t % 8 + 1) * P], KST[:, t, :], identb[:, :])
                    last.then_inc(ks_turned[part], 1)

                def turn_xn(b):
                    pe.wait_ge(xn_made, b + 1)
                    pe.wait_ge(xnT_saved, PRIME + b)
                    pe.wait_ge(bcd_saved[1], PRIME + b)
                    for c in range(CH):
                        last = nc.tensor.transpose(bank(XN)[:, c * P:(c + 1) * P], xns[:, c, :], ident)
                    last.then_inc(xn_turned, 1)

                def body(b, half, turn, before, last=False):
                    pe.wait_ge(ctx_in[half], 32 * (turn + 1))
                    turn_ctx(b, half, 0, 4)
                    turn_ctx(b, half, 1, 4)
                    if before == 2:
                        turn_stack(b - 2, 0)
                    project(b, 0)
                    turn_ctx(b, half, 2, 4)
                    turn_ctx(b, half, 3, 1)
                    project(b, 1)
                    if before == 0:
                        pe.wait_ge(kv_set, 16 * N_KEYS)
                    for q in range(4):
                        pe.wait_ge(ctxT_saved[q], PRIME + b + 1)
                    pe.wait_ge(v_saved, PRIME + b)
                    for j in range(4):
                        done = nc.tensor.matmul(PS[32 * j:32 * j + 32, KV, :], WkvS[:, :], CTXT[:, 512 * j:512 * j + 512],
                                                start=True, stop=True)
                    done.then_inc(kv_made, 1)
                    if not last:
                        turn_xn(b + 1)
                    if before == 2:
                        turn_stack(b - 2, 1)
                    pe.wait_ge(kv_saved, b + 1)
                    for t in range(4):
                        done = nc.tensor.transpose(bank(KV)[:, t * P:(t + 1) * P], KVT[:, t * P:(t + 1) * P], ident)
                    done.then_inc(kv_turned, 1)

                turn_xn(0)
                body(0, 0, 0, 0)
                body(1, 1, 0, 1)
                with pe.Fori(1, B // 2 - 1) as i:
                    for half in range(2):
                        body(2 * i + half, half, i, 2)
                body(B - 2, 0, B // 2 - 1, 2)
                body(B - 1, 1, B // 2 - 1, 2, last=True)
                turn_stack(B - 2, 0)
                turn_stack(B - 2, 1)
                turn_stack(B - 1, 0)
                pe.wait_ge(mid_vec, MID_DT)
                for c, mask in enumerate((mask_gt, mask_le)):
                    rhs = DT[:, :, :, :].rearrange("p k (b c) h -> p k b c h", c=2)[:, :, :, c, :]
                    last = nc.tensor.matmul(bank(0)[:, 64 * c:64 * c + 64], mask, rhs, start=True, stop=True)
                last.then_inc(cum_made, 1)
                turn_stack(B - 1, 1)

        with nc.Block() as block:
            mixer_zeroed = S_("mixer_zeroed")
            b_turned_in, b_plain, c_ready, dtx_made = S_("b_rotated"), S_("b_plain"), S_("c_ready"), S_("dtx_made")
            pool_steps, mix_steps, square_steps = S_("pool_steps"), S_("mix_steps"), S_("square_steps")
            seg_made = [S_("seg_made0"), S_("seg_made1")]
            btt_made, btt_saved, ctt_made, ctt_saved = S_("btt_made"), S_("btt_saved"), S_("ctt_made"), S_("ctt_saved")
            seg_summed = [S_("seg_summed0"), S_("seg_summed1")]
            decays_made = [S_("decays_made0"), S_("decays_made1")]
            products_made = [S_("products_made0"), S_("products_made1")]
            mixed = [S_("mixed0"), S_("mixed1")]
            state_made, state_saved = S_("state_made"), S_("state_saved")
            y_made, y_read, y_gated, squared = S_("y_made"), S_("y_read"), S_("y_gated"), S_("squared")
            yt_made, yt_saved, mix_out, raw_saved = S_("yt_made"), S_("yt_saved"), S_("mix_out"), S_("raw_saved")
            B_TURN, C_TURN, SEG, PRODUCTS, STATE, OUTPUT = 0, 1, 2, 4, 6, 7

            def rotate(eng, step, src, to, t1, t2, n, sem=None):
                sh = [P, CH, NH, PAIRS]
                pair = src[:, :, 0:2 * PAIRS].rearrange("p n (i two) -> p n two i", two=2)
                one, two = (pair[:, :, k, :].unsqueeze(2).to_broadcast(sh) for k in range(2))
                a = t1.rearrange("p (n h) i -> p n h i", n=CH)
                c = t2.rearrange("p (n h) i -> p n h i", n=CH)
                dst = to[:, :, :, 0:2 * PAIRS].rearrange("p n h (i two) -> p n h i two", two=2)
                cos, sin = COS[:, n, :, :], SIN[:, n, :, :]
                step(eng.tensor_tensor(a, cos, one, ALU.mult))
                step(eng.tensor_tensor(c, sin, two, ALU.mult))
                step(eng.tensor_tensor(dst[:, :, :, :, 0], a, c, ALU.add))
                step(eng.tensor_tensor(a, cos, two, ALU.mult))
                step(eng.tensor_tensor(c, sin, one, ALU.mult))
                final = eng.tensor_tensor(dst[:, :, :, :, 1], a, c, ALU.subtract)
                if sem is None:
                    step(final)
                else:
                    final.then_inc(sem, 1)

            @block.gpsimd
            def _(pool):
                def mixer(b, h):
                    p = Steps(pool, pool_steps, b, POOL_STEPS, settle)
                    n = ds(2 * b, CH)
                    Bp, Cp = BCD[:, n, PAIRS * 2:NS], BCD[:, n, NS + PAIRS * 2:2 * NS]
                    pool.wait_ge(state_made, PRIME + b - 1)
                    pool.wait_ge(btt_made, PRIME + b - 1)
                    settle(pool)
                    nc.gpsimd.tensor_copy(BT[h][:, :, :, PAIRS * 2:], bc(Bp, 2, NH)).then_inc(b_plain, 1)
                    pool.wait_ge(ctt_made, PRIME + b - 1)
                    settle(pool)
                    p(nc.gpsimd.tensor_copy(CT[h][:, :, :, PAIRS * 2:], bc(Cp, 2, NH)))
                    rotate(pool, p, BCD[:, n, NS:2 * NS], CT[h], c1, c2, n)
                    xs4 = XS[:, n, :].rearrange("p n (h e) -> p n h e", h=NH)
                    nc.gpsimd.tensor_tensor(CE[h], CT[h][:, 1, :, :], bc(EC[:, ds(2 * b + 1, 1), :].rearrange("p n h -> p (n h)"), 2, NS),
                                            ALU.mult).then_inc(c_ready, 1)
                    pool.wait_ge(y_made, PRIME + b - 1)
                    settle(pool)
                    p(nc.gpsimd.tensor_tensor(dtx[h], xs4, bc(DT[:, 0, n, :], 3, HD), ALU.mult))
                    nc.gpsimd.tensor_tensor(dtxe[h], dtx[h][:, 0], bc(EC[:, ds(2 * b, 1), :].rearrange("p n h -> p (n h)"), 2, HD),
                                            ALU.mult).then_inc(dtx_made, 1)
                    p.end()

                with pool.Fori(0, B // 2) as i:
                    for h in range(2):
                        mixer(2 * i + h, h)

            @block.scalar
            def _(act):
                def save_btt(b, h):
                    act.wait_ge(btt_made, PRIME + b + 1)
                    act.wait_ge(products_made[1], PRIME + b - 1)
                    nc.scalar.copy(BTT[h], bank(B_TURN).rearrange("p (a t) -> p a t", t=P)).then_inc(btt_saved, 1)

                def save_ctt(b, h):
                    act.wait_ge(ctt_made, PRIME + b + 1)
                    act.wait_ge(products_made[1], PRIME + b - 1)
                    v = bank(C_TURN).rearrange("p (c r t) -> p c r t", c=CH, r=2)
                    z = CTZ[h].rearrange("p c (r two) t -> p c r two t", two=2)
                    nc.scalar.copy(z[0:64, :, :, 0, :], v[0:64])
                    nc.scalar.copy(z[64:P, :, :, 1, :], v[64:P]).then_inc(ctt_saved, 1)

                def make_decays(b, h, c):
                    act.wait_ge(seg_summed[c], PRIME + b + 1)
                    act.wait_ge(y_made, PRIME + b - 1)
                    nc.scalar.activation(LM[h][:, c], bank(SEG + c).rearrange("p (h t) -> p h t", h=NH), ACT.Exp, scale=-1.0)\
                        .then_inc(decays_made[c], 1)

                def save_state(b):
                    act.wait_ge(state_made, PRIME + b + 1)
                    act.wait_ge(y_made, PRIME + b)
                    z = HZ.rearrange("p (r two) e -> p r two e", two=2)
                    v = bank(STATE)[:, 0:2 * HD].rearrange("p (r e) -> p r e", r=2)
                    nc.scalar.copy(z[0:64, :, 0, :], v[0:64])
                    nc.scalar.copy(z[64:P, :, 1, :], v[64:P])
                    nc.scalar.copy(CET, bank(STATE)[:, 2 * HD:2 * HD + 2 * P].rearrange("p (r t) -> p r t", r=2))\
                        .then_inc(state_saved, 1)

                def square_y(b):
                    r = Steps(act, square_steps, b, SQUARE_STEPS)
                    act.wait_ge(raw_saved, PRIME + b)
                    act.wait_ge(y_gated, PRIME + b + 1)
                    r(nc.scalar.activation(junk, Y[:, 0, :], ACT.Square, accum_out=rms[:, 0:1]))
                    nc.scalar.activation(junk, Y[:, 1, :], ACT.Square, accum_out=rms[:, 1:2]).then_inc(squared, 1)
                    act.wait_ge(squared, PRIME + b + 1)
                    r.end()

                def save_yt(b):
                    act.wait_ge(yt_made, PRIME + b + 1)
                    act.wait_ge(mix_out, PRIME + b)
                    nc.scalar.copy(YT, bank(B_TURN).rearrange("p (a t) -> p a t", t=P)).then_inc(yt_saved, 1)

                def ahead(b, h):
                    save_btt(b, h)
                    save_ctt(b, h)

                def body(b, h, first=False, last=False):
                    if not first:
                        save_yt(b - 1)
                    save_state(b)
                    if not last:
                        ahead(b + 1, 1 - h)
                        for c in range(CH):
                            make_decays(b + 1, 1 - h, c)
                    square_y(b)

                act.wait_ge(mixer_zeroed, 1)
                ahead(0, 0)
                for c in range(CH):
                    make_decays(0, 0, c)
                body(0, 0, first=True)
                with act.Fori(0, B // 2 - 1) as i:
                    for k in range(2):
                        body(2 * i + 1 + k, 1 - k)
                body(B - 1, 1, last=True)
                save_yt(B - 1)

            @block.vector
            def _(dve):
                def rotate_b(b, h):
                    m = Steps(dve, mix_steps, b, MIX_STEPS)
                    dve.wait_ge(btt_made, PRIME + b - 1)
                    dve.wait_ge(state_made, PRIME + b - 1)
                    settle(dve)
                    n = ds(2 * b, CH)
                    rotate(dve, m, BCD[:, n, 0:NS], BT[h], r1, r2, n, b_turned_in)
                    m.end()
                    dve.wait_ge(b_turned_in, PRIME + b + 1)

                def make_seg(b, c):
                    dve.wait_ge(seg_summed[c], PRIME + b)
                    settle(dve)
                    adt = DT[:, 1, ds(2 * b + c, 1), :].rearrange("p n h -> p (n h)")
                    nc.vector.tensor_tensor(SR[c], bc(mask_le, 1, NH), bc(adt, 2, P), ALU.mult).then_inc(seg_made[c], 1)

                def mix(b, h, c):
                    dve.wait_ge(decays_made[c], PRIME + b + 1)
                    dve.wait_ge(products_made[c], PRIME + b + 1)
                    nc.vector.tensor_tensor(LM[h][:, c], LM[h][:, c], bank(PRODUCTS + c).rearrange("p (h t) -> p h t", h=NH), ALU.mult)\
                        .then_inc(mixed[c], 1)

                def gate_y(b):
                    n = ds(2 * b, CH)
                    dve.wait_ge(yt_made, PRIME + b)
                    settle(dve)
                    m = Steps(dve, S_("skip_steps"), b, 1)
                    y4 = Y.rearrange("p n (h e) -> p n h e", h=NH)
                    dsk = hb[:, 2, :].unsqueeze(1).unsqueeze(3).to_broadcast([P, CH, NH, HD])
                    m(nc.vector.tensor_tensor(y4, XS[:, n, :].rearrange("p n (h e) -> p n h e", h=NH), dsk, ALU.mult))
                    m.end()
                    dve.wait_ge(y_made, PRIME + b + 1)
                    nc.vector.tensor_tensor(Y, Y, bank(OUTPUT).rearrange("p (c e) -> p c e", c=CH), ALU.add).then_inc(y_read, 1)
                    dve.wait_ge(y_read, PRIME + b + 1)
                    nc.vector.tensor_tensor(Y, Y, Z[:, n, :], ALU.mult).then_inc(y_gated, 1)

                def keep_raw(b):
                    n = ds(2 * b, CH)
                    dve.wait_ge(mix_out, PRIME + b + 1)
                    dve.wait_ge(squared, PRIME + b + 1)
                    settle(dve)
                    nc.vector.tensor_copy(rs[:, 0, n], rms)
                    nc.vector.tensor_copy(XC[:, n, :], bank(SEG)[:, 0:L].rearrange("p (c d) -> p c d", c=CH)).then_inc(raw_saved, 1)

                def body(b, h, first=False, last=False):
                    if not last:
                        rotate_b(b + 1, 1 - h)
                    for c in range(CH):
                        mix(b, h, c)
                    if not first:
                        keep_raw(b - 1)
                    if not last:
                        for c in range(CH):
                            make_seg(b + 1, c)
                    gate_y(b)

                rotate_b(0, 0)
                for c in range(CH):
                    make_seg(0, c)
                for what in (CTZ[0], CTZ[1]):
                    nc.vector.memset(what, 0.0)
                nc.vector.memset(HZ, 0.0).then_inc(mixer_zeroed, 1)
                body(0, 0, first=True)
                with dve.Fori(0, B // 2 - 1) as i:
                    for k in range(2):
                        body(2 * i + 1 + k, 1 - k)
                body(B - 1, 1, last=True)
                keep_raw(B - 1)

            @block.tensor
            def _(pe):
                def turned_by(b):
                    return B if isinstance(b, int) and b == B - 1 else b + 2

                def turn_b(b, h):
                    pe.wait_ge(btt_saved, PRIME + b)
                    pe.wait_ge(yt_saved, PRIME + b - 1)
                    pe.wait_ge(b_turned_in, PRIME + b + 1)
                    pe.wait_ge(b_plain, PRIME + b + 1)
                    for c in range(CH):
                        for r in range(2):
                            at = (2 * c + r) * P
                            last = nc.tensor.transpose(bank(B_TURN)[:, at:at + P], BT[h][:, c, 2 * r:2 * r + 2, :].rearrange("p h n -> p (h n)"), ident)
                    last.then_inc(btt_made, 1)

                def turn_c(b, h):
                    pe.wait_ge(ctt_saved, PRIME + b)
                    pe.wait_ge(c_ready, PRIME + b + 1)
                    for c in range(CH):
                        for r in range(2):
                            at = (2 * c + r) * P
                            last = nc.tensor.transpose(bank(C_TURN)[:, at:at + P], CT[h][:, c, 2 * r:2 * r + 2, :].rearrange("p h n -> p (h n)"), ident)
                    last.then_inc(ctt_made, 1)

                def sum_seg(b, c):
                    pe.wait_ge(decays_made[c], PRIME + b)
                    if c == 0:
                        pe.wait_ge(raw_saved, PRIME + b - 1)
                    pe.wait_ge(seg_made[c], PRIME + b + 1)
                    nc.tensor.matmul(bank(SEG + c), mask_gt, SR[c].rearrange("p h t -> p (h t)"), start=True, stop=False)
                    nc.tensor.matmul(bank(SEG + c), identb[:, :], bigb[:, :, :].rearrange("p h t -> p (h t)"), start=False, stop=True)\
                        .then_inc(seg_summed[c], 1)

                def products(b, h, c):
                    pe.wait_ge(mixed[c], PRIME + b)
                    if c == 0:
                        pe.wait_ge(btt_saved, PRIME + b + 1)
                        pe.wait_ge(ctt_saved, PRIME + b + 1)
                    for k in range(NH):
                        last = nc.tensor.matmul(bank(PRODUCTS + c)[:, k * P:(k + 1) * P], BTT[h][:, 2 * c + k // 2, :], CTZ[h][:, c, k, :],
                                                start=True, stop=True)
                    last.then_inc(products_made[c], 1)

                def state(b, h):
                    pe.wait_ge(state_saved, PRIME + b)
                    pe.wait_ge(dtx_made, PRIME + b + 1)
                    for k in range(NH):
                        r = 64 * (k % 2)
                        nc.tensor.matmul(PS[r:r + 64, STATE, (k // 2) * HD:(k // 2 + 1) * HD], BT[h][:, 0, k, :], dtxe[h][:, k, :],
                                         start=True, stop=True)
                    for r in range(2):
                        at = 2 * HD + r * P
                        last = nc.tensor.transpose(bank(STATE)[:, at:at + P], CE[h][:, 2 * r:2 * r + 2, :].rearrange("p h n -> p (h n)"), ident)
                    last.then_inc(state_made, 1)

                def outputs(b, h):
                    pe.wait_ge(y_read, PRIME + b)
                    pe.wait_ge(state_saved, PRIME + b + 1)
                    for c in range(CH):
                        pe.wait_ge(mixed[c], PRIME + b + 1)
                        for k in range(NH):
                            to = bank(OUTPUT)[:, c * DI + k * HD:c * DI + (k + 1) * HD]
                            last = nc.tensor.matmul(to, LM[h][:, c, k, :], dtx[h][:, c, k, :], start=True, stop=c == 0)
                            if c:
                                last = nc.tensor.matmul(to, CET[:, k // 2, :], HZ[:, k, :], start=False, stop=True)
                    last.then_inc(y_made, 1)

                def turn_y(b):
                    pe.wait_ge(btt_saved, PRIME + turned_by(b))
                    pe.wait_ge(y_gated, PRIME + b + 1)
                    for c in range(CH):
                        for r in range(2):
                            at = (2 * c + r) * P
                            last = nc.tensor.transpose(bank(B_TURN)[:, at:at + P], Y[:, c, r * P:(r + 1) * P], ident)
                    last.then_inc(yt_made, 1)

                def project_y(b):
                    pe.wait_ge(decays_made[0], PRIME + turned_by(b))
                    pe.wait_ge(yt_saved, PRIME + b + 1)
                    for c in range(CH):
                        for r in range(2):
                            last = nc.tensor.matmul(bank(SEG)[:, c * D:(c + 1) * D], YT[:, 2 * c + r, :], Wout[:, r, :],
                                                    start=r == 0, stop=r == 1)
                    last.then_inc(mix_out, 1)

                def body(b, h, first=False, last=False):
                    for c in range(CH):
                        products(b, h, c)
                    if not first:
                        turn_y(b - 1)
                    state(b, h)
                    if not first:
                        project_y(b - 1)
                    if not last:
                        turn_b(b + 1, 1 - h)
                        turn_c(b + 1, 1 - h)
                    outputs(b, h)
                    if not last:
                        for c in range(CH):
                            sum_seg(b + 1, c)

                turn_b(0, 0)
                turn_c(0, 0)
                for c in range(CH):
                    sum_seg(0, c)
                body(0, 0, first=True)
                with pe.Fori(0, B // 2 - 1) as i:
                    for k in range(2):
                        body(2 * i + 1 + k, 1 - k)
                body(B - 1, 1, last=True)
                turn_y(B - 1)
                project_y(B - 1)

        TB = 512
        with nc.Block() as block:
            scale_vec, scale_act, scaled = S_("scale_vec"), S_("scale_act"), S_("scaled")
            normed, normed_turned, normed_saved, q_made, q_parts_made, q_in_dram, q_vec = (
                S_(n) for n in ("normed", "normed_turned", "normed_saved", "q_made", "q_parts_made", "q_in_dram", "q_vec"))
            q_biased, q_first, q_second, buffers_set = (S_(n) for n in ("q_biased", "q_first", "q_second", "buffers_set"))
            blocks = range(NT * P // TB)
            BUFFERS_ZEROED, BUFFERS_SET = 6, 7
            q_stacked = [[S_(f"q_stacked{2 * par + g}") for g in range(2)] for par in range(2)]
            keys_max, keys_exp, values_ready = S_("keys_max"), S_("keys_exp"), S_("values_ready")
            unit_made = [S_(f"unit_made{k}") for k in range(SPANS)]
            unit_taken = [S_(f"unit_taken{k}") for k in range(SPANS)]
            max_steps, max_split, max_turned, max_saved, max_stacked = (
                S_(n) for n in ("max_steps", "max_split", "max_turned", "max_saved", "max_stacked"))
            scored = [S_("scored0"), S_("scored1")]
            powered = [S_("powered0"), S_("powered1")]
            summed = [S_("summed0"), S_("summed1")]
            sums_saved, sums_turned, out_steps, heads_out = (
                S_(n) for n in ("sums_saved", "sums_turned", "out_steps", "heads_out"))

            def score_fill(b, g, kt, j):
                return ((2 * b + g) * KT + kt) * 2 + j // 2

            def sum_count(b, g, kt):
                return KT * b + (g * KT + kt) // 2

            def parity(g, kt):
                return (g * KT + kt) % 2

            def units(b, g, kt, last):
                if kt >= AHEAD:
                    target, at = (b + 1, g), sum(UNITS_AT[AHEAD:kt])
                else:
                    target, at = following(b, g), sum(UNITS_AT[AHEAD:]) + sum(UNITS_AT[:kt])
                none = last and (kt >= AHEAD or g)
                return target, range(at, at + UNITS_AT[kt] * (not none))

            def following(b, g):
                return (b, 1) if g == 0 else (b + 1, 0)

            first_units = range(sum(UNITS_AT[AHEAD:]))

            @block.sync
            def _(sp):
                def stack_queries(b, g, par, b_before=None):
                    if b_before is not None:
                        sp.wait_ge(scored[1], PRIME + score_fill(b_before, g, KT, 1))
                    src = q_dram[g * GH:(g + 1) * GH, :, :, ds(L * b, L)].rearrange("h i d t -> (i d) h t")
                    for j in range(PARTS):
                        r = j * PARTS * DK
                        sp.dma_start(Qg[par][g][r:r + PARTS * DK, :].rearrange("p (h t) -> p h t", h=GH), src)\
                            .then_inc(q_stacked[par][g], 16)

                def stack_maxima(b, g, par):
                    sp.wait_ge(max_saved, PRIME + 2 * b + g + 1)
                    sp.dma_start(Qg[par][g][MROW:MROW + PARTS, :].rearrange("i (q t) -> i q t", q=NQ), MT[0:PARTS * NQ, :])\
                        .then_inc(max_stacked, 16)

                def body(b, par, last=False, queries=True):
                    stack_maxima(b, 1, par)
                    if queries:
                        stack_queries(b + 2, 0, par, b)
                    if not last:
                        stack_maxima(b + 1, 0, 1 - par)
                    if queries:
                        stack_queries(b + 2, 1, par, b)

                def queries_to_dram(r):
                    sp.wait_ge(q_parts_made, r + 1)
                    for i in range(PARTS):
                        sp.dma_start(q_dram[:, i, :, r * TB:(r + 1) * TB], QP[:, i, r * TB:(r + 1) * TB]).then_inc(q_in_dram, 16)

                queries_to_dram(0)
                sp.wait_ge(buffers_set, BUFFERS_ZEROED)
                sp.wait_ge(q_in_dram, 16 * PARTS)
                for par in range(2):
                    for g in range(2):
                        stack_queries(par, g, par)
                for r in blocks[1:]:
                    queries_to_dram(r)
                sp.wait_ge(q_in_dram, 16 * PARTS * len(blocks))
                stack_maxima(0, 0, 0)
                with sp.Fori(0, B // 2 - 1) as i:
                    for par in range(2):
                        body(2 * i + par, par)
                body(B - 2, 0, queries=False)
                body(B - 1, 1, last=True, queries=False)
                sp.wait_ge(max_stacked, PRIME + 16 * 2 * B)

            @block.scalar
            def _(act):
                def save_normed(r):
                    act.wait_ge(normed_turned, r + 1)
                    nc.scalar.copy(xqT[:, r * TB:(r + 1) * TB], bank(r)).then_inc(normed_saved, 1)

                def first_part(r):
                    tok = slice(r * TB, (r + 1) * TB)
                    act.wait_ge(q_made, r + 1)
                    nc.scalar.activation(QF[:, tok], bank(4 + r), ACT.Identity, bias=bqS[:, :]).then_inc(q_biased, 1)
                    act.wait_ge(q_biased, r + 1)
                    nc.scalar.copy(QP[:, 0, tok], QF[:, tok]).then_inc(q_first, 1)

                def second_part(r):
                    tok = slice(r * TB, (r + 1) * TB)
                    act.wait_ge(q_vec, r + 1)
                    nc.scalar.copy(QP[:, 1, tok], QF[:, tok]).then_inc(q_second, 1)

                warm(ACT.Sqrt)
                act.wait_ge(scale_vec, 2)
                nc.scalar.activation(rs[:, 2, :], rs[:, 1, :], ACT.Sqrt).then_inc(scale_act, 1)
                deviations(act, norms, 1, st, warm)
                save_normed(0)
                save_normed(1)
                for r in blocks:
                    first_part(r)
                    if r + 2 < len(blocks):
                        save_normed(r + 2)
                    if r:
                        second_part(r - 1)
                second_part(len(blocks) - 1)
                warm(ACT.Exp)

                def save_maxima(b, g):
                    act.wait_ge(max_turned, PRIME + 2 * b + g + 1)
                    act.wait_ge(max_stacked, PRIME + 16 * (2 * b + g))
                    nc.scalar.copy(MT[0:PARTS * NQ, :], bankb(AUX)[0:PARTS * NQ, 0:P]).then_inc(max_saved, 1)

                def save_sums(b, g):
                    act.wait_ge(summed[parity(g, KT - 1)], PRIME + sum_count(b, g, KT - 1) + 1)
                    act.wait_ge(sums_turned, PRIME + 2 * b + g)
                    nc.scalar.copy(OT, bank(ACC)).then_inc(sums_saved, 1)

                def exponentials(b, g, kt, js):
                    for j in js:
                        act.wait_ge(scored[j % 2], PRIME + score_fill(b, g, kt, j) + 1)
                        if j == 0:
                            act.wait_ge(summed[parity(g, kt)], PRIME + sum_count(b, g, kt))
                        nc.scalar.activation(PE_[:, parity(g, kt), j, :], bank(RING + j % 2), ACT.Exp).then_inc(powered[j % 2], 1)

                def body(b, first=False, last=False):
                    for g in range(2):
                        for kt in range(KT):
                            exponentials(b, g, kt, (0, 1))
                            exponentials(b, g, kt, (2,))
                            if kt == 0 and (g or not first):
                                save_sums(*((b, 0) if g else (b - 1, 1)))
                            exponentials(b, g, kt, (3,))
                            if kt == AHEAD + 1 and not (last and g):
                                save_maxima(*following(b, g))

                save_maxima(0, 0)
                body(0, first=True)
                with act.Fori(1, B - 1) as b:
                    body(b)
                body(B - 1, last=True)
                save_sums(B - 1, 1)

            @block.vector
            def _(dve):
                s = Steps(dve, scale_vec)
                s(nc.vector.tensor_scalar(rs[:, 1, :], rs[:, 0, :], 1.0 / DI, EPS, ALU.mult, ALU.add))
                s(nc.vector.reciprocal(rs[:, 1, :], rs[:, 1, :]))
                dve.wait_ge(scale_act, 1)
                for n in range(NT):
                    last = nc.vector.scalar_tensor_tensor(X[:, n, :], XC[:, n, :], rs[:, 2, n:n + 1], X[:, n, :], ALU.mult, ALU.add)
                last.then_inc(scaled, 1)
                dve.wait_ge(scaled, 1)
                moments(dve, norms, 1, X, BS, MV, st)
                normalise(dve, norms, 1, X, XC, MV, st, normed)
                m = Steps(dve, q_vec)

                def last_part(r):
                    tok = slice(r * TB, (r + 1) * TB)
                    dve.wait_ge(q_second, r + 1)
                    nc.vector.tensor_tensor(QP[:, 2, tok], QF[:, tok], QP[:, 1, tok], ALU.subtract).then_inc(q_parts_made, 1)

                for r in blocks:
                    tok = slice(r * TB, (r + 1) * TB)
                    dve.wait_ge(q_first, r + 1)
                    m(nc.vector.tensor_tensor(QF[:, tok], QF[:, tok], QP[:, 0, tok], ALU.subtract))
                    if r:
                        last_part(r - 1)
                last_part(len(blocks) - 1)

                def take_max(b, g, u):
                    qt, k = u // SPANS, u % SPANS
                    dve.wait_ge(unit_made[k], PRIME + (2 * b + g) * NQ + qt + 1)
                    nc.vector.tensor_reduce(NMX[:, k, qt:qt + 1], bank(UNIT + k)[:, 0:SPAN], axis=AX.X, op=ALU.max, negate=True)\
                        .then_inc(unit_taken[k], 1)

                def split_maxima(b, g, target=None, todo=()):
                    done = MAX_STEPS * (2 * b + g)
                    for k in range(SPANS):
                        dve.wait_ge(unit_taken[k], PRIME + (2 * b + g + 1) * NQ)
                    dve.wait_ge(max_turned, PRIME + 2 * b + g)
                    nc.vector.tensor_reduce(NM, NMX.rearrange("p k q -> p q k"), axis=AX.X, op=ALU.min).then_inc(max_steps, 1)
                    dve.wait_ge(max_steps, done + 1)
                    nc.vector.tensor_copy(MP[:, 0, :], NM).then_inc(max_steps, 1)
                    for u in todo[0:1]:
                        take_max(*target, u)
                    dve.wait_ge(max_steps, done + 2)
                    nc.vector.tensor_tensor(NR, NM, MP[:, 0, :], ALU.subtract).then_inc(max_steps, 1)
                    for u in todo[1:2]:
                        take_max(*target, u)
                    dve.wait_ge(max_steps, done + 3)
                    nc.vector.tensor_copy(MP[:, 1, :], NR).then_inc(max_steps, 1)
                    for u in todo[2:3]:
                        take_max(*target, u)
                    dve.wait_ge(max_steps, done + 4)
                    nc.vector.tensor_tensor(MP[:, 2, :], NR, MP[:, 1, :], ALU.subtract).then_inc(max_split, 1)
                    for u in todo[3:]:
                        take_max(*target, u)

                def finish(b, g):
                    m = Steps(dve, out_steps, 2 * b + g, 1)
                    v = bank(AUX).rearrange("p (s j e) -> p s j e", s=4, j=NB)
                    dve.wait_ge(sums_turned, PRIME + 2 * b + g + 1)
                    m(nc.vector.reciprocal(rdn.rearrange("p (s j) -> p s j", s=4), v[:, :, :, DK]))
                    m.end()
                    for s in range(4):
                        hh, c = s // 2, s % 2
                        to = ONall[:, ds(2 * b + c, 1), g * 64:g * 64 + 64].rearrange("p n (j hh d) -> p (n j) hh d", hh=2, d=DK)
                        last = nc.vector.tensor_tensor(to[:, :, hh, :], v[:, s, :, 0:DK], bc(rdn[:, 4 * s:4 * s + 4], 2, DK), ALU.mult)
                    last.then_inc(heads_out, 1)

                def body(b, first=False, last=False):
                    for g in range(2):
                        for kt in range(KT):
                            target, todo = units(b, g, kt, last)
                            if kt == AHEAD and not (last and g):
                                split_maxima(*following(b, g), target, todo)
                            else:
                                for u in todo:
                                    take_max(*target, u)
                            if kt == 1 and (g or not first):
                                finish(*((b, 0) if g else (b - 1, 1)))

                for u in range(SPANS * NQ):
                    take_max(0, 0, u)
                split_maxima(0, 0)
                for u in first_units:
                    take_max(0, 1, u)
                body(0, first=True)
                with dve.Fori(1, B - 1) as b:
                    body(b)
                body(B - 1, last=True)
                finish(B - 1, 1)

            @block.gpsimd
            def _(pool):
                g = Steps(pool, buffers_set)
                for par in range(2):
                    g(nc.gpsimd.memset(KSa[par], 0.0))
                    for what in Qg[par]:
                        g(nc.gpsimd.memset(what, 0.0))
                assert g.k == BUFFERS_ZEROED
                g(nc.gpsimd.tensor_copy(KSa[0][0:MROW, :], KSall[0:MROW, 0, :]))
                assert g.k == BUFFERS_SET

                def keys_for_max(b, par):
                    for k in range(SPANS):
                        pool.wait_ge(unit_taken[k], PRIME + 2 * (b - 1) * NQ)
                    settle(pool)
                    nc.gpsimd.tensor_copy(KSa[par][0:MROW, :], KSall[0:MROW, ds(b, 1), :].rearrange("p b s -> p (b s)"))\
                        .then_inc(keys_max, 1)

                def keys_for_exp(b, par):
                    pool.wait_ge(scored[1], PRIME + score_fill(b - 1, 0, 0, 0))
                    settle(pool)
                    nc.gpsimd.tensor_copy(KSb[par], KSall[:, ds(b, 1), :].rearrange("p b s -> p (b s)")).then_inc(keys_exp, 1)

                def values(b, par):
                    for r in range(2):
                        pool.wait_ge(summed[r], PRIME + KT * (b - 1))
                    settle(pool)
                    nc.gpsimd.tensor_copy(Vc[par], Vall[:, ds(b, 1), :, :].rearrange("p b k e -> p (b k) e")).then_inc(values_ready, 1)

                def copies(b, par):
                    keys_for_max(b, par)
                    keys_for_exp(b, par)
                    values(b, par)

                nc.gpsimd.tensor_copy(KSb[0], KSall[:, 0, :]).then_inc(keys_exp, 1)
                nc.gpsimd.tensor_copy(Vc[0], Vall[:, 0, :, :]).then_inc(values_ready, 1)
                with pool.Fori(0, B // 2 - 1) as i:
                    for k in range(2):
                        copies(2 * i + 1 + k, 1 - k)
                copies(B - 1, 1)

            @block.tensor
            def _(pe):
                for r in range(len(blocks) + 1):
                    if r < len(blocks):
                        pe.wait_ge(normed, r + 1)
                        for t in range(TB // P):
                            last = nc.tensor.transpose(bank(r)[:, t * P:(t + 1) * P], XC[:, 4 * r + t, :], ident)
                        last.then_inc(normed_turned, 1)
                    if r:
                        pe.wait_ge(normed_saved, r)
                        nc.tensor.matmul(bank(3 + r), WqS[:, :], xqT[:, (r - 1) * TB:r * TB], start=True, stop=True).then_inc(q_made, 1)

                def fill_unit(b, g, par, turn, u):
                    qt, k = u // SPANS, u % SPANS
                    pe.wait_ge(unit_taken[k], PRIME + (2 * b + g) * NQ + qt)
                    if u == 0:
                        pe.wait_ge(q_stacked[par][g], PRIME + 16 * PARTS * (turn + 1))
                        if g == 0:
                            pe.wait_ge(keys_max, PRIME + b)
                    at = min(k * SPAN, S - SPAN)
                    nc.tensor.matmul(bank(UNIT + k)[:, 0:SPAN], Qg[par][g][:, qt * P:(qt + 1) * P], KSa[par][:, at:at + SPAN],
                                     start=True, stop=True).then_inc(unit_made[k], 1)

                def turn_maxima(b, g):
                    pe.wait_ge(heads_out, PRIME + 2 * b + g - 1)
                    pe.wait_ge(max_split, PRIME + 2 * b + g + 1)
                    settle(pe)
                    nc.tensor.transpose(bankb(AUX)[0:PARTS * NQ, 0:P], MP.rearrange("p i q -> p (i q)"), identb[:, :])\
                        .then_inc(max_turned, 1)

                def score(b, g, par, kt, j):
                    pe.wait_ge(powered[j % 2], PRIME + score_fill(b, g, kt, j))
                    if kt == 0 and j == 0:
                        pe.wait_ge(max_stacked, PRIME + 16 * (2 * b + g + 1))
                        if g == 0:
                            pe.wait_ge(keys_exp, PRIME + b + 1)
                    nc.tensor.matmul(bank(RING + j % 2), KSb[par][:, kt * P:(kt + 1) * P], Qg[par][g][:, j * 512:(j + 1) * 512],
                                     start=True, stop=True).then_inc(scored[j % 2], 1)

                def weigh(b, g, par, kt):
                    for r in range(2):
                        pe.wait_ge(powered[r], PRIME + score_fill(b, g, kt, 2) + 1)
                    if kt == 0:
                        pe.wait_ge(sums_saved, PRIME + 2 * b + g)
                        if g == 0:
                            pe.wait_ge(values_ready, PRIME + b + 1)
                    for j in range(NB):
                        last = nc.tensor.matmul(PS[32 * j:32 * j + 32, ACC, :], Vc[par][:, kt, :], PE_[:, parity(g, kt), j, :],
                                                start=kt == 0, stop=kt == KT - 1)
                    last.then_inc(summed[parity(g, kt)], 1)

                def finish(b, g):
                    pe.wait_ge(max_saved, PRIME + 2 * b + g + 2)
                    pe.wait_ge(sums_saved, PRIME + 2 * b + g + 1)
                    for s in range(4):
                        last = nc.tensor.transpose(bank(AUX)[:, s * P:(s + 1) * P], OT[:, s * P:(s + 1) * P], ident)
                    last.then_inc(sums_turned, 1)

                def body(b, par, turn, first=False, last=False):
                    for g in range(2):
                        for kt in range(KT):
                            target, todo = units(b, g, kt, last)
                            same = g == 0 and kt < AHEAD
                            place = (par, turn) if same else (1 - par, turn + par)

                            def maxima(first, n):
                                for u in todo[first:first + n]:
                                    fill_unit(*target, *place, u)

                            maxima(0, 1)
                            score(b, g, par, kt, 0)
                            maxima(1, 2)
                            score(b, g, par, kt, 1)
                            if kt:
                                weigh(b, g, par, kt - 1)
                            elif g:
                                weigh(b, 0, par, KT - 1)
                            elif not first:
                                weigh(b - 1, 1, 1 - par, KT - 1)
                            score(b, g, par, kt, 2)
                            maxima(3, 2)
                            if kt == AHEAD + 1 and not (last and g):
                                turn_maxima(*following(b, g))
                            score(b, g, par, kt, 3)
                            maxima(5, len(todo))
                            if kt == 1 and (g or not first):
                                finish(*((b, 0) if g else (b - 1, 1)))
                pe.wait_ge(buffers_set, BUFFERS_SET)
                for u in range(SPANS * NQ):
                    fill_unit(0, 0, 0, 0, u)
                for u in first_units:
                    fill_unit(0, 1, 0, 0, u)
                turn_maxima(0, 0)
                body(0, 0, 0, first=True)
                with pe.Fori(0, B // 2 - 1) as i:
                    for k in range(2):
                        body(2 * i + 1 + k, 1 - k, i + k)
                body(B - 1, 1, B // 2 - 1, last=True)
                weigh(B - 1, 1, 1, KT - 1)
                pe.wait_ge(sums_saved, PRIME + 2 * B)
                pe.wait_ge(heads_out, PRIME + 2 * B - 1)
                for s in range(4):
                    last = nc.tensor.transpose(bank(AUX)[:, s * P:(s + 1) * P], OT[:, s * P:(s + 1) * P], ident)
                last.then_inc(sums_turned, 1)

        with nc.Block() as block:
            on_turned, onT_saved, o_made, x2_made = (S_(n) for n in ("on_turned", "onT_saved", "o_made", "x2_made"))
            bias_added = S_("bias_added")
            xn3_made, x3_turned, x3_saved, lg_made = (S_(n) for n in ("xn3_made", "x3_turned", "x3_saved", "lg_made"))
            top_steps, lg_exp, coef_split, coef_turned, coef_saved = (S_(n) for n in ("top_steps", "lg_exp", "coef_split", "coef_turned", "coef_saved"))
            gate_made = [S_("gate_made0"), S_("gate_made1")]
            gate_used = [S_("gate_used0"), S_("gate_used1")]
            up_made = [S_("up_made0"), S_("up_made1")]
            up_used = [S_("up_used0"), S_("up_used1")]
            gated, down_made, out_made, stored = S_("gated"), S_("down_made"), S_("out_made"), S_("stored")
            fills = [len(range(par, HT, 2)) for par in range(2)]

            def count(q, k):
                return fills[k % 2] * q + k // 2

            @block.sync
            def _(sp):
                o = out.rearrange("b (c p) d -> p (b c) d", p=P)
                with sp.Fori(0, NT * P // TB) as q:
                    sp.wait_ge(out_made, PRIME + q + 1)
                    sp.dma_start(o[:, ds(4 * q, 4), :], X[:, ds(4 * q, 4), :]).then_inc(stored, 16)
                sp.wait_ge(stored, 16 * (NT * P // TB))

            @block.scalar
            def _(act):
                for r in blocks:
                    act.wait_ge(on_turned, r + 1)
                    nc.scalar.copy(X3T[:, r * TB:(r + 1) * TB], bank(r)).then_inc(onT_saved, 1)
                deviations(act, norms, 2, st, warm)
                warm(ACT.Exp)
                for r in blocks:
                    act.wait_ge(x3_turned, r + 1)
                    nc.scalar.copy(X3T[:, r * TB:(r + 1) * TB], bank(r)).then_inc(x3_saved, 1)
                act.wait_ge(top_steps, TOP_SHIFT)
                nc.scalar.activation(SH, SH, ACT.Exp).then_inc(lg_exp, 1)
                warm(ACT.Silu)
                act.wait_ge(coef_turned, 2)
                nc.scalar.copy(CTs[:, :].rearrange("p (k t) -> p k t", k=2),
                               PS[0:PARTS * NE, 4:6, :].bitcast(bf16)).then_inc(coef_saved, 1)
                with act.Fori(0, NT * P // TB) as q:
                    for k in range(HT):
                        act.wait_ge(gate_made[k % 2], PRIME + count(q, k) + 1)
                        act.wait_ge(up_used[k % 2], PRIME + count(q, k))
                        nc.scalar.activation(SG[:, k % 2, :], bank(k % 2), ACT.Silu).then_inc(gate_used[k % 2], 1)

            @block.vector
            def _(dve):
                nc.vector.tensor_tensor(X[:, :, :], X[:, :, :], bc(boS[:, :], 1, NT), ALU.add).then_inc(bias_added, 1)
                dve.wait_ge(bias_added, 1)
                for r in blocks:
                    n = slice(4 * r, 4 * r + 4)
                    dve.wait_ge(o_made, r + 1)
                    nc.vector.tensor_tensor(X[:, n, :], X[:, n, :], bank(4 + r).rearrange("p (n d) -> p n d", n=4), ALU.add)\
                        .then_inc(x2_made, 1)
                dve.wait_ge(x2_made, len(blocks))
                moments(dve, norms, 2, X, BS, MV, st)
                normalise(dve, norms, 2, X, XC, MV, st, xn3_made)
                t = Steps(dve, top_steps)
                dve.wait_ge(lg_made, 1)
                LG = bank(7)[:, 0:NT * NE].rearrange("p (n e) -> p n e", e=NE)
                t(nc.vector.tensor_reduce(red, LG, axis=AX.X, op=ALU.max))
                t(nc.vector.tensor_tensor(SH, LG, bc(red, 2, NE), ALU.subtract))
                assert t.k == TOP_SHIFT
                dve.wait_ge(lg_exp, 1)
                t(nc.vector.reduce_sum(red, SH, axis=AX.X))
                t(nc.vector.reciprocal(rcp, red))
                t(nc.vector.tensor_tensor(PB, SH, bc(rcp, 2, NE), ALU.mult))
                for picked, among in ((S1, PB), (S2_, SH)):
                    t(nc.vector.tensor_reduce(red, among, axis=AX.X, op=ALU.max))
                    t(nc.vector.tensor_tensor(KY, among, bc(red, 2, NE), ALU.is_equal))
                    t(nc.vector.tensor_tensor(KY, KY, bc(rank, 1, NT), ALU.mult))
                    t(nc.vector.tensor_reduce(red, KY, axis=AX.X, op=ALU.max))
                    t(nc.vector.tensor_tensor(picked, KY, bc(red, 2, NE), ALU.is_equal))
                    if picked is S1:
                        t(nc.vector.scalar_tensor_tensor(SH, S1, -2.0, PB, ALU.mult, ALU.add))
                t(nc.vector.tensor_tensor(S1, S1, S2_, ALU.add))
                t(nc.vector.tensor_tensor(CR, PB, S1, ALU.mult))
                part = [CP[:, :, i * NE:(i + 1) * NE] for i in range(PARTS)]
                t(nc.vector.tensor_copy(part[0], CR))
                t(nc.vector.tensor_tensor(CR, CR, part[0], ALU.subtract))
                t(nc.vector.tensor_copy(part[1], CR))
                nc.vector.tensor_tensor(part[2], CR, part[1], ALU.subtract).then_inc(coef_split, 1)
                with dve.Fori(0, NT * P // TB) as q:
                    dve.wait_ge(down_made, PRIME + q)
                    for k in range(HT):
                        par = k % 2
                        dve.wait_ge(gate_used[par], PRIME + count(q, k) + 1)
                        dve.wait_ge(up_made[par], PRIME + count(q, k) + 1)
                        if k < HT - 1:
                            g = Steps(dve, gated, q, HT - 1)
                            g.k = k
                            g(nc.vector.tensor_tensor(Hb[:, k, :], SG[:, par, :], bank(2 + par), ALU.mult))
                            nc.vector.tensor_tensor(Hb[:, k, :], Hb[:, k, :], bank(4 + par), ALU.mult).then_inc(up_used[par], 1)
                        else:
                            nc.vector.tensor_tensor(Hb[:, k, :], SG[:, par, :], bank(2 + par), ALU.mult).then_inc(up_used[par], 1)
                    dve.wait_ge(down_made, PRIME + q + 1)
                    settle(dve)
                    n = ds(4 * q, 4)
                    nc.vector.tensor_tensor(X[:, n, :], X[:, n, :], bank(6).rearrange("p (n d) -> p n d", n=4), ALU.add)\
                        .then_inc(out_made, 1)

            @block.tensor
            def _(pe):
                for r in blocks:
                    for t in range(TB // P):
                        last = nc.tensor.transpose(bank(r)[:, t * P:(t + 1) * P], ONall[:, 4 * r + t, :], ident)
                    last.then_inc(on_turned, 1)
                for r in blocks:
                    pe.wait_ge(onT_saved, r + 1)
                    for t in range(TB // P):
                        at = r * TB + t * P
                        last = nc.tensor.matmul(bank(4 + r)[:, t * P:(t + 1) * P], X3T[:, at:at + P], WoS[:, :], start=True, stop=True)
                    last.then_inc(o_made, 1)
                for r in blocks:
                    pe.wait_ge(xn3_made, r + 1)
                    for t in range(TB // P):
                        last = nc.tensor.transpose(bank(r)[:, t * P:(t + 1) * P], XC[:, 4 * r + t, :], ident)
                    last.then_inc(x3_turned, 1)
                for r in blocks:
                    pe.wait_ge(x3_saved, r + 1)
                    for t in range(TB // P):
                        n = 4 * r + t
                        last = nc.tensor.matmul(bank(7)[:, n * NE:(n + 1) * NE], X3T[:, n * P:(n + 1) * P], RT[:, :], start=True, stop=True)
                last.then_inc(lg_made, 1)
                pe.wait_ge(coef_split, 1)
                for n in range(NT):
                    last = nc.tensor.transpose(bankb(4 + n // 8)[0:PARTS * NE, (n % 8) * P:(n % 8 + 1) * P],
                                               CP[:, n, 0:PARTS * NE], identb[:, :])
                    if n % 8 == 7:
                        last.then_inc(coef_turned, 1)
                pe.wait_ge(coef_saved, 1)
                with pe.Fori(0, NT * P // TB) as q:
                    tok = ds(TB * q, TB)
                    for k in range(HT):
                        par = k % 2
                        pe.wait_ge(gate_used[par], PRIME + count(q, k))
                        nc.tensor.matmul(bank(par), WG[:, k * P:(k + 1) * P], X3T[:, tok], start=True, stop=True)\
                            .then_inc(gate_made[par], 1)
                        pe.wait_ge(up_used[par], PRIME + count(q, k))
                        last = nc.tensor.matmul(bank(2 + par), WU[:, k * P:(k + 1) * P], X3T[:, tok], start=True, stop=True)
                        if k < HT - 1:
                            last = nc.tensor.matmul(bank(4 + par), selb[:, k, :], CTs[:, tok], start=True, stop=True)
                        last.then_inc(up_made[par], 1)
                    for par in range(2):
                        pe.wait_ge(up_used[par], PRIME + fills[par] * (q + 1))
                    pe.wait_ge(out_made, PRIME + q)
                    for t in range(TB // P):
                        for k in range(HT):
                            last = nc.tensor.matmul(bank(6)[:, t * D:(t + 1) * D], Hb[:, k, t * P:(t + 1) * P], WD[:, k, :],
                                                    start=k == 0, stop=k == HT - 1)
                    last.then_inc(down_made, 1)


def kernel(**inputs):
    import concourse.bacc as bacc
    from concourse.bass_utils import run_bass_kernel_spmd

    names = ["x", "ctx_1024", "L0_attn_W_in", "L0_attn_W_out", "L0_attn_dt_bias", "L0_attn_A_log", "L0_attn_D_skip",
             "L0_attn_norm_weight", "L0_xattn_Wq", "L0_xattn_bq", "L0_xattn_Wk", "L0_xattn_bk", "L0_xattn_Wv",
             "L0_xattn_bv", "L0_xattn_Wo", "L0_xattn_bo", "L0_ffn_router", "L0_ffn_experts_gate",
             "L0_ffn_experts_up", "L0_ffn_experts_down", "L0_ffn_shared_gate", "L0_ffn_shared_up",
             "L0_ffn_shared_down"]
    nc = bacc.Bacc("TRN2", target_bir_lowering=False, num_devices=1)
    arrays, args = {}, []
    for name in names + ["shape_constants"]:
        a = np.ascontiguousarray(inputs[name] if name in inputs else shape_constants())
        arrays[f"in_{name}"] = a
        args.append(nc.dram_tensor(f"in_{name}", a.shape, mybir.dt.from_np(a.dtype), kind="ExternalInput").ap())
    out = nc.dram_tensor("out_0", (B, L, D), mybir.dt.float32, kind="ExternalOutput").ap()
    build(nc, *args, out)
    r = run_bass_kernel_spmd(nc, [arrays], core_ids=[0])
    return r.results[0]["out_0"]
```
